# Optimizing a Trainium2 kernel written in Bass

```python
import numpy as np
import jax
import jax.numpy as jnp

def _softmax(x, axis=-1):
    return jax.nn.softmax(x, axis=axis)

def _gelu(x):
    return jax.nn.gelu(x, approximate=True)

def _silu(x):
    return jax.nn.silu(x)

def _sigmoid(x):
    return jax.nn.sigmoid(x)

def _layernorm(x, axis=-1, eps=1e-05):
    m = jnp.mean(x, axis=axis, keepdims=True)
    v = jnp.var(x, axis=axis, keepdims=True)
    return (x - m) / jnp.sqrt(v + eps)

def _scatter_add(tgt, idx, src, axis=0):
    return tgt.at[idx].add(src)

def _segment_sum(src, seg, n):
    return jax.ops.segment_sum(src, seg, n)
kernel_name = 'mk_decoder_preln_d2_seqx_r4_6c7102'

def setup_inputs(seed: int=0):
    np.random.seed(seed)
    _w = jnp.asarray

    def _rec_inputs():
        import jax
        import jax.numpy as jnp
        _rk = jax.random.key(seed)
        x = -0.0002928 + 1 * jax.random.normal(jax.random.fold_in(_rk, 1), (4, 512, 256), jnp.float32)
        _lenS = 512 - jax.random.randint(jax.random.fold_in(_rk, 7), (4,), 0, max(1, 512 // 4) + 1, jnp.int32)
        _lenS2 = 512 - jax.random.randint(jax.random.fold_in(_rk, 8), (4,), 0, max(1, 512 // 4) + 1, jnp.int32)
        _ctx_1024P = jax.random.normal(jax.random.fold_in(_rk, 11), (4, 16, 256), jnp.float32)
        _ctx_1024c = jax.random.dirichlet(jax.random.fold_in(_rk, 511), 0.3 * jnp.ones((16,), jnp.float32), (4, 512))
        _ctx_1024t = jnp.einsum('bsk,bkd->bsd', _ctx_1024c, _ctx_1024P)
        _ctx_1024t = _ctx_1024t * jax.lax.rsqrt(jnp.mean(jnp.square(_ctx_1024t)) + 1e-12) * 0.953939
        ctx_1024 = -1.39393e-06 + 0.999914 * (_ctx_1024t + 0.3 * jax.random.normal(jax.random.fold_in(_rk, 611), (4, 512, 256), jnp.float32))
        return (x, ctx_1024)
    x, ctx_1024 = _rec_inputs()

    def _L0_attn_setup():
        import jax, jax.numpy as jnp
        import numpy as np
        H = 16
        HD = 64
        W = 256
        G = 64
        EPS = 1e-06
        NEG = -1e+30
        key = jax.random.key(seed)
        ks = jax.random.split(key, 7)
        B, S, D = (1, 2048, 256)
        inner = H * HD
        s = 0.02
        return {'x': jax.random.normal(ks[0], (B, S, D), jnp.float32), 'norm_w': jnp.ones((D,), jnp.float32), 'w_q': jax.random.normal(ks[1], (D, inner), jnp.float32) * s, 'w_k': jax.random.normal(ks[2], (D, inner), jnp.float32) * s, 'w_v': jax.random.normal(ks[3], (D, inner), jnp.float32) * s, 'w_out': jax.random.normal(ks[4], (inner, D), jnp.float32) * s, 'scorer_w': jax.random.normal(ks[5], (D, 1), jnp.float32) * s, 'scorer_b': jnp.zeros((1,), jnp.float32)}
    _L0_attn_all = _L0_attn_setup()
    _L0_attn_in = {k: v for k, v in _L0_attn_all.items() if k in ('norm_w', 'w_q', 'w_k', 'w_v', 'w_out', 'scorer_w', 'scorer_b')}
    del _L0_attn_all

    def _L0_xattn_setup():
        import jax, jax.numpy as jnp
        import numpy as np
        D_MODEL = 256
        NUM_HEADS = 16
        HEAD_DIM = D_MODEL // NUM_HEADS
        key = jax.random.key(seed)
        ks = jax.random.split(key, 10)
        B, SQ, SKV = (2, 512, 512)
        s = 1.0 / np.sqrt(D_MODEL)
        inp = {'query': jax.random.normal(ks[0], (B, SQ, D_MODEL), jnp.float32), 'key_value': jax.random.normal(ks[1], (B, SKV, D_MODEL), jnp.float32), 'Wq': jax.random.normal(ks[2], (D_MODEL, D_MODEL), jnp.float32) * s, 'bq': jnp.zeros((D_MODEL,), jnp.float32), 'Wk': jax.random.normal(ks[3], (D_MODEL, D_MODEL), jnp.float32) * s, 'bk': jnp.zeros((D_MODEL,), jnp.float32), 'Wv': jax.random.normal(ks[4], (D_MODEL, D_MODEL), jnp.float32) * s, 'bv': jnp.zeros((D_MODEL,), jnp.float32), 'Wo': jax.random.normal(ks[5], (D_MODEL, D_MODEL), jnp.float32) * s, 'bo': jnp.zeros((D_MODEL,), jnp.float32)}
        return inp
    _L0_xattn_all = _L0_xattn_setup()
    _L0_xattn_in = {k: v for k, v in _L0_xattn_all.items() if k in ('Wq', 'bq', 'Wk', 'bk', 'Wv', 'bv', 'Wo', 'bo')}
    del _L0_xattn_all

    def _L0_ffn_setup():
        import jax, jax.numpy as jnp
        import numpy as np
        B, S, D = (2, 128, 256)
        E, K, I = (16, 8, 256)
        I_SH = 256
        ROUTE_SCALE = 2.826
        key = jax.random.key(seed)
        ks = jax.random.split(key, 8)
        s = 0.02
        return {'x': jax.random.normal(ks[0], (B, S, D), dtype=jnp.float32), 'gate_w': jax.random.normal(ks[1], (E, D), dtype=jnp.float32) * s, 'expert_bias': jnp.zeros((E,), dtype=jnp.float32), 'w_gate': jax.random.normal(ks[2], (E, I, D), dtype=jnp.float32) * s, 'w_up': jax.random.normal(ks[3], (E, I, D), dtype=jnp.float32) * s, 'w_down': jax.random.normal(ks[4], (E, D, I), dtype=jnp.float32) * s, 'shared_gate_w': jax.random.normal(ks[5], (I_SH, D), dtype=jnp.float32) * s, 'shared_up_w': jax.random.normal(ks[6], (I_SH, D), dtype=jnp.float32) * s, 'shared_down_w': jax.random.normal(ks[7], (D, I_SH), dtype=jnp.float32) * s}
    _L0_ffn_all = _L0_ffn_setup()
    _L0_ffn_in = {k: v for k, v in _L0_ffn_all.items() if k in ('gate_w', 'expert_bias', 'w_gate', 'w_up', 'w_down', 'shared_gate_w', 'shared_up_w', 'shared_down_w')}
    del _L0_ffn_all

    def _L1_attn_setup():
        import jax, jax.numpy as jnp
        import numpy as np
        EPS = 1e-05

        def layer_norm(x, gamma, beta):
            mu = jnp.mean(x, axis=-1, keepdims=True)
            var = jnp.var(x, axis=-1, keepdims=True)
            return (x - mu) * jax.lax.rsqrt(var + EPS) * gamma + beta
        key = jax.random.key(seed)
        ks = jax.random.split(key, 8)
        T, B, E, H, K = (512, 2, 256, 16, 64)
        x = jax.random.normal(ks[0], (T, B, E), dtype=jnp.float32)
        attn_mask = jnp.where(jnp.tril(jnp.ones((T, T), dtype=bool)), 0.0, -1000000000.0).astype(jnp.float32)

        def xavier(k, shape, gain):
            fan_out, fan_in = shape
            std = gain * np.sqrt(2.0 / (fan_in + fan_out))
            return jax.random.normal(k, shape, dtype=jnp.float32) * std
        Wq = xavier(ks[1], (H * K, E), 1.0)
        Wk = xavier(ks[2], (K, E), 1.0)
        Wv = xavier(ks[3], (E, E), 1.0)
        return {'x': x, 'attn_mask': attn_mask, 'Wq': Wq, 'bq': jnp.zeros((H * K,), jnp.float32), 'Wk': Wk, 'bk': jnp.zeros((K,), jnp.float32), 'Wv': Wv, 'bv': jnp.zeros((E,), jnp.float32), 'k_gamma': jnp.ones((K,), jnp.float32), 'k_beta': jnp.zeros((K,), jnp.float32), 'v_gamma': jnp.ones((E,), jnp.float32), 'v_beta': jnp.zeros((E,), jnp.float32)}
    _L1_attn_all = _L1_attn_setup()
    _L1_attn_in = {k: v for k, v in _L1_attn_all.items() if k in ('attn_mask', 'Wq', 'bq', 'Wk', 'bk', 'Wv', 'bv', 'k_gamma', 'k_beta', 'v_gamma', 'v_beta')}
    del _L1_attn_all

    def _L1_xattn_setup():
        import jax, jax.numpy as jnp
        import numpy as np
        D_MODEL = 256
        N_HEADS = 16
        HEAD_DIM = D_MODEL // N_HEADS

        def sparsemax(x):
            x = x - jnp.max(x, axis=-1, keepdims=True)
            zs = -jnp.sort(-x, axis=-1)
            L = x.shape[-1]
            rho = jnp.arange(1, L + 1, dtype=x.dtype)
            cssv = jnp.cumsum(zs, axis=-1) - 1.0
            support = zs > cssv / rho
            k = jnp.maximum(jnp.sum(support, axis=-1, keepdims=True), 1)
            tau = jnp.take_along_axis(cssv, k - 1, axis=-1) / k.astype(x.dtype)
            return jnp.clip(x - tau, 0.0)

        def _split_heads(x):
            B, L, _ = x.shape
            return x.reshape(B, L, N_HEADS, HEAD_DIM).transpose(0, 2, 1, 3)
        key = jax.random.key(seed)
        ks = jax.random.split(key, 11)
        B, L = (2, 512)
        s = 0.02
        inp = {'q': jax.random.normal(ks[0], (B, L, D_MODEL), jnp.float32), 'k': jax.random.normal(ks[1], (B, L, D_MODEL), jnp.float32), 'v': jax.random.normal(ks[2], (B, L, D_MODEL), jnp.float32), 'Wq': jax.random.normal(ks[3], (D_MODEL, D_MODEL), jnp.float32) * s, 'bq': jnp.zeros((D_MODEL,), jnp.float32), 'Wk': jax.random.normal(ks[4], (D_MODEL, D_MODEL), jnp.float32) * s, 'bk': jnp.zeros((D_MODEL,), jnp.float32), 'Wv': jax.random.normal(ks[5], (D_MODEL, D_MODEL), jnp.float32) * s, 'bv': jnp.zeros((D_MODEL,), jnp.float32), 'Wo': jax.random.normal(ks[6], (D_MODEL, D_MODEL), jnp.float32) * s, 'bo': jnp.zeros((D_MODEL,), jnp.float32)}
        return inp
    _L1_xattn_all = _L1_xattn_setup()
    _L1_xattn_in = {k: v for k, v in _L1_xattn_all.items() if k in ('Wq', 'bq', 'Wk', 'bk', 'Wv', 'bv', 'Wo', 'bo')}
    del _L1_xattn_all

    def _L1_ffn_setup():
        import jax, jax.numpy as jnp
        import numpy as np
        B, S, D, T = (4, 1024, 256, 8)
        key = jax.random.key(seed)
        k1, k2, k3, k4 = jax.random.split(key, 4)
        x = jax.random.normal(k1, (B, S, D), dtype=jnp.float32)
        tile_sigs = jax.random.normal(k2, (T, D), dtype=jnp.float32)
        bound = 1.0 / np.sqrt(D)
        W = jax.random.uniform(k3, (T, D, D), minval=-bound, maxval=bound, dtype=jnp.float32)
        b = jax.random.uniform(k4, (T, D), minval=-bound, maxval=bound, dtype=jnp.float32)
        return {'x': x, 'tile_sigs': tile_sigs, 'W': W, 'b': b}
    _L1_ffn_all = _L1_ffn_setup()
    _L1_ffn_in = {k: v for k, v in _L1_ffn_all.items() if k in ('tile_sigs', 'W', 'b')}
    del _L1_ffn_all
    return {'x': x, 'ctx_1024': ctx_1024, 'L0_attn_norm_w': _L0_attn_in['norm_w'], 'L0_attn_w_q': _L0_attn_in['w_q'], 'L0_attn_w_k': _L0_attn_in['w_k'], 'L0_attn_w_v': _L0_attn_in['w_v'], 'L0_attn_w_out': _L0_attn_in['w_out'], 'L0_attn_scorer_w': _L0_attn_in['scorer_w'], 'L0_attn_scorer_b': _L0_attn_in['scorer_b'], 'L0_xattn_Wq': _L0_xattn_in['Wq'], 'L0_xattn_bq': _L0_xattn_in['bq'], 'L0_xattn_Wk': _L0_xattn_in['Wk'], 'L0_xattn_bk': _L0_xattn_in['bk'], 'L0_xattn_Wv': _L0_xattn_in['Wv'], 'L0_xattn_bv': _L0_xattn_in['bv'], 'L0_xattn_Wo': _L0_xattn_in['Wo'], 'L0_xattn_bo': _L0_xattn_in['bo'], 'L0_ffn_gate_w': _L0_ffn_in['gate_w'], 'L0_ffn_expert_bias': _L0_ffn_in['expert_bias'], 'L0_ffn_w_gate': _L0_ffn_in['w_gate'], 'L0_ffn_w_up': _L0_ffn_in['w_up'], 'L0_ffn_w_down': _L0_ffn_in['w_down'], 'L0_ffn_shared_gate_w': _L0_ffn_in['shared_gate_w'], 'L0_ffn_shared_up_w': _L0_ffn_in['shared_up_w'], 'L0_ffn_shared_down_w': _L0_ffn_in['shared_down_w'], 'L1_attn_attn_mask': _L1_attn_in['attn_mask'], 'L1_attn_Wq': _L1_attn_in['Wq'], 'L1_attn_bq': _L1_attn_in['bq'], 'L1_attn_Wk': _L1_attn_in['Wk'], 'L1_attn_bk': _L1_attn_in['bk'], 'L1_attn_Wv': _L1_attn_in['Wv'], 'L1_attn_bv': _L1_attn_in['bv'], 'L1_attn_k_gamma': _L1_attn_in['k_gamma'], 'L1_attn_k_beta': _L1_attn_in['k_beta'], 'L1_attn_v_gamma': _L1_attn_in['v_gamma'], 'L1_attn_v_beta': _L1_attn_in['v_beta'], 'L1_xattn_Wq': _L1_xattn_in['Wq'], 'L1_xattn_bq': _L1_xattn_in['bq'], 'L1_xattn_Wk': _L1_xattn_in['Wk'], 'L1_xattn_bk': _L1_xattn_in['bk'], 'L1_xattn_Wv': _L1_xattn_in['Wv'], 'L1_xattn_bv': _L1_xattn_in['bv'], 'L1_xattn_Wo': _L1_xattn_in['Wo'], 'L1_xattn_bo': _L1_xattn_in['bo'], 'L1_ffn_tile_sigs': _L1_ffn_in['tile_sigs'], 'L1_ffn_W': _L1_ffn_in['W'], 'L1_ffn_b': _L1_ffn_in['b']}

def reference(x, ctx_1024, L0_attn_norm_w, L0_attn_w_q, L0_attn_w_k, L0_attn_w_v, L0_attn_w_out, L0_attn_scorer_w, L0_attn_scorer_b, L0_xattn_Wq, L0_xattn_bq, L0_xattn_Wk, L0_xattn_bk, L0_xattn_Wv, L0_xattn_bv, L0_xattn_Wo, L0_xattn_bo, L0_ffn_gate_w, L0_ffn_expert_bias, L0_ffn_w_gate, L0_ffn_w_up, L0_ffn_w_down, L0_ffn_shared_gate_w, L0_ffn_shared_up_w, L0_ffn_shared_down_w, L1_attn_attn_mask, L1_attn_Wq, L1_attn_bq, L1_attn_Wk, L1_attn_bk, L1_attn_Wv, L1_attn_bv, L1_attn_k_gamma, L1_attn_k_beta, L1_attn_v_gamma, L1_attn_v_beta, L1_xattn_Wq, L1_xattn_bq, L1_xattn_Wk, L1_xattn_bk, L1_xattn_Wv, L1_xattn_bv, L1_xattn_Wo, L1_xattn_bo, L1_ffn_tile_sigs, L1_ffn_W, L1_ffn_b):
    import jax
    import jax.numpy as jnp

    def _L0_attn_ref(x, norm_w, w_q, w_k, w_v, w_out, scorer_w, scorer_b):
        import jax, jax.numpy as jnp
        import numpy as np
        H = 16
        HD = 64
        W = 256
        G = 64
        EPS = 1e-06
        NEG = -1e+30
        B, S, D = x.shape
        h = x * jax.lax.rsqrt(jnp.mean(x * x, axis=-1, keepdims=True) + EPS) * norm_w

        def proj(w):
            return jnp.einsum('bsd,de->bse', h, w).reshape(B, S, H, HD).transpose(0, 2, 1, 3)
        q, k, v = (proj(w_q), proj(w_k), proj(w_v))
        scale = HD ** (-0.5)
        nW = S // W
        qw = q.reshape(B, H, nW, W, HD)
        kw = k.reshape(B, H, nW, W, HD)
        vw = v.reshape(B, H, nW, W, HD)
        ll = jnp.einsum('bhnqd,bhnkd->bhnqk', qw, kw) * scale
        cm = jnp.tril(jnp.ones((W, W), bool))
        ll = jnp.where(cm, ll, NEG).reshape(B, H, S, W)
        scores = (jnp.einsum('bsd,do->bso', h, scorer_w) + scorer_b)[..., 0]
        _, idx = jax.lax.top_k(scores, G)
        kg = jnp.take_along_axis(k, idx[:, None, :, None], axis=2)
        vg = jnp.take_along_axis(v, idx[:, None, :, None], axis=2)
        lg = jnp.einsum('bhsd,bhgd->bhsg', q, kg) * scale
        pos = jnp.arange(S)
        gmask = idx[:, None, None, :] <= pos[None, None, :, None]
        lg = jnp.where(gmask, lg, NEG)
        attn = jax.nn.softmax(jnp.concatenate([ll, lg], axis=-1), axis=-1)
        a_loc = attn[..., :W].reshape(B, H, nW, W, W)
        o = jnp.einsum('bhnqk,bhnkd->bhnqd', a_loc, vw).reshape(B, H, S, HD)
        o = o + jnp.einsum('bhsg,bhgd->bhsd', attn[..., W:], vg)
        o = o.transpose(0, 2, 1, 3).reshape(B, S, H * HD)
        return x + jnp.einsum('bse,ed->bsd', o, w_out)

    def _L0_xattn_ref(query, key_value, Wq, bq, Wk, bk, Wv, bv, Wo, bo):
        import jax, jax.numpy as jnp
        import numpy as np
        D_MODEL = 256
        NUM_HEADS = 16
        HEAD_DIM = D_MODEL // NUM_HEADS
        B, SQ, _ = query.shape
        SKV = key_value.shape[1]
        Q = query @ Wq.T + bq
        K = key_value @ Wk.T + bk
        V = key_value @ Wv.T + bv
        Q = Q.reshape(B, SQ, NUM_HEADS, HEAD_DIM).transpose(0, 2, 1, 3)
        K = K.reshape(B, SKV, NUM_HEADS, HEAD_DIM).transpose(0, 2, 1, 3)
        V = V.reshape(B, SKV, NUM_HEADS, HEAD_DIM).transpose(0, 2, 1, 3)
        scores = jnp.einsum('bhqd,bhkd->bhqk', Q, K) / np.sqrt(HEAD_DIM)
        causal = jnp.tril(jnp.ones((SQ, SKV), bool))
        scores = jnp.where(causal[None, None], scores, -jnp.inf)
        attn = jax.nn.softmax(scores, axis=-1)
        out = jnp.einsum('bhqk,bhkd->bhqd', attn, V)
        out = out.transpose(0, 2, 1, 3).reshape(B, SQ, D_MODEL)
        return out @ Wo.T + bo

    def _L0_ffn_ref(x, gate_w, expert_bias, w_gate, w_up, w_down, shared_gate_w, shared_up_w, shared_down_w):
        import jax, jax.numpy as jnp
        import numpy as np
        B, S, D = (2, 128, 256)
        E, K, I = (16, 8, 256)
        I_SH = 256
        ROUTE_SCALE = 2.826
        gates = jnp.einsum('bsd,ed->bse', x, gate_w)
        scores = jax.nn.sigmoid(gates.astype(jnp.float32))
        sel_scores = scores + expert_bias
        _, inds = jax.lax.top_k(sel_scores, K)
        selected = jnp.take_along_axis(scores, inds, axis=-1)
        selected = selected / selected.sum(axis=-1, keepdims=True)
        selected = selected * ROUTE_SCALE
        onehot = jax.nn.one_hot(inds, E, dtype=selected.dtype)
        combine = jnp.einsum('bske,bsk->bse', onehot, selected)
        hg = jnp.einsum('bsd,eid->bsei', x, w_gate)
        hu = jnp.einsum('bsd,eid->bsei', x, w_up)
        h = jax.nn.silu(hg) * hu
        ye = jnp.einsum('bsei,edi->bsed', h, w_down)
        y = jnp.einsum('bsed,bse->bsd', ye, combine).astype(x.dtype)
        g = jnp.einsum('bsd,id->bsi', x, shared_gate_w)
        u = jnp.einsum('bsd,id->bsi', x, shared_up_w)
        y = y + jnp.einsum('bsi,di->bsd', jax.nn.silu(g) * u, shared_down_w)
        return y

    def _L1_attn_ref(x, attn_mask, Wq, bq, Wk, bk, Wv, bv, k_gamma, k_beta, v_gamma, v_beta):
        import jax, jax.numpy as jnp
        import numpy as np
        EPS = 1e-05

        def layer_norm(x, gamma, beta):
            mu = jnp.mean(x, axis=-1, keepdims=True)
            var = jnp.var(x, axis=-1, keepdims=True)
            return (x - mu) * jax.lax.rsqrt(var + EPS) * gamma + beta
        T, B, E = x.shape
        K = Wk.shape[0]
        H = Wq.shape[0] // K
        q = (x @ Wq.T + bq).reshape(T, B, H, K)
        k = layer_norm(x @ Wk.T + bk, k_gamma, k_beta)
        v = layer_norm(x @ Wv.T + bv, v_gamma, v_beta)
        outer = jnp.einsum('tbk,tbd->tbkd', k, v)
        s = jnp.cumsum(outer, axis=0)
        scaling = jax.lax.rsqrt(jnp.arange(1, T + 1, dtype=x.dtype))
        s = s * scaling[:, None, None, None]
        qn = jnp.mean(jax.nn.softmax(q, axis=-1), axis=2)
        attn = jnp.einsum('tbk,tbkd->tbd', qn, s)
        return attn

    def _L1_xattn_ref(q, k, v, Wq, bq, Wk, bk, Wv, bv, Wo, bo):
        import jax, jax.numpy as jnp
        import numpy as np
        D_MODEL = 256
        N_HEADS = 16
        HEAD_DIM = D_MODEL // N_HEADS

        def sparsemax(x):
            x = x - jnp.max(x, axis=-1, keepdims=True)
            zs = -jnp.sort(-x, axis=-1)
            L = x.shape[-1]
            rho = jnp.arange(1, L + 1, dtype=x.dtype)
            cssv = jnp.cumsum(zs, axis=-1) - 1.0
            support = zs > cssv / rho
            k = jnp.maximum(jnp.sum(support, axis=-1, keepdims=True), 1)
            tau = jnp.take_along_axis(cssv, k - 1, axis=-1) / k.astype(x.dtype)
            return jnp.clip(x - tau, 0.0)

        def _split_heads(x):
            B, L, _ = x.shape
            return x.reshape(B, L, N_HEADS, HEAD_DIM).transpose(0, 2, 1, 3)
        qh = _split_heads(q @ Wq + bq)
        kh = _split_heads(k @ Wk + bk)
        vh = _split_heads(v @ Wv + bv)
        scale = HEAD_DIM ** (-0.5)
        scores = jnp.einsum('bhqd,bhkd->bhqk', qh, kh) * scale
        attn = sparsemax(scores)
        out = jnp.einsum('bhqk,bhkd->bhqd', attn, vh)
        B, L = (q.shape[0], q.shape[1])
        out = out.transpose(0, 2, 1, 3).reshape(B, L, D_MODEL)
        return out @ Wo + bo

    def _L1_ffn_ref(x, tile_sigs, W, b):
        import jax, jax.numpy as jnp
        import numpy as np
        B, S, D, T = (4, 1024, 256, 8)
        scores = jnp.einsum('bsd,td->bst', x, jnp.sign(tile_sigs))
        idx = jnp.argmax(scores, axis=-1)
        all_out = jnp.einsum('bsd,tde->bste', x, W) + b[None, None]
        out = jnp.take_along_axis(all_out, idx[:, :, None, None], axis=2)
        return out[:, :, 0, :]
    x = x + _L0_attn_ref(_layernorm(x, axis=-1), L0_attn_norm_w, L0_attn_w_q, L0_attn_w_k, L0_attn_w_v, L0_attn_w_out, L0_attn_scorer_w, L0_attn_scorer_b)
    x = x + _L0_xattn_ref(_layernorm(x, axis=-1), ctx_1024, L0_xattn_Wq, L0_xattn_bq, L0_xattn_Wk, L0_xattn_bk, L0_xattn_Wv, L0_xattn_bv, L0_xattn_Wo, L0_xattn_bo)
    x = x + _L0_ffn_ref(_layernorm(x, axis=-1), L0_ffn_gate_w, L0_ffn_expert_bias, L0_ffn_w_gate, L0_ffn_w_up, L0_ffn_w_down, L0_ffn_shared_gate_w, L0_ffn_shared_up_w, L0_ffn_shared_down_w)
    x = x + _L1_attn_ref(_layernorm(x, axis=-1), L1_attn_attn_mask, L1_attn_Wq, L1_attn_bq, L1_attn_Wk, L1_attn_bk, L1_attn_Wv, L1_attn_bv, L1_attn_k_gamma, L1_attn_k_beta, L1_attn_v_gamma, L1_attn_v_beta)
    x = x + _L1_xattn_ref(_layernorm(x, axis=-1), ctx_1024, ctx_1024, L1_xattn_Wq, L1_xattn_bq, L1_xattn_Wk, L1_xattn_bk, L1_xattn_Wv, L1_xattn_bv, L1_xattn_Wo, L1_xattn_bo)
    x = x + _L1_ffn_ref(_layernorm(x, axis=-1), L1_ffn_tile_sigs, L1_ffn_W, L1_ffn_b)
    return x

_drawn_inputs = setup_inputs


def setup_inputs(seed=0):
    import zlib

    import numpy as np

    out = dict(_drawn_inputs(seed))
    spreads = {'L0_attn_norm_w': (1.0, 0.6),
     'L0_xattn_bq': (0.0, 0.1),
     'L0_xattn_bk': (0.0, 2.0),
     'L0_xattn_bv': (0.0, 0.1),
     'L0_xattn_bo': (0.0, 0.1),
     'L0_ffn_expert_bias': (0.0, 0.827),
     'L1_attn_bq': (0.0, 0.561),
     'L1_attn_bk': (0.0, 0.678),
     'L1_attn_bv': (0.0, 0.397),
     'L1_attn_k_gamma': (1.0, 0.2),
     'L1_attn_k_beta': (0.0, 0.561),
     'L1_attn_v_gamma': (1.0, 0.577),
     'L1_attn_v_beta': (0.0, 0.437),
     'L1_xattn_bq': (0.0, 0.1),
     'L1_xattn_bk': (0.0, 2.0),
     'L1_xattn_bv': (0.0, 0.1),
     'L1_xattn_bo': (0.0, 0.1)}
    factors = {'L0_attn_w_q': 5.699,
     'L0_attn_w_k': 5.536,
     'L0_attn_scorer_w': 2.894,
     'L1_ffn_b': 3.5,
     'L0_ffn_gate_w': 8.563}
    for name, (base, spread) in spreads.items():
        noise = np.random.default_rng([zlib.crc32(name.encode()), seed]).standard_normal(out[name].shape)
        drawn = base * np.exp(spread * noise) if base else spread * noise
        out[name] = jnp.asarray(drawn.astype(out[name].dtype))
    for name, factor in factors.items():
        out[name] = (out[name] * factor).astype(out[name].dtype)
    return out
```

```python
from contextlib import ExitStack

import numpy as np

import concourse.bass as bass
from concourse import mybir

P = 128
B, S, D = 4, 512, 256
KC = D // P
TOK = B * S
NT = S // P

H0, HD0, WIN, G0 = 16, 64, 256, 64
PAIRS = H0 // 2
INNER = H0 * HD0
NWIN = S // WIN
LG = G0 + WIN

HX, HDX = 16, 16
GX = 2
HPG = P // HDX
E, TOPK, I = 16, 8, 256
ROUTE_SCALE = 2.826
H1, K1 = 16, 64
KV1 = K1 + D
T1 = 8
NEG = -1.0e30
BIG = 3.0e38
EPS_LN, EPS_RMS = 1e-5, 1e-6
NEWTON = 8

F32 = mybir.dt.float32
BF16 = mybir.dt.bfloat16
ALU = mybir.AluOpType
ACT = mybir.ActivationFunctionType
AX = mybir.AxisListType

def offsets(parts):
    at, n = {}, 0
    for name, width in parts:
        at[name] = (n, n + width)
        n += width
    return at, n

COLS, NCOLS = offsets([("norm_w", KC), ("scorer_w", KC), ("bq0", KC), ("bk0", KC), ("bo0", KC),
                       ("bq1", KC), ("bk1", KC), ("bo1", KC), ("sigs", KC * T1), ("gate_w", KC * E)])
ROWS, NROWS = offsets([("bv0", D), ("scorer_b", 1), ("expert_bias", E), ("bq", INNER), ("bkv", KV1),
                       ("gkv", KV1), ("betakv", KV1), ("bv1", D)])
CONSTS, NCONSTS = offsets([("ident", P), ("tri", S), ("earlier", 896), ("slots", P), ("pos", NT), ("heads", HPG),
                           ("before", E * E), ("first", T1), ("scal", B), ("onehot", T1 * P)])


def constants():
    c = np.zeros((P, NCONSTS), np.float32)
    p = np.arange(P)[:, None]

    def put(name, v):
        a, b = CONSTS[name]
        c[:, a:b] = v

    put("ident", np.eye(P))
    put("tri", np.where(np.arange(S)[None] - (S - P) <= p, 0.0, NEG))
    put("earlier", (np.arange(896)[None] - (S - P) < p))
    put("slots", np.arange(P)[None] % G0)
    put("pos", np.arange(NT)[None] * P + p)
    put("heads", p // HDX == np.arange(HPG)[None])
    e, f = np.arange(E)[:, None], np.arange(E)[None]
    put("before", (f < e).reshape(1, -1))
    put("first", T1 - np.arange(T1)[None])
    put("scal", 1.0 / (np.sqrt(np.arange(1, B + 1))[None] * H1))
    put("onehot", (p == (np.arange(T1 * P) // P)[None]))
    return c


def program(nc, a):
    with ExitStack() as ctx:
        def sb(name, shape, dt=F32, c=ctx):
            return c.enter_context(nc.sbuf_tensor(name, shape, dt))

        def sem(name):
            return ctx.enter_context(nc.semaphore(name))

        xT = sb("xT", [P, KC, TOK])
        rows = sb("rows", [P, NROWS])
        cols = sb("cols", [P, NCOLS])
        cst = sb("cst", [P, NCONSTS])
        meanw = sb("meanw", [P, P])
        eps = sb("eps", [P, 2])
        xw = [[sb(f"xw{l}_{n}", [P, KC, D]) for n in "qkvo"] for l in range(2)]
        wq1 = sb("wq1", [P, KC, INNER])
        wkv1 = sb("wkv1", [P, KC, KV1])
        wt1 = sb("wt1", [P, T1, KC, D])
        bt1 = sb("bt1", [T1, D])

        def col(name):
            lo, hi = COLS[name]
            return cols[:, lo:hi]

        def row(name):
            lo, hi = ROWS[name]
            return rows[:, lo:hi]

        def const(name):
            lo, hi = CONSTS[name]
            return cst[:, lo:hi]

        ident = const("ident")
        ps = ctx.enter_context(nc.psum_tensor("ps", [P, 8, 512], F32))
        S_BANKS, PT_BANK, O_BANK, G_BANK = 3, 3, 5, 6

        with ExitStack() as st:
            aw = [sb(f"aw_{n}", [P, KC, INNER], c=st) for n in "qkv"] + [sb("aw_o", [P, PAIRS, D], c=st)]
            a_h = sb("a_h", [P, KC, S], c=st)
            a_xc = sb("a_xc", [P, KC, S], c=st)
            a_sq = sb("a_sq", [P, KC, S], c=st)
            a_r = sb("a_r", [P, 2, S], c=st)
            a_q = sb("a_q", [P, 2, S], c=st)
            a_kz = sb("a_kz", [P, 2, 2, NWIN, LG], c=st)
            a_v = sb("a_v", [P, 2, NT, P], c=st)
            a_vg = sb("a_vg", [P, 2, P], c=st)
            a_scw = sb("a_scw", [P, KC, P], c=st)
            a_tokid = sb("a_tokid", [P, NT, P], c=st)
            a_sc = sb("a_sc", [P, S], c=st)
            a_junk = sb("a_junk", [P, S], c=st)
            a_col = sb("a_col", [P, 4, NT], c=st)
            a_sel = sb("a_sel", [P, NT, P], c=st)
            a_hg = sb("a_hg", [P, KC, P], c=st)
            a_mask = sb("a_mask", [P, NT, 2, LG], c=st)
            a_s = sb("a_s", [P, 3, LG], c=st)
            a_p = sb("a_p", [P, 3, 2 * LG], c=st)
            a_mn = sb("a_mn", [P, 64], c=st)
            a_den = sb("a_den", [P, 64], c=st)
            a_rd = sb("a_rd", [P, 64], c=st)
            a_pt = sb("a_pt", [P, 2, 5, WIN], c=st)
            a_o = sb("a_o", [P, PAIRS, S], c=st)

        with ExitStack() as st:
            x_h = sb("x_h", [P, KC, S], c=st)
            x_xc = sb("x_xc", [P, KC, S], c=st)
            x_sq = sb("x_sq", [P, KC, S], c=st)
            x_o = x_sq
            x_r = sb("x_r", [P, 2, S], c=st)
            x_c = sb("x_c", [P, KC, S], c=st)
            x_q = sb("x_q", [P, GX, S], c=st)
            x_k = sb("x_k", [P, S], c=st)
            x_kz = sb("x_kz", [P, HPG, S], c=st)
            x_vz = sb("x_vz", [P, NT, HPG * (P + HDX)], c=st)
            x_pt = sb("x_pt", [P, 2, NT, S], c=st)
            x_s = sb("x_s", [P, 2, 2, NT, S], c=st)
            x_ja = sb("x_ja", [P, 2, NT, S], BF16, c=st)
            x_jd = sb("x_jd", [P, 2, NT, S], BF16, c=st)
            x_st = sb("x_st", [P, 8, 64], c=st)
        with ExitStack() as st:
            m_hc, m_xc, m_sq, m_r = (sb("m_" + n, [P, KC, S], c=st) for n in ("hc", "xc", "sq", "r"))
            m_h = sb("m_h", [P, KC, TOK], c=st)
            m_w17 = sb("m_w17", [P, NT, E + 1], c=st)
            m_comb = sb("m_comb", [E + 1, TOK], c=st)
            m_sg, m_sel = (sb("m_" + n, [P, NT, E], c=st) for n in ("sg", "sel"))
            m_sum = sb("m_sum", [P, NT], c=st)
            m_gt, m_eq = (sb("m_" + n, [P, NT, E, E], c=st) for n in ("gt", "eq"))
            m_wg, m_wu, m_wd = (sb("m_" + n, [P, 2, KC, D], c=st) for n in ("wg", "wu", "wd"))
            m_cb = sb("m_cb", [P, 2, TOK], c=st)
            m_g, m_m = (sb("m_" + n, [P, 2, S], c=st) for n in ("g", "m"))
            m_a = sb("m_a", [P, 2, KC, S], c=st)
        with ExitStack() as st:
            n_h, n_xc, n_sq, n_r = (sb("n_" + n, [P, KC, S], c=st) for n in ("h", "xc", "sq", "r"))
            n_hist = sb("n_hist", [P, NT, B, KV1], c=st)
            n_kv = sb("n_kv", [P, NT, KV1], c=st)
            n_bs, n_ba = sb("n_bs", [P, NT, 2, 6], c=st), sb("n_ba", [P, NT, 2, 2], c=st)
            n_mv = sb("n_mv", [P, 2, NT, 2], c=st)
            n_q = sb("n_q", [P, 3, INNER], c=st)
            n_sm = sb("n_sm", [P, 3, NT, H1], c=st)
            n_qn = sb("n_qn", [P, 2, K1], c=st)
            n_jk, n_d = sb("n_jk", [P, B, K1], c=st), sb("n_d", [P, B], c=st)
            n_y = sb("n_y", [P, NT, D], c=st)
        with ExitStack() as st:
            f_h, f_xc, f_sq, f_r = (sb("f_" + n, [P, KC, S], c=st) for n in ("h", "xc", "sq", "r"))
            f_sg = sb("f_sg", [P, KC * T1], c=st)
            f_one = sb("f_one", [T1, T1 * P], BF16, c=st)
            f_oh, f_ohb = sb("f_oh", [T1, S], c=st), sb("f_ohb", [T1, S], BF16, c=st)
            f_c, f_mx = sb("f_c", [P, NT, T1], c=st), sb("f_mx", [P, 2, NT], c=st)
            f_m = sb("f_m", [P, 4, KC, S], c=st)

        loads = {n: sem(f"load_{n}") for n in ("x", "small", "aw", "xw0", "xw1", "w1", "wt1")}
        init_pool = sem("init_pool")
        init_dve = sem("init_dve")
        stored = sem("stored")

        class Gen:
            def __init__(self, tag, per):
                self.full = [sem(f"{tag}_full{k}") for k in range(2)]
                self.free = [sem(f"{tag}_free{k}") for k in range(2)]
                self.half = per // 2
                assert per % 2 == 0

            def bank(self, n):
                return ps[:, G_BANK + n % 2, :]

            def claim(self, pe, b, n):
                if n >= 2:
                    pe.wait_ge(self.free[n % 2], b * self.half + n // 2)

            def filled(self, ins, n):
                ins.then_inc(self.full[n % 2], 1)

            def wait(self, eng, b, n):
                eng.wait_ge(self.full[n % 2], b * self.half + n // 2 + 1)

            def read(self, ins, n):
                ins.then_inc(self.free[n % 2], 1)

        class Count:
            def __init__(self, name, per):
                self.sem, self.per, self.n = sem(name), per, 0

            def inc(self, ins):
                ins.then_inc(self.sem, 1)
                self.n += 1
                return self.n

            def wait(self, eng, b, n):
                eng.wait_ge(self.sem, b * self.per + n)

            def link(self, eng, b, ins):
                self.inc(ins)
                self.wait(eng, b, self.n)

            def close(self):
                assert self.n == self.per, (self.sem, self.n, self.per)

        blk = ctx.enter_context(nc.Block())

        carried = {}

        def settle(eng):
            if eng.engine not in carried:
                carried[eng.engine] = sem(f"carried{len(carried)}")
            eng.sem_inc(carried[eng.engine], 1)

        def chunk(b):
            return bass.ds(b * S, S)

        NU = PAIRS * NWIN * 2 * 2
        GA_MEAN, GA_VAR, GA_RMS, GA_TOK, GA_SC, GA_HG, GA_IDX, GA_PAIR = 0, 1, 2, 3, 5, 6, 7, 8
        GA_OUT = GA_PAIR + 4 * PAIRS
        GA = Gen("ga", GA_OUT + 2)
        a_go = sem("a_go")
        A_GO = 2
        a_ln = Count("a_ln", 6)
        a_lnact = Count("a_lnact", 4)
        a_xn = Count("a_xn", 1)
        a_tok = Count("a_tok", 2)
        a_dv = Count("a_dv", 26)
        a_selr = Count("a_selr", 1)
        a_hgr = Count("a_hgr", 1)
        a_qr = Count("a_qr", PAIRS)
        a_vr = Count("a_vr", PAIRS)
        a_kr = Count("a_kr", 8 * PAIRS)
        a_sf = Count("a_sf", NU)
        a_ttr = Count("a_ttr", NU)
        a_exp = Count("a_exp", NU)
        a_rdn = Count("a_rdn", NU)
        a_scl = Count("a_scl", NU)
        a_t = Count("a_t", NU)
        a_pe = [Count("a_pteA", NU // 2), Count("a_pteD", NU // 2)]
        a_pv = Count("a_pv", PAIRS * NWIN)
        a_oev = Count("a_oev", PAIRS)

        def unit_a(n):
            p, r = divmod(n, 8)
            w, r = divmod(r, 4)
            j, h = divmod(r, 2)
            return p, w, j, h

        def a_span(j, h):
            w = G0 + P * (j + 1)
            return slice(0, w) if h else slice(LG - w, LG)

        def a_local(k, h):
            o = G0 + k * P if h else (1 - k) * P
            return slice(o, o + P)

        def a_global(h):
            return slice(0, G0) if h else slice(WIN, LG)

        def probs(n):
            h, sp = n % 2, a_span(n // 2 % 2, n % 2)
            return a_p[:, (n // 2) % 3, h * LG + sp.start:h * LG + sp.stop]

        LAG_E, LAG_T, LAG_PV = 1, 3, 4

        def stage1_pe(pe):
            wq, wk, wv, wo = aw
            pe.wait_ge(loads["x"], 16)
            pe.wait_ge(loads["small"], 48)
            pe.wait_ge(init_pool, 3)
            pe.wait_ge(init_dve, 16)
            with pe.Fori(0, B) as b:
                pe.wait_ge(a_go, b * A_GO + 1)

                def model_mean(n, src):
                    GA.claim(pe, b, n)
                    for k in range(KC):
                        mm = pe.matmul(GA.bank(n), meanw[:], src(k), start=(k == 0), stop=(k == KC - 1))
                    GA.filled(mm, n)

                model_mean(GA_MEAN, lambda k: xT[:, k, chunk(b)])
                a_lnact.wait(pe, b, 1)
                model_mean(GA_VAR, lambda k: a_sq[:, k, :])
                a_lnact.wait(pe, b, 3)
                model_mean(GA_RMS, lambda k: a_sq[:, k, :])
                a_ln.wait(pe, b, 6)
                for k in range(KC):
                    GA.claim(pe, b, GA_TOK + k)
                    for i in range(NT):
                        mm = pe.transpose(GA.bank(GA_TOK + k)[:, i * P:(i + 1) * P], a_h[:, k, i * P:(i + 1) * P], ident)
                    GA.filled(mm, GA_TOK + k)
                GA.claim(pe, b, GA_SC)
                for k in range(KC):
                    mm = pe.matmul(GA.bank(GA_SC), a_scw[:, k, :], a_h[:, k, :], start=(k == 0), stop=(k == KC - 1))
                GA.filled(mm, GA_SC)
                a_selr.wait(pe, b, 1)
                a_tok.wait(pe, b, 2)
                GA.claim(pe, b, GA_HG)
                for k in range(KC):
                    for i in range(NT):
                        mm = pe.matmul(GA.bank(GA_HG)[:, k * P:(k + 1) * P], htok(i, k), a_sel[:, i, :],
                                       start=(i == 0), stop=(i == NT - 1))
                GA.filled(mm, GA_HG)
                GA.claim(pe, b, GA_IDX)
                for i in range(NT):
                    mm = pe.matmul(GA.bank(GA_IDX)[:, 0:G0], a_tokid[:, i, :], a_sel[:, i, 0:G0],
                                   start=(i == 0), stop=(i == NT - 1))
                GA.filled(mm, GA_IDX)
                pe.wait_ge(loads["aw"], 64)
                a_hgr.wait(pe, b, 1)

                def project(p):
                    g = GA_PAIR + 4 * p
                    sl = slice(p * P, (p + 1) * P)
                    for m, w in ((0, wq), (1, wk)):
                        GA.claim(pe, b, g + m)
                        for k in range(KC):
                            mm = pe.matmul(GA.bank(g + m), w[:, k, sl], a_h[:, k, :], start=(k == 0), stop=(k == KC - 1))
                        GA.filled(mm, g + m)
                    GA.claim(pe, b, g + 2)
                    for i in range(NT):
                        for k in range(KC):
                            mm = pe.matmul(GA.bank(g + 2)[:, i * P:(i + 1) * P], a_h[:, k, i * P:(i + 1) * P], wv[:, k, sl],
                                           start=(k == 0), stop=(k == KC - 1))
                    GA.filled(mm, g + 2)
                    GA.claim(pe, b, g + 3)
                    for k in range(KC):
                        pe.matmul(GA.bank(g + 3)[:, 0:P], wk[:, k, sl], a_hg[:, k, :], start=(k == 0), stop=(k == KC - 1))
                    for k in range(KC):
                        mm = pe.matmul(GA.bank(g + 3)[:, P:2 * P], a_hg[:, k, :], wv[:, k, sl], start=(k == 0), stop=(k == KC - 1))
                    GA.filled(mm, g + 3)

                def scores(n):
                    p, w, j, h = unit_a(n)
                    if n % 8 == 0:
                        a_qr.wait(pe, b, p + 1)
                        a_kr.wait(pe, b, 8 * (p + 1))
                    if n >= S_BANKS:
                        a_ttr.wait(pe, b, n - S_BANKS + 1)
                    sp = a_span(j, h)
                    t = (w * 2 + j) * P
                    a_sf.inc(pe.matmul(ps[:, n % S_BANKS, sp], a_q[:, p % 2, t:t + P], a_kz[:, p % 2, h, w, sp],
                                       start=True, stop=True))

                def turn(n):
                    p, w, j, h = unit_a(n)
                    a_scl.wait(pe, b, n + 1)
                    if n >= 2:
                        a_pe[h].wait(pe, b, n // 2)
                    pb = a_p[:, (n // 2) % 3]
                    for k in range(j + 1):
                        lo = a_local(k, h)
                        mm = pe.transpose(ps[:, PT_BANK + h, k * P:(k + 1) * P], pb[:, h * LG + lo.start:h * LG + lo.stop],
                                          ident)
                    if h == 1:
                        mm = pe.transpose(ps[:, PT_BANK + 1, (j + 1) * P:(j + 2) * P], pb[:, WIN:WIN + 2 * G0], ident)
                    a_t.inc(mm)

                def values(wi):
                    p, w = divmod(wi, NWIN)
                    for q in a_pe:
                        q.wait(pe, b, 2 * (wi + 1))
                    if w == 0:
                        a_vr.wait(pe, b, p + 1)
                        if p >= 1:
                            a_oev.wait(pe, b, p)
                    pt = a_pt[:, wi % 2]
                    o = ps[:, O_BANK, w * WIN:(w + 1) * WIN]
                    pe.matmul(o, a_vg[:, p % 2, :], pt[:, 4, :], start=True, stop=False, skip_group_check=True)
                    for h in range(2):
                        for k in range(2):
                            v = a_v[:, p % 2, w * 2 + k, h * HD0:(h + 1) * HD0]
                            mm = pe.matmul(ps[h * HD0:(h + 1) * HD0, O_BANK, w * WIN + k * P:(w + 1) * WIN], v,
                                           pt[:, 2 * h + k, k * P:WIN], start=False, stop=(h == 1 and k == 1),
                                           skip_group_check=True)
                    a_pv.inc(mm)

                project(0)
                for n in range(NU + LAG_PV + 1):
                    if n < NU:
                        scores(n)
                        if n % 8 == 5 and n // 8 + 1 < PAIRS:
                            project(n // 8 + 1)
                    if 0 <= n - LAG_T < NU:
                        turn(n - LAG_T)
                    m = n - LAG_PV - 1
                    if m >= 0 and m % 4 == 3:
                        values(m // 4)
                a_oev.wait(pe, b, PAIRS)
                for k in range(KC):
                    GA.claim(pe, b, GA_OUT + k)
                    for p in range(PAIRS):
                        mm = pe.matmul(GA.bank(GA_OUT + k), wo[:, p, k * P:(k + 1) * P], a_o[:, p, :],
                                       start=(p == 0), stop=(p == PAIRS - 1))
                    GA.filled(mm, GA_OUT + k)

        def htok(i, k):
            return a_htok[:, i, k * P:(k + 1) * P]

        def stage1_act(act):
            act.wait_ge(init_dve, 16)
            with act.Fori(0, B) as b:
                a_ln.wait(act, b, 1)
                a_lnact.inc(act.activation(a_sq[:], a_xc[:], ACT.Square))
                GA.wait(act, b, GA_VAR)
                i = act.activation(a_r[:, 0, :], GA.bank(GA_VAR), ACT.Sqrt, bias=eps[:, 0:1])
                a_lnact.inc(i)
                i_free(act, GA, b, GA_VAR, a_lnact, 2)
                a_ln.wait(act, b, 3)
                a_lnact.inc(act.activation(a_sq[:], a_xc[:], ACT.Square))
                GA.wait(act, b, GA_RMS)
                a_lnact.inc(act.activation(a_r[:, 0, :], GA.bank(GA_RMS), ACT.Sqrt, bias=eps[:, 1:2]))
                i_free(act, GA, b, GA_RMS, a_lnact, 4)
                for k in range(KC):
                    GA.wait(act, b, GA_TOK + k)
                    i = act.copy(a_htok[:, :, k * P:(k + 1) * P], GA.bank(GA_TOK + k).rearrange("p (i c) -> p i c", i=NT))
                    a_tok.inc(i)
                    i_free(act, GA, b, GA_TOK + k, a_tok, k + 1)
                GA.wait(act, b, GA_HG)
                i = act.copy(a_hg[:].rearrange("p k c -> p (k c)"), GA.bank(GA_HG)[:, 0:KC * P])
                a_hgr.inc(i)
                i_free(act, GA, b, GA_HG, a_hgr, 1)

                def evac_qv(p):
                    g = GA_PAIR + 4 * p
                    GA.wait(act, b, g)
                    if p >= 2:
                        a_sf.wait(act, b, 8 * (p - 1))
                    a_qr.inc(act.copy(a_q[:, p % 2, :], GA.bank(g)))
                    i_free(act, GA, b, g, a_qr, p + 1)
                    GA.wait(act, b, g + 2)
                    if p >= 2:
                        a_pv.wait(act, b, NWIN * (p - 1))
                    a_vr.inc(act.copy(a_v[:, p % 2].rearrange("p i c -> p (i c)"), GA.bank(g + 2)))
                    i_free(act, GA, b, g + 2, a_vr, p + 1)

                def exps(n):
                    p, w, j, h = unit_a(n)
                    sp = a_span(j, h)
                    a_ttr.wait(act, b, n + 1)
                    if n >= 6:
                        a_t.wait(act, b, n - 4)
                    a_exp.inc(act.activation(probs(n), a_s[:, n % 3, sp], ACT.Exp, scale=-1.0,
                                             bias=a_mn[:, n:n + 1], accum_out=a_den[:, n:n + 1]))

                def evac_pt(n):
                    p, w, j, h = unit_a(n)
                    wi = n // 4
                    a_t.wait(act, b, n + 1)
                    if wi >= 2:
                        a_pv.wait(act, b, wi - 1)
                    a_pe[0].inc(act.copy(a_pt[:, wi % 2, 0:j + 1, j * P:(j + 1) * P],
                                         ps[:, PT_BANK, 0:(j + 1) * P].rearrange("p (k c) -> p k c", c=P)))

                evac_qv(0)
                for n in range(NU + LAG_T + 1):
                    if 0 <= n - LAG_E < NU:
                        exps(n - LAG_E)
                    if n < NU and n % 8 == 5 and n // 8 + 1 < PAIRS:
                        evac_qv(n // 8 + 1)
                    m = n - LAG_T
                    if 0 <= m < NU and m % 2 == 0:
                        evac_pt(m)

        def i_free(eng, G, b, g, count, n):
            count.wait(eng, b, n)
            eng.sem_inc(G.free[g % 2], 1)

        def stage1_pool(pool):
            with pool.Fori(0, B) as b:
                a_ln.wait(pool, b, 3)
                a_xn.inc(pool.tensor_tensor(xT[:, :, chunk(b)], xT[:, :, chunk(b)], a_xc[:], ALU.add))
                for n in range(NU):
                    p, w, j, h = unit_a(n)
                    a_rdn.wait(pool, b, n + 1)
                    settle(pool)
                    v = probs(n)
                    a_scl.inc(pool.tensor_scalar(v, v, a_rd[:, n:n + 1], 1.0, ALU.mult, ALU.mult))

        a_htok = a_o[:, 0:2, :].rearrange("p a (i c) -> p (a i) c", c=D)

        def stage1_dve(dve):
            tri = const("tri")
            dve.wait_ge(loads["small"], 48)
            for t in range(NT):
                for h in range(2):
                    for k in range(t % 2 + 1):
                        o = S - P * (t % 2 - k + 1)
                        dve.tensor_copy(a_mask[:, t, h, a_local(k, h)], tri[:, o:o + P]).then_inc(init_dve, 1)
            dve.tensor_copy(a_scw[:], col("scorer_w").unsqueeze(2).broadcast_to([P, KC, P])).then_inc(init_dve, 1)
            dve.tensor_copy(a_tokid[:], const("pos").unsqueeze(2).broadcast_to([P, NT, P])).then_inc(init_dve, 1)
            dve.wait_ge(init_dve, 16)
            dve.wait_ge(init_pool, 3)
            dve.wait_ge(loads["x"], 16)
            dve.memset(eps[0:1, 0:1], EPS_LN).then_inc(a_go, 1)
            with dve.Fori(0, B) as b:
                lk = lambda ins: a_ln.link(dve, b, ins)
                x = xT[:, :, chunk(b)]
                dve.wait_ge(a_go, b * A_GO + 1)
                GA.wait(dve, b, GA_MEAN)
                lk(dve.tensor_tensor(a_xc[:], x, GA.bank(GA_MEAN).unsqueeze(1).broadcast_to([P, KC, S]), ALU.subtract))
                dve.sem_inc(GA.free[GA_MEAN % 2], 1)
                a_lnact.wait(dve, b, 2)
                lk(dve.reciprocal(a_r[:, 1, :], a_r[:, 0, :]))
                lk(dve.tensor_tensor(a_xc[:], a_xc[:], a_r[:, 1, :].unsqueeze(1).broadcast_to([P, KC, S]), ALU.mult))
                a_lnact.wait(dve, b, 4)
                lk(dve.reciprocal(a_r[:, 1, :], a_r[:, 0, :]))
                for k in range(KC):
                    a_ln.inc(dve.scalar_tensor_tensor(a_h[:, k, :], a_xc[:, k, :], col("norm_w")[:, k:k + 1],
                                                      a_r[:, 1, :], ALU.mult, ALU.mult))
                ch = lambda ins: a_dv.link(dve, b, ins)
                GA.wait(dve, b, GA_SC)
                ch(dve.tensor_scalar(a_sc[:], GA.bank(GA_SC), row("scorer_b"), None, ALU.add))
                dve.sem_inc(GA.free[GA_SC % 2], 1)
                for i in range(NT):
                    ch(dve.tensor_tensor_reduce(a_junk[:, 0:P], a_sc[:, i * P:(i + 1) * P], ident, 1.0, 0.0,
                                                ALU.mult, ALU.add, a_col[:, 0, i:i + 1]))
                for i in range(NT):
                    ch(dve.tensor_scalar(a_junk[:], a_sc[:], a_col[:, 0, i:i + 1], None, ALU.is_gt, ALU.add,
                                         accum_out=a_col[:, 1, i:i + 1]))
                    o = S - P - i * P
                    ch(dve.scalar_tensor_tensor(a_junk[:], a_sc[:], a_col[:, 0, i:i + 1], const("earlier")[:, o:o + S],
                                                ALU.is_equal, ALU.mult, accum_out=a_col[:, 2, i:i + 1]))
                ch(dve.tensor_tensor(a_col[:, 3, :], a_col[:, 1, :], a_col[:, 2, :], ALU.add))
                for i in range(NT):
                    ch(dve.tensor_scalar(a_sel[:, i, :], const("slots"), a_col[:, 3, i:i + 1], None, ALU.is_equal))
                a_selr.inc(dve.tensor_copy(a_col[0:1, 0, 0:1], a_col[0:1, 0, 0:1]))
                GA.wait(dve, b, GA_IDX)
                for t in range(NT):
                    for h in range(2):
                        ch(dve.tensor_scalar(a_mask[:, t, h, a_global(h)], GA.bank(GA_IDX)[:, 0:G0],
                                             const("pos")[:, t:t + 1], NEG, ALU.is_gt, ALU.mult))
                dve.sem_inc(GA.free[GA_IDX % 2], 1)

                def evac_k(p):
                    g = GA_PAIR + 4 * p
                    GA.wait(dve, b, g + 1)
                    if p >= 2:
                        a_sf.wait(dve, b, 8 * (p - 1))
                    for h in range(2):
                        r = slice(h * HD0, (h + 1) * HD0)
                        kb = ps[r, G_BANK + (g + 1) % 2, :].rearrange("p (w k c) -> p w k c", w=NWIN, c=P)
                        for k in range(2):
                            a_kr.inc(dve.tensor_copy(a_kz[r, p % 2, h, :, a_local(k, h)], kb[:, :, k, :]))
                    a_kr.wait(dve, b, a_kr.n)
                    dve.sem_inc(GA.free[(g + 1) % 2], 1)
                    GA.wait(dve, b, g + 3)
                    if p >= 2:
                        a_pv.wait(dve, b, NWIN * (p - 1))
                    for h in range(2):
                        r = slice(h * HD0, (h + 1) * HD0)
                        gb = ps[r, G_BANK + (g + 3) % 2, :]
                        a_kr.inc(dve.tensor_copy(a_kz[r, p % 2, h, :, a_global(h)], gb[:, 0:G0].unsqueeze(1).broadcast_to([HD0, NWIN, G0])))
                        a_kr.inc(dve.tensor_copy(a_vg[r, p % 2, h * HD0:(h + 1) * HD0], gb[:, P + h * HD0:P + (h + 1) * HD0]))
                    a_kr.wait(dve, b, a_kr.n)
                    dve.sem_inc(GA.free[(g + 3) % 2], 1)

                def ttr(n):
                    p, w, j, h = unit_a(n)
                    sp = a_span(j, h)
                    a_sf.wait(dve, b, n + 1)
                    if n >= 3:
                        a_exp.wait(dve, b, n - 2)
                    settle(dve)
                    a_ttr.inc(dve.tensor_tensor_reduce(a_s[:, n % 3, sp], ps[:, n % S_BANKS, sp],
                                                       a_mask[:, w * 2 + j, h, sp], -HD0 ** -0.5, BIG, ALU.add, ALU.min,
                                                       a_mn[:, n:n + 1]))

                def recip(n):
                    a_exp.wait(dve, b, n + 1)
                    a_rdn.inc(dve.reciprocal(a_rd[:, n:n + 1], a_den[:, n:n + 1]))

                def evac_pt(n):
                    p, w, j, h = unit_a(n)
                    wi = n // 4
                    a_t.wait(dve, b, n + 1)
                    if wi >= 2:
                        a_pv.wait(dve, b, wi - 1)
                    v = ps[:, PT_BANK + 1, 0:(j + 2) * P].rearrange("p (k c) -> p k c", c=P)
                    step = 2 if j == 0 else 1
                    a_pe[1].inc(dve.tensor_copy(a_pt[:, wi % 2, 2:5:step, j * P:(j + 1) * P], v))

                def evac_o(p):
                    a_pv.wait(dve, b, NWIN * (p + 1))
                    a_oev.inc(dve.tensor_copy(a_o[:, p, :], ps[:, O_BANK, :]))

                evac_k(0)
                for n in range(NU + LAG_PV + 3):
                    if n < NU:
                        ttr(n)
                    if 0 <= n - LAG_E < NU:
                        recip(n - LAG_E)
                    if n < NU and n % 8 == 5 and n // 8 + 1 < PAIRS:
                        evac_k(n // 8 + 1)
                    m = n - LAG_T
                    if 0 <= m < NU and m % 2 == 1:
                        evac_pt(m)
                    m = n - LAG_PV - 2
                    if m >= 0 and m % 8 == 7:
                        evac_o(m // 8)
                a_xn.wait(dve, b, 1)
                for k in range(KC):
                    GA.wait(dve, b, GA_OUT + k)
                    xk = xT[:, k, chunk(b)]
                    dve.tensor_tensor(xk, xk, GA.bank(GA_OUT + k), ALU.add).then_inc(a_go, 1)
                dve.wait_ge(a_go, b * A_GO + 3)
                for k in range(KC):
                    dve.sem_inc(GA.free[(GA_OUT + k) % 2], 1)
            for q in (a_ln, a_dv, a_selr, a_kr, a_ttr, a_rdn, a_pe[1], a_oev):
                q.close()

        SCX = HDX ** -0.5
        NG = HPG * NT
        NX = GX * NG
        NQ = GX * HPG

        def cross(l):
            sparse = l == 1
            T = f"x{l}_"
            wq, wk, wv, wo = xw[l]
            bq, bk, bo, bv = col(f"bq{l}"), col(f"bk{l}"), col(f"bo{l}"), row(f"bv{l}")
            X_MEAN, X_VAR, X_GRP, X_OUT = 0, 1, 2, 2 + 3 * GX
            G = Gen(T + "g", X_OUT + KC)
            go = sem(T + "go")
            ln, lnact = Count(T + "ln", 3), Count(T + "lnact", 2)
            cld = sem(T + "ctx")
            cused = Count(T + "cused", GX)
            qr, kr, kz, vr = Count(T + "q", GX), Count(T + "k", GX), Count(T + "kz", GX * HPG), Count(T + "v", GX * NT)
            sf, ttr, ex, rdn, scl = (Count(T + n, NX) for n in ("s", "ttr", "exp", "rdn", "scl"))
            tn = Count(T + "t", NX)
            pte = [Count(T + "pteA", NX // 2), Count(T + "pteD", NX // 2)]
            pv, oev = Count(T + "pv", NQ), Count(T + "oev", GX)
            sev = Count(T + "sev", NX)
            fs = Count(T + "f", NX * NEWTON)
            cn = Count(T + "cnt", NX * NEWTON)
            th = Count(T + "tau", NQ * (2 + 5 * NEWTON))
            pr = Count(T + "p", NX)

            def width(j):
                return S if sparse else P * (j + 1)

            LAG_E, LAG_T, LAG_PV = 1, 3, 4

            def xbuf(n):
                return x_s[:, n // 8 % 2, n // 4 % 2, n % 4, :]

            def probs(n):
                return xbuf(n) if sparse else x_s[:, 1, 0, n % 3, 0:width(n % NT)]

            def f_steps(q, it):
                return 8 * NEWTON * (q // 2) + 8 * it + 4 * (q % 2 + 1)

            def th_steps(q, it):
                base = q // 2 * 2 * (2 + 5 * NEWTON) + 4
                return base if it == 0 else base + (2 * (it - 1) + q % 2 + 1) * 5

            def on_pe(pe):
                def mean(b, n, src):
                    G.claim(pe, b, n)
                    for k in range(KC):
                        mm = pe.matmul(G.bank(n), meanw[:], src(k), start=(k == 0), stop=(k == KC - 1))
                    G.filled(mm, n)

                with pe.Fori(0, B) as b:
                    pe.wait_ge(go, b * KC + 1)
                    mean(b, X_MEAN, lambda k: xT[:, k, chunk(b)])
                    lnact.wait(pe, b, 1)
                    mean(b, X_VAR, lambda k: x_sq[:, k, :])
                    ln.wait(pe, b, 3)
                    pe.wait_ge(loads[f"xw{l}"], 64)

                    def project(g):
                        u = X_GRP + 3 * g
                        sl = slice(g * P, (g + 1) * P)
                        for m, w, src in ((0, wq, x_h), (1, wk, x_c)):
                            if m == 1 and g == 0:
                                pe.wait_ge(cld, b * 16 + 16)
                            G.claim(pe, b, u + m)
                            for k in range(KC):
                                mm = pe.matmul(G.bank(u + m), w[:, k, sl], src[:, k, :], start=(k == 0), stop=(k == KC - 1))
                            G.filled(mm, u + m)
                        G.claim(pe, b, u + 2)
                        for i in range(NT):
                            for k in range(KC):
                                mm = pe.matmul(G.bank(u + 2)[:, i * P:(i + 1) * P], x_c[:, k, i * P:(i + 1) * P], wv[:, k, sl],
                                               start=(k == 0), stop=(k == KC - 1))
                        G.filled(mm, u + 2)

                    def scores(n):
                        g, hh, j = n // NG, n // NT % HPG, n % NT
                        if hh == 0 and j == 0:
                            qr.wait(pe, b, g + 1)
                        if j == 0:
                            kz.wait(pe, b, n // NT + 1)
                        if n >= S_BANKS:
                            (sev if sparse else ttr).wait(pe, b, n - S_BANKS + 1)
                        W = width(j)
                        sf.inc(pe.matmul(ps[:, n % S_BANKS, 0:W], x_q[:, g, j * P:(j + 1) * P], x_kz[:, hh, 0:W],
                                         start=True, stop=True))

                    def turn(n):
                        (pr if sparse else scl).wait(pe, b, n + 1)
                        if n >= 2:
                            pte[n % 2].wait(pe, b, n // 2)
                        for k in range(width(n % NT) // P):
                            mm = pe.transpose(ps[:, PT_BANK + n % 2, k * P:(k + 1) * P], probs(n)[:, k * P:(k + 1) * P], ident)
                        tn.inc(mm)

                    def values(q):
                        g, hh = divmod(q, HPG)
                        for c in pte:
                            c.wait(pe, b, 2 * (q + 1))
                        if hh == 0:
                            vr.wait(pe, b, NT * (g + 1))
                        for k in range(NT):
                            lo = 0 if sparse else k * P
                            mm = pe.matmul(ps[:, O_BANK, lo:S], x_vz[:, k, hh * P:(hh + 1) * P], x_pt[:, q % 2, k, lo:S],
                                           start=(hh == 0 and k == 0), stop=(hh == HPG - 1 and k == NT - 1),
                                           skip_group_check=True)
                        pv.inc(mm)

                    for g in range(GX):
                        if g:
                            oev.wait(pe, b, g)
                        project(g)
                        N0 = g * NG
                        if not sparse:
                            for n in range(NG + LAG_PV + 1):
                                if n < NG:
                                    scores(N0 + n)
                                if 0 <= n - LAG_T < NG:
                                    turn(N0 + n - LAG_T)
                                m = n - LAG_PV - 1
                                if m >= 0 and m % NT == NT - 1:
                                    values((N0 + m) // NT)
                        else:
                            for n0 in range(0, NG + 8, 8):
                                for n in range(n0, n0 + 8):
                                    if n < NG:
                                        scores(N0 + n)
                                for n in range(n0 - 8, n0):
                                    if n >= 0:
                                        turn(N0 + n)
                                        if n % NT == NT - 1:
                                            values((N0 + n) // NT)
                    oev.wait(pe, b, GX)
                    for k in range(KC):
                        G.claim(pe, b, X_OUT + k)
                        for g in range(GX):
                            mm = pe.matmul(G.bank(X_OUT + k), wo[:, g, k * P:(k + 1) * P], x_o[:, g, :],
                                           start=(g == 0), stop=(g == GX - 1))
                        G.filled(mm, X_OUT + k)

            def on_act(act):
                with act.Fori(0, B) as b:
                    ln.wait(act, b, 1)
                    lnact.inc(act.activation(x_sq[:], x_xc[:], ACT.Square))
                    G.wait(act, b, X_VAR)
                    lnact.inc(act.activation(x_r[:, 0, :], G.bank(X_VAR), ACT.Sqrt, bias=eps[:, 0:1]))
                    i_free(act, G, b, X_VAR, lnact, 2)

                    def evac_pt(n):
                        q = n // NT
                        tn.wait(act, b, n + 1)
                        if q >= 2:
                            pv.wait(act, b, q - 1)
                        W = width(n % NT)
                        j = n % NT
                        pte[0].inc(act.copy(x_pt[:, q % 2, 0:W // P, j * P:(j + 1) * P],
                                            ps[:, PT_BANK, 0:W].rearrange("p (k c) -> p k c", c=P)))

                    for g in range(GX):
                        u = X_GRP + 3 * g
                        G.wait(act, b, u)
                        qr.inc(act.activation(x_q[:, g, :], G.bank(u), ACT.Identity, bias=bq[:, g:g + 1]))
                        i_free(act, G, b, u, qr, g + 1)
                        N0 = g * NG
                        if not sparse:
                            for n in range(NG + LAG_T + 1):
                                m = N0 + n - LAG_E
                                if 0 <= n - LAG_E < NG:
                                    ttr.wait(act, b, m + 1)
                                    if m >= 3:
                                        tn.wait(act, b, m - 2)
                                    ex.inc(act.activation(probs(m), x_s[:, 0, 0, m % 3, 0:width(m % NT)], ACT.Exp, scale=-1.0,
                                                          bias=x_st[:, 0, m:m + 1], accum_out=x_st[:, 1, m:m + 1]))
                                m = n - LAG_T
                                if 0 <= m < NG and m % 2 == 0:
                                    evac_pt(N0 + m)
                        else:
                            for n0 in range(0, NG + 8, 8):
                                quads = range((N0 + n0) // NT, (N0 + n0) // NT + 2)
                                if n0 < NG:
                                    for n in range(N0 + n0, N0 + n0 + 8):
                                        sf.wait(act, b, n + 1)
                                        if n >= 16:
                                            tn.wait(act, b, n - 15)
                                        sev.inc(act.activation(xbuf(n), ps[:, n % S_BANKS, :], ACT.Identity, scale=SCX,
                                                               accum_out=x_st[:, 0, n:n + 1]))
                                for it in range(NEWTON):
                                    if n0 < NG:
                                        for q in quads:
                                            th.wait(act, b, th_steps(q, it))
                                            for n in range(4 * q, 4 * q + 4):
                                                fs.inc(act.activation(x_ja[:, q % 2, n % 4, :], xbuf(n), ACT.Relu,
                                                                      bias=x_st[:, 1, n:n + 1], accum_out=x_st[:, 2, n:n + 1]))
                                    if n0 and it % 2 == 0:
                                        evac_pt(N0 + n0 - 8 + it)

            def on_pool(pool):
                with pool.Fori(0, B) as b:
                    for g in range(GX):
                        kr.wait(pool, b, g + 1)
                        settle(pool)
                        for hh in range(HPG):
                            kz.inc(pool.tensor_scalar(x_kz[:, hh, :], x_k[:], const("heads")[:, hh:hh + 1], 1.0,
                                                      ALU.mult, ALU.mult))
                        if not sparse:
                            for n in range(g * NG, (g + 1) * NG):
                                rdn.wait(pool, b, n + 1)
                                settle(pool)
                                scl.inc(pool.tensor_scalar(probs(n), probs(n), x_st[:, 2, n:n + 1], 1.0, ALU.mult, ALU.mult))

            def on_dve(dve, before, count):
                dve.wait_ge(before, count)
                dve.memset(x_vz[:], 0.0).then_inc(go, 1)
                with dve.Fori(0, B) as b:
                    x = xT[:, :, chunk(b)]
                    dve.wait_ge(go, b * KC + 1)
                    G.wait(dve, b, X_MEAN)
                    ln.link(dve, b, dve.tensor_tensor(x_xc[:], x, G.bank(X_MEAN).unsqueeze(1).broadcast_to([P, KC, S]), ALU.subtract))
                    dve.sem_inc(G.free[X_MEAN % 2], 1)
                    lnact.wait(dve, b, 2)
                    ln.link(dve, b, dve.reciprocal(x_r[:, 1, :], x_r[:, 0, :]))
                    ln.inc(dve.tensor_tensor(x_h[:], x_xc[:], x_r[:, 1, :].unsqueeze(1).broadcast_to([P, KC, S]), ALU.mult))

                    def evac_pt(n):
                        q = n // NT
                        tn.wait(dve, b, n + 1)
                        if q >= 2:
                            pv.wait(dve, b, q - 1)
                        W = width(n % NT)
                        j = n % NT
                        pte[1].inc(dve.tensor_copy(x_pt[:, q % 2, 0:W // P, j * P:(j + 1) * P],
                                                   ps[:, PT_BANK + 1, 0:W].rearrange("p (k c) -> p k c", c=P)))

                    for g in range(GX):
                        u = X_GRP + 3 * g
                        N0 = g * NG
                        G.wait(dve, b, u + 1)
                        kr.link(dve, b, dve.tensor_scalar(x_k[:], G.bank(u + 1), bk[:, g:g + 1], None, ALU.add))
                        dve.sem_inc(G.free[(u + 1) % 2], 1)
                        G.wait(dve, b, u + 2)
                        for i in range(NT):
                            o = x_vz[:, i, :].rearrange("p (h c) -> p h c", h=HPG)[:, :, 0:HDX]
                            vr.inc(dve.tensor_tensor(o, G.bank(u + 2)[:, i * P:(i + 1) * P].rearrange("p (h c) -> p h c", h=HPG),
                                                     bv[:, g * P:(g + 1) * P].rearrange("p (h c) -> p h c", h=HPG), ALU.add))
                        vr.wait(dve, b, vr.n)
                        dve.sem_inc(G.free[(u + 2) % 2], 1)
                        dve.sem_inc(cused.sem, 1)
                        if not sparse:
                            for n in range(NG + LAG_T + 1):
                                if n < NG:
                                    m = N0 + n
                                    sf.wait(dve, b, m + 1)
                                    if m >= 3:
                                        ex.wait(dve, b, m - 2)
                                    settle(dve)
                                    W = width(m % NT)
                                    ttr.inc(dve.tensor_tensor_reduce(x_s[:, 0, 0, m % 3, 0:W], ps[:, m % S_BANKS, 0:W],
                                                                     const("tri")[:, S - W:S], -SCX, BIG, ALU.add, ALU.min,
                                                                     x_st[:, 0, m:m + 1]))
                                m = N0 + n - LAG_E
                                if 0 <= n - LAG_E < NG:
                                    ex.wait(dve, b, m + 1)
                                    rdn.inc(dve.reciprocal(x_st[:, 2, m:m + 1], x_st[:, 1, m:m + 1]))
                                m = n - LAG_T
                                if 0 <= m < NG and m % 2 == 1:
                                    evac_pt(N0 + m)
                        else:
                            for n0 in range(0, NG + 8, 8):
                                quads = range((N0 + n0) // NT, (N0 + n0) // NT + 2)
                                if n0 < NG:
                                    for q in quads:
                                        sev.wait(dve, b, 4 * (q + 1))
                                        v = slice(4 * q, 4 * q + 4)
                                        th.link(dve, b, dve.tensor_scalar(x_st[:, 3, v], x_st[:, 0, v], -1.0, 1.0 / S, ALU.add, ALU.mult))
                                        th.inc(dve.tensor_scalar(x_st[:, 1, v], x_st[:, 3, v], -1.0, None, ALU.mult))
                                for it in range(NEWTON):
                                    if n0 < NG:
                                        for q in quads:
                                            v = slice(4 * q, 4 * q + 4)
                                            for n in range(4 * q, 4 * q + 4):
                                                cn.inc(dve.tensor_scalar(x_jd[:, q % 2, n % 4, :], xbuf(n), x_st[:, 3, n:n + 1], None,
                                                                         ALU.is_gt, ALU.add, accum_out=x_st[:, 4, n:n + 1]))
                                            cn.wait(dve, b, cn.n)
                                            th.link(dve, b, dve.tensor_scalar(x_st[:, 5, v], x_st[:, 4, v], 1.0, None, ALU.max))
                                            th.link(dve, b, dve.reciprocal(x_st[:, 5, v], x_st[:, 5, v]))
                                            fs.wait(dve, b, f_steps(q, it))
                                            th.link(dve, b, dve.scalar_tensor_tensor(x_st[:, 6, v], x_st[:, 2, v], -1.0, x_st[:, 5, v],
                                                                                     ALU.add, ALU.mult))
                                            th.inc(dve.tensor_tensor(x_st[:, 3, v], x_st[:, 3, v], x_st[:, 6, v], ALU.add))
                                            th.link(dve, b, dve.tensor_tensor(x_st[:, 1, v], x_st[:, 1, v], x_st[:, 6, v], ALU.subtract))
                                    if n0 and it % 2 == 1:
                                        evac_pt(N0 + n0 - 8 + it)
                                if n0 < NG:
                                    for n in range(N0 + n0, N0 + n0 + 8):
                                        pr.inc(dve.tensor_scalar(xbuf(n), xbuf(n), x_st[:, 3, n:n + 1], 0.0, ALU.subtract, ALU.max))
                        pv.wait(dve, b, HPG * (g + 1))
                        oev.inc(dve.tensor_copy(x_o[:, g, :], ps[:, O_BANK, :]))
                    for k in range(KC):
                        G.wait(dve, b, X_OUT + k)
                        xk = xT[:, k, chunk(b)]
                        dve.scalar_tensor_tensor(xk, G.bank(X_OUT + k), bo[:, k:k + 1], xk, ALU.add, ALU.add).then_inc(go, 1)
                    dve.wait_ge(go, b * KC + 1 + KC)
                    for k in range(KC):
                        dve.sem_inc(G.free[(X_OUT + k) % 2], 1)

            return on_pe, on_act, on_pool, on_dve, go, cld, cused

        class Norm:
            def __init__(self, tag, G, h, xc, sq, r):
                self.G, self.h, self.xc, self.sq, self.r = G, h, xc, sq, r
                self.steps, self.act_steps = Count(tag + "ln", 3), Count(tag + "lnact", 2)

            def on_pe(self, pe, b):
                for n, src in ((0, lambda k: xT[:, k, chunk(b)]), (1, lambda k: self.sq[:, k, :])):
                    if n:
                        self.act_steps.wait(pe, b, 1)
                    self.G.claim(pe, b, n)
                    for k in range(KC):
                        mm = pe.matmul(self.G.bank(n), meanw[:], src(k), start=(k == 0), stop=(k == KC - 1))
                    self.G.filled(mm, n)

            def on_act(self, act, b):
                self.steps.wait(act, b, 1)
                self.act_steps.inc(act.activation(self.sq[:], self.xc[:], ACT.Square))
                self.G.wait(act, b, 1)
                self.act_steps.inc(act.activation(self.r[:, 0, :], self.G.bank(1), ACT.Sqrt, bias=eps[:, 0:1]))
                i_free(act, self.G, b, 1, self.act_steps, 2)

            def on_dve(self, dve, b):
                self.G.wait(dve, b, 0)
                m = self.G.bank(0).unsqueeze(1).broadcast_to([P, KC, S])
                self.steps.link(dve, b, dve.tensor_tensor(self.xc[:], xT[:, :, chunk(b)], m, ALU.subtract))
                dve.sem_inc(self.G.free[0], 1)
                self.act_steps.wait(dve, b, 2)
                self.steps.link(dve, b, dve.reciprocal(self.r[:, 1, :], self.r[:, 0, :]))
                rs = self.r[:, 1, :].unsqueeze(1).broadcast_to([P, KC, S])
                self.steps.inc(dve.tensor_tensor(self.h[:], self.xc[:], rs, ALU.mult))

            def ready(self, eng, b):
                self.steps.wait(eng, b, 3)

        EG_GATE, EG_COMB = 2, 3
        EG = Gen("mg", 4)
        e_norm = Norm("m_", EG, m_hc, m_xc, m_sq, m_r)
        e_ones = sem("m_ones")
        e_go = sem("m_go")
        e_hcp = Count("m_hcp", 1)
        e_sig = Count("m_sig", 1)
        e_gate = Count("m_gate", 14)
        e_rec, e_fin = Count("m_rec", 2), Count("m_fin", 1)
        e_comb = sem("m_comb_out")
        e_wl = [sem(f"m_weights{k}") for k in range(2)]
        e_cbl = [sem(f"m_cb{k}") for k in range(2)]
        e_guf, e_silu, e_mul, e_act, e_dn, e_acc = (sem(f"m_{n}") for n in ("gu", "silu", "mul", "act", "down", "acc"))
        UE = 2 * B
        NE = E + 1
        DN_BANK = 4

        def at(eng, s, e, n):
            if not (isinstance(e, int) and e * UE + n <= 0):
                eng.wait_ge(s, e * UE + n)

        def experts(eng, step):
            step(0, 0, 0)
            with eng.Fori(0, E // 2) as i:
                step(i * 2 + 1, 1, i)
                step(i * 2 + 2, 0, i + 1)

        def stage3_pe(pe):
            with pe.Fori(0, B) as b:
                pe.wait_ge(e_go, b + 1)
                e_norm.on_pe(pe, b)
                e_norm.ready(pe, b)
                EG.claim(pe, b, EG_GATE)
                gw = col("gate_w").rearrange("p (k e) -> p k e", k=KC)
                for i in range(NT):
                    for k in range(KC):
                        mm = pe.matmul(EG.bank(EG_GATE)[:, i * E:(i + 1) * E], m_hc[:, k, i * P:(i + 1) * P], gw[:, k, :],
                                       start=(k == 0), stop=(k == KC - 1))
                EG.filled(mm, EG_GATE)
                e_fin.wait(pe, b, 1)
                EG.claim(pe, b, EG_COMB)
                for i in range(NT):
                    mm = pe.transpose(EG.bank(EG_COMB)[0:NE, i * P:(i + 1) * P], m_w17[:, i, :], ident)
                EG.filled(mm, EG_COMB)
            e_hcp.wait(pe, B - 1, 1)

            def down(e, buf, c):
                at(pe, e_act, e, 2 * c + 2)
                for m in range(KC):
                    at(pe, e_acc, e, 2 * c + m - 3)
                    for k in range(KC):
                        mm = pe.matmul(ps[:, DN_BANK + (2 * c + m) % 4, :], m_wd[:, buf, k, m * P:(m + 1) * P],
                                       m_a[:, c % 2, k, :], start=(k == 0), stop=(k == KC - 1))
                    mm.then_inc(e_dn, 1)

            def expert(e, buf, r):
                pe.wait_ge(e_wl[buf], r * 48 + 48)
                for c in range(B):
                    for h in range(2):
                        u = 2 * c + h
                        at(pe, e_mul, e, u - 1)
                        for m, w in ((0, m_wg), (1, m_wu)):
                            for k in range(KC):
                                mm = pe.matmul(ps[:, 2 * h + m, :], w[:, buf, k, h * P:(h + 1) * P],
                                               m_h[:, k, c * S:(c + 1) * S], start=(k == 0), stop=(k == KC - 1))
                        mm.then_inc(e_guf, 1)
                    if c:
                        down(e, buf, c - 1)
                    elif not isinstance(e, int):
                        down(e - 1, 1 - buf, B - 1)
            experts(pe, expert)
            down(E, 0, B - 1)

        def stage3_act(act):
            act.wait_ge(e_ones, 1)
            act.sem_inc(e_go, 1)
            with act.Fori(0, B) as b:
                e_norm.on_act(act, b)
                e_norm.ready(act, b)
                e_hcp.inc(act.copy(m_h[:, :, chunk(b)], m_hc[:]))
                EG.wait(act, b, EG_GATE)
                e_sig.inc(act.activation(m_sg[:].rearrange("p i e -> p (i e)"), EG.bank(EG_GATE)[:, 0:NT * E], ACT.Sigmoid))
                i_free(act, EG, b, EG_GATE, e_sig, 1)
                EG.wait(act, b, EG_COMB)
                act.copy(m_comb[:, chunk(b)], EG.bank(EG_COMB)[0:NE, :]).then_inc(e_go, 1)
                act.wait_ge(e_go, b + 2)
                act.sem_inc(EG.free[EG_COMB % 2], 1)

            def expert(e, buf, r):
                for u in range(UE):
                    at(act, e_guf, e, u + 1)
                    at(act, e_mul, e, u - 1)
                    act.activation(m_g[:, u % 2, :], ps[:, 2 * (u % 2), :], ACT.Silu).then_inc(e_silu, 1)
            experts(act, expert)

        def stage3_pool(pool):
            def expert(e, buf, r):
                pool.wait_ge(e_cbl[buf], r * 16 + 16)
                for u in range(UE):
                    c, h = divmod(u, 2)
                    at(pool, e_mul, e, u + 1)
                    at(pool, e_dn, e, 2 * c - 2)
                    pool.tensor_tensor(m_a[:, c % 2, h, :], m_m[:, u % 2, :], m_cb[:, buf, c * S:(c + 1) * S],
                                       ALU.mult).then_inc(e_act, 1)
            experts(pool, expert)

        def stage3_dve(dve, before, count):
            dve.wait_ge(before, count)
            dve.memset(m_w17[:], 1.0).then_inc(e_ones, 1)
            with dve.Fori(0, B) as b:
                e_norm.on_dve(dve, b)
                ch = lambda ins: e_gate.link(dve, b, ins)
                e_sig.wait(dve, b, 1)
                ch(dve.tensor_tensor(m_sel[:], m_sg[:], row("expert_bias").unsqueeze(1).broadcast_to([P, NT, E]), ALU.add))
                for i in range(NT):
                    o = m_sel[:, i, :].unsqueeze(1).broadcast_to([P, E, E])
                    s = m_sel[:, i, :].unsqueeze(2).broadcast_to([P, E, E])
                    e_gate.inc(dve.tensor_tensor(m_gt[:, i], o, s, ALU.is_gt))
                    e_gate.inc(dve.tensor_tensor(m_eq[:, i], o, s, ALU.is_equal))
                e_gate.wait(dve, b, 9)
                ch(dve.tensor_tensor(m_eq[:].rearrange("p i e f -> p i (e f)"), m_eq[:].rearrange("p i e f -> p i (e f)"),
                                     const("before").unsqueeze(1).broadcast_to([P, NT, E * E]), ALU.mult))
                ch(dve.tensor_tensor(m_gt[:].rearrange("p i e f -> p (i e f)"), m_gt[:].rearrange("p i e f -> p (i e f)"),
                                     m_eq[:].rearrange("p i e f -> p (i e f)"), ALU.add))
                ch(dve.tensor_reduce(m_sel[:], m_gt[:], AX.X, ALU.add))
                ch(dve.scalar_tensor_tensor(m_sel[:], m_sel[:], TOPK - 0.5, m_sg[:], ALU.is_lt, ALU.mult))
                ch(dve.tensor_reduce(m_sum[:], m_sel[:], AX.X, ALU.add))
                e_rec.link(dve, b, dve.reciprocal(m_sum[:], m_sum[:]))
                e_rec.link(dve, b, dve.tensor_tensor(m_sel[:], m_sel[:], m_sum[:].unsqueeze(2).broadcast_to([P, NT, E]), ALU.mult))
                dve.wait_ge(e_go, b + 1)
                e_fin.inc(dve.tensor_scalar(m_w17[:, :, 0:E], m_sel[:], ROUTE_SCALE, None, ALU.mult))

            def acc(e, c):
                for m in range(KC):
                    at(dve, e_dn, e, 2 * c + m + 1)
                    at(dve, e_acc, e, 2 * c + m - 1)
                    xk = xT[:, m, c * S:(c + 1) * S]
                    dve.tensor_tensor(xk, xk, ps[:, DN_BANK + (2 * c + m) % 4, :], ALU.add).then_inc(e_acc, 1)

            def expert(e, buf, r):
                for u in range(UE):
                    at(dve, e_silu, e, u + 1)
                    at(dve, e_act, e, u - 1)
                    dve.tensor_tensor(m_m[:, u % 2, :], m_g[:, u % 2, :], ps[:, 2 * (u % 2) + 1, :], ALU.mult).then_inc(e_mul, 1)
                    if u % 2:
                        if u > 1:
                            acc(e, u // 2 - 1)
                        elif not isinstance(e, int):
                            acc(e - 1, B - 1)
            experts(dve, expert)
            acc(E, B - 1)

        def stage3_loads(sp):
            def matrices(e, buf):
                for w, n in ((m_wg, "eg"), (m_wu, "eu"), (m_wd, "ed")):
                    src = a[n][:, bass.ds(e, 1)].rearrange("p o k n -> p (o k) n")
                    sp.dma_start(w[:, buf], src).then_inc(e_wl[buf], 16)

            def weights(e, buf):
                sp.dma_start(m_cb[:, buf, :], a["comb"][bass.ds(e, 1), :].broadcast_to([P, TOK])).then_inc(e_cbl[buf], 16)

            matrices(0, 0)
            matrices(1, 1)
            sp.wait_ge(e_go, 1 + B)
            sp.dma_start(a["comb"], m_comb[:]).then_inc(e_comb, 16)
            sp.wait_ge(e_comb, 16)
            weights(0, 0)
            weights(1, 1)
            def refill(e, buf):
                at(sp, e_dn, e - 1, 0)
                matrices(e, buf)
                at(sp, e_act, e - 1, 0)
                weights(e, buf)

            with sp.Fori(0, E // 2 - 1) as i:
                refill(i * 2 + 2, 0)
                refill(i * 2 + 3, 1)
            refill(E, 0)

        END3 = UE * NE

        NG_OUT = 2
        NGB = Gen("ng", NG_OUT + KC)
        n_norm = Norm("n_", NGB, n_h, n_xc, n_sq, n_r)
        n_go = sem("n_go")
        n_kvf, n_kva = Count("n_kvf", NT), Count("n_kva", NT)
        n_ch = Count("n_ch", 5 * NT + 3)
        n_agg, n_var, n_qh = Count("n_agg", NT), Count("n_var", 1), Count("n_qh", NT)
        n_rt = Count("n_root", 1)
        n_qf, n_qa, n_mx = Count("n_qf", NT), Count("n_qa", NT), Count("n_mx", NT)
        n_sub, n_ex, n_sum, n_rc, n_nm = (Count("n_" + x, NT) for x in ("sub", "exp", "sum", "rec", "nrm"))
        n_fin = Count("n_fin", NT * (2 + 2 * B))

        def stage4_pe(pe):
            with pe.Fori(0, B) as b:
                pe.wait_ge(n_go, b * KC + 1)
                n_norm.on_pe(pe, b)
                n_norm.ready(pe, b)
                pe.wait_ge(loads["w1"], 32)
                for i in range(NT):
                    if i >= 2:
                        n_kva.wait(pe, b, i - 1)
                    for k in range(KC):
                        mm = pe.matmul(ps[:, 4 + i % 2, 0:KV1], n_h[:, k, i * P:(i + 1) * P], wkv1[:, k, :],
                                       start=(k == 0), stop=(k == KC - 1))
                    n_kvf.inc(mm)
                for i in range(NT):
                    if i >= 2:
                        n_qa.wait(pe, b, i - 1)
                    for m in range(2):
                        for k in range(KC):
                            mm = pe.matmul(ps[:, 2 * (i % 2) + m, :], n_h[:, k, i * P:(i + 1) * P],
                                           wq1[:, k, m * S:(m + 1) * S], start=(k == 0), stop=(k == KC - 1))
                    n_qf.inc(mm)
                for k in range(KC):
                    NGB.claim(pe, b, NG_OUT + k)
                for i in range(NT):
                    n_fin.wait(pe, b, (i + 1) * (2 + 2 * B))
                    for k in range(KC):
                        mm = pe.transpose(NGB.bank(NG_OUT + k)[:, i * P:(i + 1) * P], n_y[:, i, k * P:(k + 1) * P], ident)
                        if i == NT - 1:
                            NGB.filled(mm, NG_OUT + k)

        def stage4_act(act):
            with act.Fori(0, B) as b:
                n_norm.on_act(act, b)
                n_var.wait(act, b, 1)
                n_rt.inc(act.activation(n_mv[:, 1], n_mv[:, 0], ACT.Sqrt, bias=eps[:, 0:1]))
                for i in range(NT):
                    n_sub.wait(act, b, i + 1)
                    n_ex.inc(act.activation(n_q[:, i % 3, :], n_q[:, i % 3, :], ACT.Exp))

        def heads_of(v):
            return v.rearrange("p (h c) -> p h c", h=H1)

        def stage4_pool(pool):
            with pool.Fori(0, B) as b:
                def normalise(i):
                    n_rc.wait(pool, b, i + 1)
                    q = heads_of(n_q[:, i % 3, :])
                    n_nm.inc(pool.tensor_tensor(q, q, n_sm[:, 2, i, :].unsqueeze(2).broadcast_to([P, H1, K1]), ALU.mult))
                for i in range(NT):
                    n_mx.wait(pool, b, i + 1)
                    q = heads_of(n_q[:, i % 3, :])
                    n_sub.inc(pool.tensor_tensor(q, q, n_sm[:, 0, i, :].unsqueeze(2).broadcast_to([P, H1, K1]), ALU.subtract))
                    if i:
                        normalise(i - 1)
                normalise(NT - 1)

        def stage4_dve(dve, before, count):
            dve.wait_ge(before, count)
            dve.memset(n_hist[:], 0.0).then_inc(n_go, 1)
            with dve.Fori(0, B) as b:
                ch = lambda ins: n_ch.link(dve, b, ins)
                dve.wait_ge(n_go, b * KC + 1)
                n_norm.on_dve(dve, b)
                for i in range(NT):
                    n_kvf.wait(dve, b, i + 1)
                    n_kva.link(dve, b, dve.tensor_tensor(n_kv[:, i, :], ps[:, 4 + i % 2, 0:KV1], row("bkv"), ALU.add))
                    for m, sl in ((0, slice(0, K1)), (1, slice(K1, KV1))):
                        n_ch.inc(dve.bn_stats(n_bs[:, i, m, :], n_kv[:, i, sl]))
                n_ch.wait(dve, b, 2 * NT)
                settle(dve)
                for i in range(NT):
                    for m in range(2):
                        ins = dve.bn_aggr(n_ba[:, i, m, :], n_bs[:, i, m, :])
                        if m:
                            n_ch.inc(ins)
                        else:
                            n_agg.inc(ins)
                n_agg.wait(dve, b, NT)
                n_ch.wait(dve, b, 3 * NT)
                n_var.inc(dve.tensor_copy(n_mv[:, 0], n_ba[:, :, :, 1]))

                def queries(i):
                    n_qf.wait(dve, b, i + 1)
                    if i >= 3:
                        n_fin.wait(dve, b, (i - 3) * (2 + 2 * B) + 1)
                    for m in range(2):
                        sl = slice(m * S, (m + 1) * S)
                        ins = dve.tensor_tensor(n_q[:, i % 3, sl], ps[:, 2 * (i % 2) + m, :], row("bq")[:, sl], ALU.add)
                        (n_qa if m else n_qh).inc(ins)
                    n_qh.wait(dve, b, i + 1)
                    n_qa.wait(dve, b, i + 1)
                    n_mx.inc(dve.tensor_reduce(n_sm[:, 0, i, :], heads_of(n_q[:, i % 3, :]), AX.X, ALU.max))

                def sums(i):
                    n_ex.wait(dve, b, i + 1)
                    n_sum.link(dve, b, dve.tensor_reduce(n_sm[:, 1, i, :], heads_of(n_q[:, i % 3, :]), AX.X, ALU.add))
                    n_rc.inc(dve.reciprocal(n_sm[:, 2, i, :], n_sm[:, 1, i, :]))

                def result(i):
                    fin = lambda ins: n_fin.link(dve, b, ins)
                    n_nm.wait(dve, b, i + 1)
                    fin(dve.tensor_reduce(n_qn[:, 0, :], n_q[:, i % 3, :].rearrange("p (h c) -> p c h", h=H1), AX.X, ALU.add))
                    fin(dve.tensor_scalar(n_qn[:, 1, :], n_qn[:, 0, :], const("scal")[:, bass.ds(b, 1)], None, ALU.mult))
                    for s in range(B):
                        n_fin.inc(dve.scalar_tensor_tensor(n_jk[:, s, :], n_qn[:, 1, :], 1.0, n_hist[:, i, s, 0:K1], ALU.mult, ALU.mult,
                                                           accum_out=n_d[:, s:s + 1]))
                    n_fin.wait(dve, b, n_fin.n)
                    v = lambda s: n_hist[:, i, s, K1:KV1]
                    fin(dve.tensor_scalar(n_y[:, i, :], v(0), n_d[:, 0:1], None, ALU.mult))
                    for s in range(1, B):
                        fin(dve.scalar_tensor_tensor(n_y[:, i, :], v(s), n_d[:, s:s + 1], n_y[:, i, :], ALU.mult, ALU.add))

                queries(0)
                n_rt.wait(dve, b, 1)
                ch(dve.reciprocal(n_mv[:, 1], n_mv[:, 1]))
                for i in range(NT):
                    for m, sl in ((0, slice(0, K1)), (1, slice(K1, KV1))):
                        n_ch.inc(dve.tensor_scalar(n_kv[:, i, sl], n_kv[:, i, sl], n_ba[:, i, m, 0:1], n_mv[:, 1, i, m:m + 1],
                                                   ALU.subtract, ALU.mult))
                queries(1)
                n_ch.wait(dve, b, n_ch.n)
                ch(dve.tensor_tensor(n_kv[:], n_kv[:], row("gkv").unsqueeze(1).broadcast_to([P, NT, KV1]), ALU.mult))
                ch(dve.tensor_tensor(n_hist[:, :, bass.ds(b, 1), :].rearrange("p i o c -> p i (o c)"), n_kv[:],
                                     row("betakv").unsqueeze(1).broadcast_to([P, NT, KV1]), ALU.add))
                sums(0)
                for i in range(2, NT + 2):
                    if i < NT:
                        queries(i)
                    if i - 1 < NT:
                        sums(i - 1)
                    result(i - 2)
                for k in range(KC):
                    NGB.wait(dve, b, NG_OUT + k)
                    xk = xT[:, k, chunk(b)]
                    dve.tensor_tensor(xk, xk, NGB.bank(NG_OUT + k), ALU.add).then_inc(n_go, 1)
                dve.wait_ge(n_go, b * KC + 1 + KC)
                for k in range(KC):
                    dve.sem_inc(NGB.free[(NG_OUT + k) % 2], 1)

        FG_SC, FG_OH, FG_OUT = 2, 3, 4
        FG = Gen("fg", 6)
        f_norm = Norm("f_", FG, f_h, f_xc, f_sq, f_r)
        f_go = sem("f_go")
        f_sgn = sem("f_sign")
        f_ch = Count("f_ch", 5)
        f_ohr = Count("f_ohr", 2)
        f_bc, f_hm = Count("f_bc", T1), Count("f_hm", T1)
        f_use = Count("f_use", T1 - 1)

        def stage6_pe(pe):
            pe.wait_ge(f_sgn, 1)
            pe.wait_ge(loads["wt1"], 32)
            with pe.Fori(0, B) as b:
                pe.wait_ge(f_go, b * KC + 1)
                f_norm.on_pe(pe, b)
                f_norm.ready(pe, b)
                FG.claim(pe, b, FG_SC)
                for i in range(NT):
                    for k in range(KC):
                        mm = pe.matmul(FG.bank(FG_SC)[:, i * T1:(i + 1) * T1], f_h[:, k, i * P:(i + 1) * P],
                                       f_sg[:, k * T1:(k + 1) * T1], start=(k == 0), stop=(k == KC - 1))
                FG.filled(mm, FG_SC)
                f_ch.wait(pe, b, 5)
                FG.claim(pe, b, FG_OH)
                for i in range(NT):
                    mm = pe.transpose(FG.bank(FG_OH)[0:T1, i * P:(i + 1) * P], f_c[:, i, :], ident)
                FG.filled(mm, FG_OH)
                f_ohr.wait(pe, b, 2)
                for k in range(KC):
                    FG.claim(pe, b, FG_OUT + k)
                    pe.matmul(FG.bank(FG_OUT + k), bt1[:, k * P:(k + 1) * P], f_oh[:], start=True, stop=False, skip_group_check=True)

                def spread(t):
                    if t >= 4:
                        f_hm.wait(pe, b, t - 3)
                    f_bc.inc(pe.matmul(ps[:, t % 4, :], f_one[:, t * P:(t + 1) * P], f_ohb[:], start=True, stop=True))

                spread(0)
                spread(1)
                for t in range(T1):
                    if t + 2 < T1:
                        spread(t + 2)
                    f_hm.wait(pe, b, t + 1)
                    for k in range(KC):
                        for c in range(KC):
                            mm = pe.matmul(FG.bank(FG_OUT + k), wt1[:, t, c, k * P:(k + 1) * P], f_m[:, t % 4, c, :], start=False,
                                           stop=(t == T1 - 1 and c == KC - 1), skip_group_check=True)
                        if t == T1 - 1:
                            FG.filled(mm, FG_OUT + k)
                    if t < T1 - 1:
                        f_use.inc(mm)

        def stage6_act(act):
            act.wait_ge(f_go, 1)
            act.activation(f_sg[:], col("sigs"), ACT.Sign).then_inc(f_sgn, 1)
            with act.Fori(0, B) as b:
                f_norm.on_act(act, b)
                FG.wait(act, b, FG_OH)
                f_ohr.inc(act.copy(f_oh[:], FG.bank(FG_OH)[0:T1, :]))
                f_ohr.inc(act.copy(f_ohb[:], FG.bank(FG_OH)[0:T1, :]))
                i_free(act, FG, b, FG_OH, f_ohr, 2)

        def stage6_dve(dve, before, count):
            dve.wait_ge(before, count)
            dve.tensor_copy(f_one[:], const("onehot")[0:T1, :]).then_inc(f_go, 1)
            with dve.Fori(0, B) as b:
                ch = lambda ins: f_ch.link(dve, b, ins)
                dve.wait_ge(f_go, b * KC + 1)
                f_norm.on_dve(dve, b)
                FG.wait(dve, b, FG_SC)
                s = FG.bank(FG_SC)[:, 0:NT * T1].rearrange("p (i t) -> p i t", t=T1)
                wide = lambda v: v.unsqueeze(2).broadcast_to([P, NT, T1])
                ch(dve.tensor_reduce(f_mx[:, 0, :], s, AX.X, ALU.max))
                ch(dve.tensor_tensor(f_c[:], s, wide(f_mx[:, 0, :]), ALU.is_equal))
                dve.sem_inc(FG.free[FG_SC % 2], 1)
                ch(dve.tensor_tensor(f_c[:], f_c[:], const("first").unsqueeze(1).broadcast_to([P, NT, T1]), ALU.mult))
                ch(dve.tensor_reduce(f_mx[:, 1, :], f_c[:], AX.X, ALU.max))
                ch(dve.tensor_tensor(f_c[:], f_c[:], wide(f_mx[:, 1, :]), ALU.is_equal))
                for t in range(T1):
                    f_bc.wait(dve, b, t + 1)
                    if t >= 4:
                        f_use.wait(dve, b, t - 3)
                    f_hm.inc(dve.tensor_tensor(f_m[:, t % 4], f_h[:], ps[:, t % 4, :].unsqueeze(1).broadcast_to([P, KC, S]), ALU.mult))
                for k in range(KC):
                    FG.wait(dve, b, FG_OUT + k)
                    xk = xT[:, k, chunk(b)]
                    dve.tensor_tensor(xk, xk, FG.bank(FG_OUT + k), ALU.add).then_inc(f_go, 1)
                dve.wait_ge(f_go, b * KC + 1 + KC)
                for k in range(KC):
                    dve.sem_inc(FG.free[(FG_OUT + k) % 2], 1)

        cross0, cross1 = cross(0), cross(1)
        END1 = 1 + A_GO * B
        ENDX = 1 + KC * B

        def context(sp, stage):
            cld, cused = stage[5], stage[6]
            c = a["ctx"]
            sp.dma_start(x_c[:], c[:, :, 0:S]).then_inc(cld, 16)
            with sp.Fori(1, B) as b:
                cused.wait(sp, b - 1, GX)
                sp.dma_start(x_c[:], c[:, :, chunk(b)]).then_inc(cld, 16)

        chain = [(1, a_go, END1), (2, cross0[4], ENDX), (3, e_acc, END3), (4, n_go, ENDX), (5, cross1[4], ENDX), (6, f_go, ENDX)]

        def before(k):
            return chain[k - 2][1:]

        loaded = {"x": 1, "small": 3, "aw": 4, "xw0": 4, "xw1": 4, "w1": 2, "wt1": 2}

        @blk.sync
        def _(sp):
            sp.dma_start(xT[:], a["x"]).then_inc(loads["x"], 16)
            sp.dma_start(cols[:], a["cols"]).then_inc(loads["small"], 16)
            sp.dma_start(cst[:], a["consts"]).then_inc(loads["small"], 16)
            sp.dma_start(rows[:], a["rows"].broadcast_to([P, NROWS])).then_inc(loads["small"], 16)
            for n, w in zip("qkvo", aw):
                sp.dma_start(w[:], a[f"w0{n}"]).then_inc(loads["aw"], 16)
            for l in range(2):
                for n, w in zip("qkvo", xw[l]):
                    sp.dma_start(w[:], a[f"wx{l}{n}"]).then_inc(loads[f"xw{l}"], 16)
            sp.dma_start(wq1[:], a["w1q"]).then_inc(loads["w1"], 16)
            sp.dma_start(wkv1[:], a["w1kv"]).then_inc(loads["w1"], 16)
            sp.dma_start(wt1[:], a["wt1"]).then_inc(loads["wt1"], 16)
            sp.dma_start(bt1[:], a["bt1"]).then_inc(loads["wt1"], 16)
            sp.wait_ge(*before(2))
            context(sp, cross0)
            sp.wait_ge(*before(3))
            stage3_loads(sp)
            sp.wait_ge(*before(5))
            context(sp, cross1)
            sp.wait_ge(*chain[-1][1:])
            for name, n in loaded.items():
                sp.wait_ge(loads[name], 16 * n)
            sp.dma_start(a["out"], xT[:]).then_inc(stored, 16)
            sp.wait_ge(stored, 16)

        @blk.gpsimd
        def _(pool):
            pool.memset(meanw[:], 1.0 / D).then_inc(init_pool, 1)
            pool.memset(a_kz[:], 0.0).then_inc(init_pool, 1)
            pool.memset(a_vg[:], 0.0).then_inc(init_pool, 1)
            stage1_pool(pool)
            cross0[2](pool)
            stage3_pool(pool)
            stage4_pool(pool)
            cross1[2](pool)

        @blk.scalar
        def _(act):
            stage1_act(act)
            cross0[1](act)
            stage3_act(act)
            stage4_act(act)
            cross1[1](act)
            stage6_act(act)

        @blk.vector
        def _(dve):
            dve.memset(eps[:, 0:1], EPS_LN).then_inc(init_dve, 1)
            dve.memset(eps[:, 1:2], EPS_RMS).then_inc(init_dve, 1)
            stage1_dve(dve)
            cross0[3](dve, *before(2))
            stage3_dve(dve, *before(3))
            stage4_dve(dve, *before(4))
            cross1[3](dve, *before(5))
            stage6_dve(dve, *before(6))

        @blk.tensor
        def _(pe):
            stage1_pe(pe)
            cross0[0](pe)
            stage3_pe(pe)
            stage4_pe(pe)
            cross1[0](pe)
            stage6_pe(pe)


def kernel(**inputs):
    import concourse.bacc as bacc
    from concourse.bass_utils import run_bass_kernel_spmd

    i = {k: np.asarray(v) for k, v in inputs.items()}

    def halves(w):
        return np.ascontiguousarray(w.reshape(KC, P, -1).transpose(1, 0, 2))

    def tokens(x):
        return halves(np.ascontiguousarray(x.transpose(2, 0, 1)).reshape(D, TOK))

    arrays = {
        "x": tokens(i["x"]),
        "w0q": halves(i["L0_attn_w_q"]), "w0k": halves(i["L0_attn_w_k"]), "w0v": halves(i["L0_attn_w_v"]),
        "w0o": np.ascontiguousarray(i["L0_attn_w_out"].reshape(PAIRS, P, D).transpose(1, 0, 2)),
        "consts": constants(),
        "ctx": tokens(i["ctx_1024"]),
    }
    vec = {"norm_w": "L0_attn_norm_w", "scorer_w": "L0_attn_scorer_w", "bq0": "L0_xattn_bq", "bk0": "L0_xattn_bk",
           "bo0": "L0_xattn_bo", "bq1": "L1_xattn_bq", "bk1": "L1_xattn_bk", "bo1": "L1_xattn_bo"}
    parts = [halves(i[n].reshape(D, 1)).reshape(P, KC) for n in vec.values()]
    parts += [halves(i["L1_ffn_tile_sigs"].T).reshape(P, -1), halves(i["L0_ffn_gate_w"].T).reshape(P, -1)]
    arrays["cols"] = np.concatenate(parts, axis=1)
    arrays["rows"] = np.concatenate([i[n].reshape(-1) for n in (
        "L0_xattn_bv", "L0_attn_scorer_b", "L0_ffn_expert_bias", "L1_attn_bq", "L1_attn_bk", "L1_attn_bv",
        "L1_attn_k_gamma", "L1_attn_v_gamma", "L1_attn_k_beta", "L1_attn_v_beta", "L1_xattn_bv")])[None]
    for n in "qkvo":
        arrays[f"wx0{n}"] = halves(i[f"L0_xattn_W{n}"].T)
        arrays[f"wx1{n}"] = halves(i[f"L1_xattn_W{n}"])
    arrays["w1q"] = halves(i["L1_attn_Wq"].T)
    arrays["w1kv"] = halves(np.concatenate([i["L1_attn_Wk"], i["L1_attn_Wv"]]).T)
    arrays["wt1"] = np.ascontiguousarray(i["L1_ffn_W"].reshape(T1, KC, P, D).transpose(2, 0, 1, 3))
    arrays["bt1"] = i["L1_ffn_b"]
    for n, routed in (("gate", "L0_ffn_w_gate"), ("up", "L0_ffn_w_up"), ("down", "L0_ffn_w_down")):
        w = np.concatenate([i[routed], i[f"L0_ffn_shared_{n}_w"][None]]).transpose(0, 2, 1)
        arrays["e" + n[0]] = np.ascontiguousarray(w.reshape(E + 1, KC, P, -1).transpose(2, 0, 1, 3))
    nc = bacc.Bacc("TRN2", target_bir_lowering=False, num_devices=1)
    args = {n: nc.dram_tensor(f"in_{n}", v.shape, F32, kind="ExternalInput").ap() for n, v in arrays.items()}
    args["comb"] = nc.dram_tensor("combine", (E + 1, TOK), F32, kind="Internal").ap()
    args["out"] = nc.dram_tensor("out_x", (P, KC, TOK), F32, kind="ExternalOutput").ap()
    program(nc, args)
    r = run_bass_kernel_spmd(nc, [{f"in_{n}": v for n, v in arrays.items()}], core_ids=[0])
    y = r.results[0]["out_x"]
    return np.ascontiguousarray(y.transpose(1, 0, 2).reshape(D, B, S).transpose(1, 2, 0))
```

```python
from contextlib import ExitStack

import numpy as np

import concourse.bass as bass
from concourse import mybir

P = 128
B, S, D = 4, 512, 256
KC = D // P
TOK = B * S
NT = S // P

H0, HD0, WIN, G0 = 16, 64, 256, 64
PAIRS = H0 // 2
INNER = H0 * HD0
NWIN = S // WIN
LG = G0 + WIN

HX, HDX = 16, 16
GX = 2
HPG = P // HDX
E, TOPK, I = 16, 8, 256
ROUTE_SCALE = 2.826
H1, K1 = 16, 64
KV1 = K1 + D
T1 = 8
NEG = -1.0e30
BIG = 3.0e38
EPS_LN, EPS_RMS = 1e-5, 1e-6
NEWTON = 24

F32 = mybir.dt.float32
BF16 = mybir.dt.bfloat16
ALU = mybir.AluOpType
ACT = mybir.ActivationFunctionType
AX = mybir.AxisListType

def offsets(parts):
    at, n = {}, 0
    for name, width in parts:
        at[name] = (n, n + width)
        n += width
    return at, n

COLS, NCOLS = offsets([("norm_w", KC), ("scorer_w", KC), ("bq0", KC), ("bk0", KC), ("bo0", KC),
                       ("bq1", KC), ("bk1", KC), ("bo1", KC), ("sigs", KC * T1), ("gate_w", KC * E)])
ROWS, NROWS = offsets([("bv0", D), ("scorer_b", 1), ("expert_bias", E), ("bq", INNER), ("bkv", KV1),
                       ("gkv", KV1), ("betakv", KV1), ("bv1", D)])
CONSTS, NCONSTS = offsets([("ident", P), ("tri", S), ("earlier", 896), ("slots", P), ("pos", NT), ("heads", HPG),
                           ("before", E * E), ("first", T1), ("scal", B)])


def constants():
    c = np.zeros((P, NCONSTS), np.float32)
    p = np.arange(P)[:, None]

    def put(name, v):
        a, b = CONSTS[name]
        c[:, a:b] = v

    put("ident", np.eye(P))
    put("tri", np.where(np.arange(S)[None] - (S - P) <= p, 0.0, NEG))
    put("earlier", (np.arange(896)[None] - (S - P) < p))
    put("slots", np.arange(P)[None] % G0)
    put("pos", np.arange(NT)[None] * P + p)
    put("heads", p // HDX == np.arange(HPG)[None])
    e, f = np.arange(E)[:, None], np.arange(E)[None]
    put("before", (f < e).reshape(1, -1))
    put("first", T1 - np.arange(T1)[None])
    put("scal", 1.0 / (np.sqrt(np.arange(1, B + 1))[None] * H1))
    return c


def program(nc, a):
    with ExitStack() as ctx:
        def sb(name, shape, dt=F32, c=ctx):
            return c.enter_context(nc.sbuf_tensor(name, shape, dt))

        sems, raised = {}, {}

        def sem(name):
            if name not in sems:
                sems[name] = ctx.enter_context(nc.semaphore(name))
            return sems[name]

        def shared(name, total):
            base = raised.get(name, 0)
            raised[name] = base + total
            return sem(name), base

        xT = sb("xT", [P, KC, TOK])
        rows = sb("rows", [P, NROWS])
        cols = sb("cols", [P, NCOLS])
        cst = sb("cst", [P, NCONSTS])
        meanw = sb("meanw", [P, P])
        eps = sb("eps", [P, 2])
        xw = [[sb(f"xw{l}_{n}", [P, KC, D]) for n in "qkvo"] for l in range(2)]
        wq1 = sb("wq1", [P, KC, INNER])
        wkv1 = sb("wkv1", [P, KC, KV1])
        wt1 = sb("wt1", [P, T1, KC, D])
        bt1 = sb("bt1", [T1, D])

        def col(name):
            lo, hi = COLS[name]
            return cols[:, lo:hi]

        def row(name):
            lo, hi = ROWS[name]
            return rows[:, lo:hi]

        def const(name):
            lo, hi = CONSTS[name]
            return cst[:, lo:hi]

        ident = const("ident")
        ps = ctx.enter_context(nc.psum_tensor("ps", [P, 8, 512], F32))
        S_BANKS, PT_BANK, O_BANK, G_BANK = 3, 3, 5, 6

        with ExitStack() as st:
            aw = [sb(f"aw_{n}", [P, KC, INNER], c=st) for n in "qkv"] + [sb("aw_o", [P, PAIRS, D], c=st)]
            a_h = sb("a_h", [P, KC, S], c=st)
            a_xc = sb("a_xc", [P, KC, S], c=st)
            a_sq = sb("a_sq", [P, KC, S], c=st)
            a_r = sb("a_r", [P, 2, S], c=st)
            a_q = sb("a_q", [P, 2, S], c=st)
            a_kz = sb("a_kz", [P, 2, 2, NWIN, LG], c=st)
            a_v = sb("a_v", [P, 2, NT, P], c=st)
            a_vg = sb("a_vg", [P, 2, P], c=st)
            a_scw = sb("a_scw", [P, KC, P], c=st)
            a_tokid = sb("a_tokid", [P, NT, P], c=st)
            a_sc = sb("a_sc", [P, S], c=st)
            a_junk = sb("a_junk", [P, S], c=st)
            a_col = sb("a_col", [P, 4, NT], c=st)
            a_sel = sb("a_sel", [P, NT, P], c=st)
            a_hg = sb("a_hg", [P, KC, P], c=st)
            a_mask = sb("a_mask", [P, NT, 2, LG], c=st)
            a_s = sb("a_s", [P, 3, LG], c=st)
            a_p = sb("a_p", [P, 3, 2 * LG], c=st)
            a_mn = sb("a_mn", [P, 64], c=st)
            a_den = sb("a_den", [P, 64], c=st)
            a_rd = sb("a_rd", [P, 64], c=st)
            a_pt = sb("a_pt", [P, 2, 5, WIN], c=st)
            a_o = sb("a_o", [P, PAIRS, S], c=st)

        with ExitStack() as st:
            x_h = sb("x_h", [P, KC, S], c=st)
            x_xc = sb("x_xc", [P, KC, S], c=st)
            x_sq = sb("x_sq", [P, KC, S], c=st)
            x_o = x_sq
            x_r = sb("x_r", [P, 2, S], c=st)
            x_c = sb("x_c", [P, KC, S], c=st)
            x_q = sb("x_q", [P, GX, S], c=st)
            x_k = sb("x_k", [P, GX, S], c=st)
            x_kz = sb("x_kz", [P, HPG // 2, S], c=st)
            x_vz = sb("x_vz", [P, NT, HPG * (P + HDX)], c=st)
            x_pt = sb("x_pt", [P, 2, NT, S], c=st)
            x_ring = sb("x_ring", [P, 7, NT, S], c=st)
            x_s = x_ring[:, 0:4].rearrange("p (a b) t s -> p a b t s", a=2)
            x_ja, x_jd = x_ring[:, 4], x_ring[:, 5]
            x_gm = x_h[:].rearrange("p k (a w) -> p (k a) w", w=S // 2)
            x_gd = sb("x_gd", [P, 2, NT, 64], c=st)
            x_flagi = sb("x_flagi", [1, 1], mybir.dt.int32, c=st)
            x_st = sb("x_st", [P, 8, 64], c=st)
            x_sf = x_st[:, 4, 0:4 * NT].rearrange("p (a b i) -> p a b i", a=2, b=2)
            x_bad, x_flag = x_st[:, 5, 0:2], x_st[0:1, 5, 2:4]
        with ExitStack() as st:
            m_hc, m_xc, m_sq, m_r = (sb("m_" + n, [P, KC, S], c=st) for n in ("hc", "xc", "sq", "r"))
            m_h = sb("m_h", [P, KC, TOK], c=st)
            m_w17 = sb("m_w17", [P, NT, E + 1], c=st)
            m_comb = sb("m_comb", [E + 1, TOK], c=st)
            m_sg, m_sel = (sb("m_" + n, [P, NT, E], c=st) for n in ("sg", "sel"))
            m_sum = sb("m_sum", [P, NT], c=st)
            m_gt, m_eq = (sb("m_" + n, [P, NT, E, E], c=st) for n in ("gt", "eq"))
            m_wg, m_wu, m_wd = (sb("m_" + n, [P, 2, KC, D], c=st) for n in ("wg", "wu", "wd"))
            m_cb = sb("m_cb", [P, 2, TOK], c=st)
            m_g, m_m = (sb("m_" + n, [P, 2, S], c=st) for n in ("g", "m"))
            m_a = sb("m_a", [P, 2, KC, S], c=st)
        with ExitStack() as st:
            n_h, n_xc, n_sq, n_r = (sb("n_" + n, [P, KC, S], c=st) for n in ("h", "xc", "sq", "r"))
            n_hist = sb("n_hist", [P, NT, B, KV1], c=st)
            n_kv = sb("n_kv", [P, NT, KV1], c=st)
            n_bs, n_ba = sb("n_bs", [P, NT, 2, 6], c=st), sb("n_ba", [P, NT, 2, 2], c=st)
            n_mv = sb("n_mv", [P, 2, NT, 2], c=st)
            n_q = sb("n_q", [P, 3, INNER], c=st)
            n_sm = sb("n_sm", [P, 3, NT, H1], c=st)
            n_qn = sb("n_qn", [P, 2, K1], c=st)
            n_jk, n_d = sb("n_jk", [P, B, K1], c=st), sb("n_d", [P, B], c=st)
            n_y = sb("n_y", [P, NT, D], c=st)
        with ExitStack() as st:
            f_h, f_xc, f_sq, f_r = (sb("f_" + n, [P, KC, S], c=st) for n in ("h", "xc", "sq", "r"))
            f_sg = sb("f_sg", [P, KC * T1], c=st)
            f_one = sb("f_one", [T1, T1 * P], BF16, c=st)
            f_oh, f_ohb = sb("f_oh", [T1, S], c=st), sb("f_ohb", [T1, S], BF16, c=st)
            f_c, f_mx = sb("f_c", [P, NT, T1], c=st), sb("f_mx", [P, 2, NT], c=st)
            f_m = sb("f_m", [P, 4, KC, S], c=st)

        loads = {n: sem(f"load_{n}") for n in ("x", "small", "aw", "xw0", "xw1", "w1", "wt1")}
        init_pool = sem("init_pool")
        init_dve = sem("init_dve")
        stored = sem("stored")

        class Gen:
            def __init__(self, tag, per):
                self.full = [sem(f"{tag}_full{k}") for k in range(2)]
                self.free = [sem(f"{tag}_free{k}") for k in range(2)]
                self.half = per // 2
                self.base = shared(f"{tag}_full0", B * self.half)[1]
                assert per % 2 == 0

            def bank(self, n):
                return ps[:, G_BANK + n % 2, :]

            def claim(self, pe, b, n):
                if n >= 2:
                    pe.wait_ge(self.free[n % 2], b * self.half + self.base + n // 2)

            def filled(self, ins, n):
                ins.then_inc(self.full[n % 2], 1)

            def wait(self, eng, b, n):
                eng.wait_ge(self.full[n % 2], b * self.half + self.base + n // 2 + 1)

            def read(self, ins, n):
                ins.then_inc(self.free[n % 2], 1)

        class Count:
            def __init__(self, name, per):
                self.per, self.n = per, 0
                self.sem, self.base = shared(name, B * per)

            def inc(self, ins):
                ins.then_inc(self.sem, 1)
                self.n += 1
                return self.n

            def wait(self, eng, b, n):
                eng.wait_ge(self.sem, b * self.per + self.base + n)

            def link(self, eng, b, ins):
                self.inc(ins)
                self.wait(eng, b, self.n)

            def close(self):
                assert self.n == self.per, (self.sem, self.n, self.per)

        blk = ctx.enter_context(nc.Block())

        carried = {}

        def settle(eng):
            if eng.engine not in carried:
                carried[eng.engine] = sem(f"carried{len(carried)}")
            eng.sem_inc(carried[eng.engine], 1)

        def chunk(b):
            return bass.ds(b * S, S)

        NU = PAIRS * NWIN * 2 * 2
        GA_MEAN, GA_VAR, GA_RMS, GA_TOK, GA_SC, GA_HG, GA_IDX, GA_PAIR = 0, 1, 2, 3, 5, 6, 7, 8
        GA_OUT = GA_PAIR + 4 * PAIRS
        GA = Gen("ga", GA_OUT + 2)
        a_go = sem("a_go")
        A_GO = 2
        a_ln = Count("a_ln", 6)
        a_lnact = Count("a_lnact", 4)
        a_xn = Count("a_xn", 1)
        a_tok = Count("a_tok", 2)
        a_dv = Count("a_dv", 26)
        a_selr = Count("a_selr", 1)
        a_hgr = Count("a_hgr", 1)
        a_qr = Count("a_qr", PAIRS)
        a_vr = Count("a_vr", PAIRS)
        a_kr = Count("a_kr", 8 * PAIRS)
        a_sf = Count("a_sf", NU)
        a_ttr = Count("a_ttr", NU)
        a_exp = Count("a_exp", NU)
        a_rdn = Count("a_rdn", NU)
        a_scl = Count("a_scl", NU)
        a_t = Count("a_t", NU)
        a_pe = [Count("a_pteA", NU // 2), Count("a_pteD", NU // 2)]
        a_pv = Count("a_pv", PAIRS * NWIN)
        a_oev = Count("a_oev", PAIRS)

        def unit_a(n):
            p, r = divmod(n, 8)
            w, r = divmod(r, 4)
            j, h = divmod(r, 2)
            return p, w, j, h

        def a_span(j, h):
            w = G0 + P * (j + 1)
            return slice(0, w) if h else slice(LG - w, LG)

        def a_local(k, h):
            o = G0 + k * P if h else (1 - k) * P
            return slice(o, o + P)

        def a_global(h):
            return slice(0, G0) if h else slice(WIN, LG)

        def probs(n):
            h, sp = n % 2, a_span(n // 2 % 2, n % 2)
            return a_p[:, (n // 2) % 3, h * LG + sp.start:h * LG + sp.stop]

        LAG_E, LAG_T, LAG_PV = 1, 3, 4

        def stage1_pe(pe):
            wq, wk, wv, wo = aw
            pe.wait_ge(loads["x"], 16)
            pe.wait_ge(loads["small"], 48)
            pe.wait_ge(init_pool, 3)
            pe.wait_ge(init_dve, 16)
            with pe.Fori(0, B) as b:
                pe.wait_ge(a_go, b * A_GO + 1)

                def model_mean(n, src):
                    GA.claim(pe, b, n)
                    for k in range(KC):
                        mm = pe.matmul(GA.bank(n), meanw[:], src(k), start=(k == 0), stop=(k == KC - 1))
                    GA.filled(mm, n)

                model_mean(GA_MEAN, lambda k: xT[:, k, chunk(b)])
                a_lnact.wait(pe, b, 1)
                model_mean(GA_VAR, lambda k: a_sq[:, k, :])
                a_lnact.wait(pe, b, 3)
                model_mean(GA_RMS, lambda k: a_sq[:, k, :])
                a_ln.wait(pe, b, 6)
                for k in range(KC):
                    GA.claim(pe, b, GA_TOK + k)
                    for i in range(NT):
                        mm = pe.transpose(GA.bank(GA_TOK + k)[:, i * P:(i + 1) * P], a_h[:, k, i * P:(i + 1) * P], ident)
                    GA.filled(mm, GA_TOK + k)
                GA.claim(pe, b, GA_SC)
                for k in range(KC):
                    mm = pe.matmul(GA.bank(GA_SC), a_scw[:, k, :], a_h[:, k, :], start=(k == 0), stop=(k == KC - 1))
                GA.filled(mm, GA_SC)
                a_selr.wait(pe, b, 1)
                a_tok.wait(pe, b, 2)
                GA.claim(pe, b, GA_HG)
                for k in range(KC):
                    for i in range(NT):
                        mm = pe.matmul(GA.bank(GA_HG)[:, k * P:(k + 1) * P], htok(i, k), a_sel[:, i, :],
                                       start=(i == 0), stop=(i == NT - 1))
                GA.filled(mm, GA_HG)
                GA.claim(pe, b, GA_IDX)
                for i in range(NT):
                    mm = pe.matmul(GA.bank(GA_IDX)[:, 0:G0], a_tokid[:, i, :], a_sel[:, i, 0:G0],
                                   start=(i == 0), stop=(i == NT - 1))
                GA.filled(mm, GA_IDX)
                pe.wait_ge(loads["aw"], 64)
                a_hgr.wait(pe, b, 1)

                def project(p):
                    g = GA_PAIR + 4 * p
                    sl = slice(p * P, (p + 1) * P)
                    for m, w in ((0, wq), (1, wk)):
                        GA.claim(pe, b, g + m)
                        for k in range(KC):
                            mm = pe.matmul(GA.bank(g + m), w[:, k, sl], a_h[:, k, :], start=(k == 0), stop=(k == KC - 1))
                        GA.filled(mm, g + m)
                    GA.claim(pe, b, g + 2)
                    for i in range(NT):
                        for k in range(KC):
                            mm = pe.matmul(GA.bank(g + 2)[:, i * P:(i + 1) * P], a_h[:, k, i * P:(i + 1) * P], wv[:, k, sl],
                                           start=(k == 0), stop=(k == KC - 1))
                    GA.filled(mm, g + 2)
                    GA.claim(pe, b, g + 3)
                    for k in range(KC):
                        pe.matmul(GA.bank(g + 3)[:, 0:P], wk[:, k, sl], a_hg[:, k, :], start=(k == 0), stop=(k == KC - 1))
                    for k in range(KC):
                        mm = pe.matmul(GA.bank(g + 3)[:, P:2 * P], a_hg[:, k, :], wv[:, k, sl], start=(k == 0), stop=(k == KC - 1))
                    GA.filled(mm, g + 3)

                def scores(n):
                    p, w, j, h = unit_a(n)
                    if n % 8 == 0:
                        a_qr.wait(pe, b, p + 1)
                        a_kr.wait(pe, b, 8 * (p + 1))
                    if n >= S_BANKS:
                        a_ttr.wait(pe, b, n - S_BANKS + 1)
                    sp = a_span(j, h)
                    t = (w * 2 + j) * P
                    a_sf.inc(pe.matmul(ps[:, n % S_BANKS, sp], a_q[:, p % 2, t:t + P], a_kz[:, p % 2, h, w, sp],
                                       start=True, stop=True))

                def turn(n):
                    p, w, j, h = unit_a(n)
                    a_scl.wait(pe, b, n + 1)
                    if n >= 2:
                        a_pe[h].wait(pe, b, n // 2)
                    pb = a_p[:, (n // 2) % 3]
                    for k in range(j + 1):
                        lo = a_local(k, h)
                        mm = pe.transpose(ps[:, PT_BANK + h, k * P:(k + 1) * P], pb[:, h * LG + lo.start:h * LG + lo.stop],
                                          ident)
                    if h == 1:
                        mm = pe.transpose(ps[:, PT_BANK + 1, (j + 1) * P:(j + 2) * P], pb[:, WIN:WIN + 2 * G0], ident)
                    a_t.inc(mm)

                def values(wi):
                    p, w = divmod(wi, NWIN)
                    for q in a_pe:
                        q.wait(pe, b, 2 * (wi + 1))
                    if w == 0:
                        a_vr.wait(pe, b, p + 1)
                        if p >= 1:
                            a_oev.wait(pe, b, p)
                    pt = a_pt[:, wi % 2]
                    o = ps[:, O_BANK, w * WIN:(w + 1) * WIN]
                    pe.matmul(o, a_vg[:, p % 2, :], pt[:, 4, :], start=True, stop=False, skip_group_check=True)
                    for h in range(2):
                        for k in range(2):
                            v = a_v[:, p % 2, w * 2 + k, h * HD0:(h + 1) * HD0]
                            mm = pe.matmul(ps[h * HD0:(h + 1) * HD0, O_BANK, w * WIN + k * P:(w + 1) * WIN], v,
                                           pt[:, 2 * h + k, k * P:WIN], start=False, stop=(h == 1 and k == 1),
                                           skip_group_check=True)
                    a_pv.inc(mm)

                project(0)
                for n in range(NU + LAG_PV + 1):
                    if n < NU:
                        scores(n)
                        if n % 8 == 5 and n // 8 + 1 < PAIRS:
                            project(n // 8 + 1)
                    if 0 <= n - LAG_T < NU:
                        turn(n - LAG_T)
                    m = n - LAG_PV - 1
                    if m >= 0 and m % 4 == 3:
                        values(m // 4)
                a_oev.wait(pe, b, PAIRS)
                for k in range(KC):
                    GA.claim(pe, b, GA_OUT + k)
                    for p in range(PAIRS):
                        mm = pe.matmul(GA.bank(GA_OUT + k), wo[:, p, k * P:(k + 1) * P], a_o[:, p, :],
                                       start=(p == 0), stop=(p == PAIRS - 1))
                    GA.filled(mm, GA_OUT + k)

        def htok(i, k):
            return a_htok[:, i, k * P:(k + 1) * P]

        def stage1_act(act):
            act.wait_ge(init_dve, 16)
            with act.Fori(0, B) as b:
                a_ln.wait(act, b, 1)
                a_lnact.inc(act.activation(a_sq[:], a_xc[:], ACT.Square))
                GA.wait(act, b, GA_VAR)
                i = act.activation(a_r[:, 0, :], GA.bank(GA_VAR), ACT.Sqrt, bias=eps[:, 0:1])
                a_lnact.inc(i)
                i_free(act, GA, b, GA_VAR, a_lnact, 2)
                a_ln.wait(act, b, 3)
                a_lnact.inc(act.activation(a_sq[:], a_xc[:], ACT.Square))
                GA.wait(act, b, GA_RMS)
                a_lnact.inc(act.activation(a_r[:, 0, :], GA.bank(GA_RMS), ACT.Sqrt, bias=eps[:, 1:2]))
                i_free(act, GA, b, GA_RMS, a_lnact, 4)
                for k in range(KC):
                    GA.wait(act, b, GA_TOK + k)
                    i = act.copy(a_htok[:, :, k * P:(k + 1) * P], GA.bank(GA_TOK + k).rearrange("p (i c) -> p i c", i=NT))
                    a_tok.inc(i)
                    i_free(act, GA, b, GA_TOK + k, a_tok, k + 1)
                GA.wait(act, b, GA_HG)
                i = act.copy(a_hg[:].rearrange("p k c -> p (k c)"), GA.bank(GA_HG)[:, 0:KC * P])
                a_hgr.inc(i)
                i_free(act, GA, b, GA_HG, a_hgr, 1)

                def evac_qv(p):
                    g = GA_PAIR + 4 * p
                    GA.wait(act, b, g)
                    if p >= 2:
                        a_sf.wait(act, b, 8 * (p - 1))
                    a_qr.inc(act.copy(a_q[:, p % 2, :], GA.bank(g)))
                    i_free(act, GA, b, g, a_qr, p + 1)
                    GA.wait(act, b, g + 2)
                    if p >= 2:
                        a_pv.wait(act, b, NWIN * (p - 1))
                    a_vr.inc(act.copy(a_v[:, p % 2].rearrange("p i c -> p (i c)"), GA.bank(g + 2)))
                    i_free(act, GA, b, g + 2, a_vr, p + 1)

                def exps(n):
                    p, w, j, h = unit_a(n)
                    sp = a_span(j, h)
                    a_ttr.wait(act, b, n + 1)
                    if n >= 6:
                        a_t.wait(act, b, n - 4)
                    a_exp.inc(act.activation(probs(n), a_s[:, n % 3, sp], ACT.Exp, scale=-1.0,
                                             bias=a_mn[:, n:n + 1], accum_out=a_den[:, n:n + 1]))

                def evac_pt(n):
                    p, w, j, h = unit_a(n)
                    wi = n // 4
                    a_t.wait(act, b, n + 1)
                    if wi >= 2:
                        a_pv.wait(act, b, wi - 1)
                    a_pe[0].inc(act.copy(a_pt[:, wi % 2, 0:j + 1, j * P:(j + 1) * P],
                                         ps[:, PT_BANK, 0:(j + 1) * P].rearrange("p (k c) -> p k c", c=P)))

                evac_qv(0)
                for n in range(NU + LAG_T + 1):
                    if 0 <= n - LAG_E < NU:
                        exps(n - LAG_E)
                    if n < NU and n % 8 == 5 and n // 8 + 1 < PAIRS:
                        evac_qv(n // 8 + 1)
                    m = n - LAG_T
                    if 0 <= m < NU and m % 2 == 0:
                        evac_pt(m)

        def i_free(eng, G, b, g, count, n):
            count.wait(eng, b, n)
            eng.sem_inc(G.free[g % 2], 1)

        def stage1_pool(pool):
            with pool.Fori(0, B) as b:
                a_ln.wait(pool, b, 3)
                a_xn.inc(pool.tensor_tensor(xT[:, :, chunk(b)], xT[:, :, chunk(b)], a_xc[:], ALU.add))
                for n in range(NU):
                    p, w, j, h = unit_a(n)
                    a_rdn.wait(pool, b, n + 1)
                    settle(pool)
                    v = probs(n)
                    a_scl.inc(pool.tensor_scalar(v, v, a_rd[:, n:n + 1], 1.0, ALU.mult, ALU.mult))

        a_htok = a_o[:, 0:2, :].rearrange("p a (i c) -> p (a i) c", c=D)

        def stage1_dve(dve):
            tri = const("tri")
            dve.wait_ge(loads["small"], 48)
            for t in range(NT):
                for h in range(2):
                    for k in range(t % 2 + 1):
                        o = S - P * (t % 2 - k + 1)
                        dve.tensor_copy(a_mask[:, t, h, a_local(k, h)], tri[:, o:o + P]).then_inc(init_dve, 1)
            dve.tensor_copy(a_scw[:], col("scorer_w").unsqueeze(2).broadcast_to([P, KC, P])).then_inc(init_dve, 1)
            dve.tensor_copy(a_tokid[:], const("pos").unsqueeze(2).broadcast_to([P, NT, P])).then_inc(init_dve, 1)
            dve.wait_ge(init_dve, 16)
            dve.wait_ge(init_pool, 3)
            dve.wait_ge(loads["x"], 16)
            dve.memset(eps[0:1, 0:1], EPS_LN).then_inc(a_go, 1)
            with dve.Fori(0, B) as b:
                lk = lambda ins: a_ln.link(dve, b, ins)
                x = xT[:, :, chunk(b)]
                dve.wait_ge(a_go, b * A_GO + 1)
                GA.wait(dve, b, GA_MEAN)
                lk(dve.tensor_tensor(a_xc[:], x, GA.bank(GA_MEAN).unsqueeze(1).broadcast_to([P, KC, S]), ALU.subtract))
                dve.sem_inc(GA.free[GA_MEAN % 2], 1)
                a_lnact.wait(dve, b, 2)
                lk(dve.reciprocal(a_r[:, 1, :], a_r[:, 0, :]))
                lk(dve.tensor_tensor(a_xc[:], a_xc[:], a_r[:, 1, :].unsqueeze(1).broadcast_to([P, KC, S]), ALU.mult))
                a_lnact.wait(dve, b, 4)
                lk(dve.reciprocal(a_r[:, 1, :], a_r[:, 0, :]))
                for k in range(KC):
                    a_ln.inc(dve.scalar_tensor_tensor(a_h[:, k, :], a_xc[:, k, :], col("norm_w")[:, k:k + 1],
                                                      a_r[:, 1, :], ALU.mult, ALU.mult))
                ch = lambda ins: a_dv.link(dve, b, ins)
                GA.wait(dve, b, GA_SC)
                ch(dve.tensor_scalar(a_sc[:], GA.bank(GA_SC), row("scorer_b"), None, ALU.add))
                dve.sem_inc(GA.free[GA_SC % 2], 1)
                for i in range(NT):
                    ch(dve.tensor_tensor_reduce(a_junk[:, 0:P], a_sc[:, i * P:(i + 1) * P], ident, 1.0, 0.0,
                                                ALU.mult, ALU.add, a_col[:, 0, i:i + 1]))
                for i in range(NT):
                    ch(dve.tensor_scalar(a_junk[:], a_sc[:], a_col[:, 0, i:i + 1], None, ALU.is_gt, ALU.add,
                                         accum_out=a_col[:, 1, i:i + 1]))
                    o = S - P - i * P
                    ch(dve.scalar_tensor_tensor(a_junk[:], a_sc[:], a_col[:, 0, i:i + 1], const("earlier")[:, o:o + S],
                                                ALU.is_equal, ALU.mult, accum_out=a_col[:, 2, i:i + 1]))
                ch(dve.tensor_tensor(a_col[:, 3, :], a_col[:, 1, :], a_col[:, 2, :], ALU.add))
                for i in range(NT):
                    ch(dve.tensor_scalar(a_sel[:, i, :], const("slots"), a_col[:, 3, i:i + 1], None, ALU.is_equal))
                a_selr.inc(dve.tensor_copy(a_col[0:1, 0, 0:1], a_col[0:1, 0, 0:1]))
                GA.wait(dve, b, GA_IDX)
                for t in range(NT):
                    for h in range(2):
                        ch(dve.tensor_scalar(a_mask[:, t, h, a_global(h)], GA.bank(GA_IDX)[:, 0:G0],
                                             const("pos")[:, t:t + 1], NEG, ALU.is_gt, ALU.mult))
                dve.sem_inc(GA.free[GA_IDX % 2], 1)

                def evac_k(p):
                    g = GA_PAIR + 4 * p
                    GA.wait(dve, b, g + 1)
                    if p >= 2:
                        a_sf.wait(dve, b, 8 * (p - 1))
                    for h in range(2):
                        r = slice(h * HD0, (h + 1) * HD0)
                        kb = ps[r, G_BANK + (g + 1) % 2, :].rearrange("p (w k c) -> p w k c", w=NWIN, c=P)
                        for k in range(2):
                            a_kr.inc(dve.tensor_copy(a_kz[r, p % 2, h, :, a_local(k, h)], kb[:, :, k, :]))
                    a_kr.wait(dve, b, a_kr.n)
                    dve.sem_inc(GA.free[(g + 1) % 2], 1)
                    GA.wait(dve, b, g + 3)
                    if p >= 2:
                        a_pv.wait(dve, b, NWIN * (p - 1))
                    for h in range(2):
                        r = slice(h * HD0, (h + 1) * HD0)
                        gb = ps[r, G_BANK + (g + 3) % 2, :]
                        a_kr.inc(dve.tensor_copy(a_kz[r, p % 2, h, :, a_global(h)], gb[:, 0:G0].unsqueeze(1).broadcast_to([HD0, NWIN, G0])))
                        a_kr.inc(dve.tensor_copy(a_vg[r, p % 2, h * HD0:(h + 1) * HD0], gb[:, P + h * HD0:P + (h + 1) * HD0]))
                    a_kr.wait(dve, b, a_kr.n)
                    dve.sem_inc(GA.free[(g + 3) % 2], 1)

                def ttr(n):
                    p, w, j, h = unit_a(n)
                    sp = a_span(j, h)
                    a_sf.wait(dve, b, n + 1)
                    if n >= 3:
                        a_exp.wait(dve, b, n - 2)
                    settle(dve)
                    a_ttr.inc(dve.tensor_tensor_reduce(a_s[:, n % 3, sp], ps[:, n % S_BANKS, sp],
                                                       a_mask[:, w * 2 + j, h, sp], -HD0 ** -0.5, BIG, ALU.add, ALU.min,
                                                       a_mn[:, n:n + 1]))

                def recip(n):
                    a_exp.wait(dve, b, n + 1)
                    a_rdn.inc(dve.reciprocal(a_rd[:, n:n + 1], a_den[:, n:n + 1]))

                def evac_pt(n):
                    p, w, j, h = unit_a(n)
                    wi = n // 4
                    a_t.wait(dve, b, n + 1)
                    if wi >= 2:
                        a_pv.wait(dve, b, wi - 1)
                    v = ps[:, PT_BANK + 1, 0:(j + 2) * P].rearrange("p (k c) -> p k c", c=P)
                    step = 2 if j == 0 else 1
                    a_pe[1].inc(dve.tensor_copy(a_pt[:, wi % 2, 2:5:step, j * P:(j + 1) * P], v))

                def evac_o(p):
                    a_pv.wait(dve, b, NWIN * (p + 1))
                    a_oev.inc(dve.tensor_copy(a_o[:, p, :], ps[:, O_BANK, :]))

                evac_k(0)
                for n in range(NU + LAG_PV + 3):
                    if n < NU:
                        ttr(n)
                    if 0 <= n - LAG_E < NU:
                        recip(n - LAG_E)
                    if n < NU and n % 8 == 5 and n // 8 + 1 < PAIRS:
                        evac_k(n // 8 + 1)
                    m = n - LAG_T
                    if 0 <= m < NU and m % 2 == 1:
                        evac_pt(m)
                    m = n - LAG_PV - 2
                    if m >= 0 and m % 8 == 7:
                        evac_o(m // 8)
                a_xn.wait(dve, b, 1)
                for k in range(KC):
                    GA.wait(dve, b, GA_OUT + k)
                    xk = xT[:, k, chunk(b)]
                    dve.tensor_tensor(xk, xk, GA.bank(GA_OUT + k), ALU.add).then_inc(a_go, 1)
                dve.wait_ge(a_go, b * A_GO + 3)
                for k in range(KC):
                    dve.sem_inc(GA.free[(GA_OUT + k) % 2], 1)
            for q in (a_ln, a_dv, a_selr, a_kr, a_ttr, a_rdn, a_pe[1], a_oev):
                q.close()

        SCX = HDX ** -0.5
        NG = HPG * NT
        NX = GX * NG
        NQ = GX * HPG

        def cross(l):
            sparse = l == 1
            T = "x_"
            wq, wk, wv, wo = xw[l]
            bq, bk, bo, bv = col(f"bq{l}"), col(f"bk{l}"), col(f"bo{l}"), row(f"bv{l}")
            X_MEAN, X_VAR, X_GRP, X_OUT = 0, 1, 2, 2 + 3 * GX
            G = Gen(T + "g", X_OUT + KC)
            go, go0 = shared(T + "go", 1 + KC * B)
            ln, lnact = Count(T + "ln", 3), Count(T + "lnact", 2)
            cld, cld0 = shared(T + "ctx", 16 * B)
            cused = Count(T + "cused", GX)
            qr, kr, kz, vr = Count(T + "q", GX), Count(T + "k", GX), Count(T + "kz", GX * HPG), Count(T + "v", GX * NT)
            sf, ttr, ex, rdn, scl = (Count(T + n, NX) for n in ("s", "ttr", "exp", "rdn", "scl"))
            tn = Count(T + "t", NX)
            pte = [Count(T + "pteA", NX // 2), Count(T + "pteD", NX // 2)]
            pv, oev = Count(T + "pv", NQ), Count(T + "oev", GX)
            if sparse:
                sev = Count(T + "sev", NX)
                fs = Count(T + "f", NX * NEWTON)
                cn = Count(T + "cnt", NX * NEWTON)
                th = Count(T + "tau", NQ * (5 + 5 * NEWTON))
                pr = Count(T + "p", NX)

            def width(j):
                return S if sparse else P * (j + 1)

            LAG_E, LAG_T, LAG_PV = 1, 3, 4

            def head_keys(hh):
                return x_kz[:, hh, :] if hh < 4 else x_ring[:, 6, hh - 4, :]

            def xbuf(n):
                return x_s[:, n // 8 % 2, n // 4 % 2, n % 4, :]

            def probs(n):
                return xbuf(n) if sparse else x_s[:, 1, 0, n % 3, 0:width(n % NT)]

            def f_steps(q, it):
                return 8 * NEWTON * (q // 2) + 8 * it + 4 * (q % 2 + 1)

            def th_steps(q, it):
                base = q // 2 * 2 * (5 + 5 * NEWTON) + 10
                return base if it == 0 else base + (2 * (it - 1) + q % 2 + 1) * 5

            def on_pe(pe):
                def mean(b, n, src):
                    G.claim(pe, b, n)
                    for k in range(KC):
                        mm = pe.matmul(G.bank(n), meanw[:], src(k), start=(k == 0), stop=(k == KC - 1))
                    G.filled(mm, n)

                with pe.Fori(0, B) as b:
                    pe.wait_ge(go, b * KC + go0 + 1)
                    mean(b, X_MEAN, lambda k: xT[:, k, chunk(b)])
                    lnact.wait(pe, b, 1)
                    mean(b, X_VAR, lambda k: x_sq[:, k, :])
                    ln.wait(pe, b, 3)
                    pe.wait_ge(loads[f"xw{l}"], 64)

                    def project(g):
                        u = X_GRP + 3 * g
                        sl = slice(g * P, (g + 1) * P)
                        for m, w, src in ((0, wq, x_h), (1, wk, x_c)):
                            if m == 1 and g == 0:
                                pe.wait_ge(cld, b * 16 + cld0 + 16)
                            G.claim(pe, b, u + m)
                            for k in range(KC):
                                mm = pe.matmul(G.bank(u + m), w[:, k, sl], src[:, k, :], start=(k == 0), stop=(k == KC - 1))
                            G.filled(mm, u + m)
                        G.claim(pe, b, u + 2)
                        for i in range(NT):
                            for k in range(KC):
                                mm = pe.matmul(G.bank(u + 2)[:, i * P:(i + 1) * P], x_c[:, k, i * P:(i + 1) * P], wv[:, k, sl],
                                               start=(k == 0), stop=(k == KC - 1))
                        G.filled(mm, u + 2)

                    def scores(n):
                        g, hh, j = n // NG, n // NT % HPG, n % NT
                        if hh == 0 and j == 0:
                            qr.wait(pe, b, g + 1)
                        if j == 0:
                            kz.wait(pe, b, n // NT + 1)
                        if n >= S_BANKS:
                            (sev if sparse else ttr).wait(pe, b, n - S_BANKS + 1)
                        W = width(j)
                        sf.inc(pe.matmul(ps[:, n % S_BANKS, 0:W], x_q[:, g, j * P:(j + 1) * P], head_keys(hh)[:, 0:W],
                                         start=True, stop=True))

                    def turn(n):
                        (pr if sparse else scl).wait(pe, b, n + 1)
                        if n >= 2:
                            pte[n % 2].wait(pe, b, n // 2)
                        for k in range(width(n % NT) // P):
                            mm = pe.transpose(ps[:, PT_BANK + n % 2, k * P:(k + 1) * P], probs(n)[:, k * P:(k + 1) * P], ident)
                        tn.inc(mm)

                    def values(q):
                        g, hh = divmod(q, HPG)
                        for c in pte:
                            c.wait(pe, b, 2 * (q + 1))
                        if hh == 0:
                            vr.wait(pe, b, NT * (g + 1))
                        for k in range(NT):
                            lo = 0 if sparse else k * P
                            mm = pe.matmul(ps[:, O_BANK, lo:S], x_vz[:, k, hh * P:(hh + 1) * P], x_pt[:, q % 2, k, lo:S],
                                           start=(hh == 0 and k == 0), stop=(hh == HPG - 1 and k == NT - 1),
                                           skip_group_check=True)
                        pv.inc(mm)

                    for g in range(GX):
                        if g:
                            oev.wait(pe, b, g)
                        project(g)
                        N0 = g * NG
                        if not sparse:
                            for n in range(NG + LAG_PV + 1):
                                if n < NG:
                                    scores(N0 + n)
                                if 0 <= n - LAG_T < NG:
                                    turn(N0 + n - LAG_T)
                                m = n - LAG_PV - 1
                                if m >= 0 and m % NT == NT - 1:
                                    values((N0 + m) // NT)
                        else:
                            for n0 in range(0, NG + 8, 8):
                                for n in range(n0, n0 + 8):
                                    if n < NG:
                                        scores(N0 + n)
                                for n in range(n0 - 8, n0):
                                    if n >= 0:
                                        turn(N0 + n)
                                        if n % NT == NT - 1:
                                            values((N0 + n) // NT)
                    oev.wait(pe, b, GX)
                    for k in range(KC):
                        G.claim(pe, b, X_OUT + k)
                        for g in range(GX):
                            mm = pe.matmul(G.bank(X_OUT + k), wo[:, g, k * P:(k + 1) * P], x_o[:, g, :],
                                           start=(g == 0), stop=(g == GX - 1))
                        G.filled(mm, X_OUT + k)

            def on_act(act):
                with act.Fori(0, B) as b:
                    ln.wait(act, b, 1)
                    lnact.inc(act.activation(x_sq[:], x_xc[:], ACT.Square))
                    G.wait(act, b, X_VAR)
                    lnact.inc(act.activation(x_r[:, 0, :], G.bank(X_VAR), ACT.Sqrt, bias=eps[:, 0:1]))
                    i_free(act, G, b, X_VAR, lnact, 2)

                    def evac_pt(n):
                        q = n // NT
                        tn.wait(act, b, n + 1)
                        if q >= 2:
                            pv.wait(act, b, q - 1)
                        W = width(n % NT)
                        j = n % NT
                        pte[0].inc(act.copy(x_pt[:, q % 2, 0:W // P, j * P:(j + 1) * P],
                                            ps[:, PT_BANK, 0:W].rearrange("p (k c) -> p k c", c=P)))

                    for g in range(GX):
                        u = X_GRP + 3 * g
                        G.wait(act, b, u)
                        qr.inc(act.activation(x_q[:, g, :], G.bank(u), ACT.Identity, bias=bq[:, g:g + 1]))
                        i_free(act, G, b, u, qr, g + 1)
                        N0 = g * NG
                        if not sparse:
                            for n in range(NG + LAG_T + 1):
                                m = N0 + n - LAG_E
                                if 0 <= n - LAG_E < NG:
                                    ttr.wait(act, b, m + 1)
                                    if m >= 3:
                                        tn.wait(act, b, m - 2)
                                    ex.inc(act.activation(probs(m), x_s[:, 0, 0, m % 3, 0:width(m % NT)], ACT.Exp, scale=-1.0,
                                                          bias=x_st[:, 0, m:m + 1], accum_out=x_st[:, 1, m:m + 1]))
                                m = n - LAG_T
                                if 0 <= m < NG and m % 2 == 0:
                                    evac_pt(N0 + m)
                        else:
                            for n0 in range(0, NG + 8, 8):
                                quads = range((N0 + n0) // NT, (N0 + n0) // NT + 2)
                                if n0 < NG:
                                    for n in range(N0 + n0, N0 + n0 + 8):
                                        sf.wait(act, b, n + 1)
                                        if n >= 16:
                                            tn.wait(act, b, n - 15)
                                        sev.inc(act.activation(xbuf(n), ps[:, n % S_BANKS, :], ACT.Identity, scale=SCX,
                                                               accum_out=x_st[:, 0, n:n + 1]))
                                for it in range(NEWTON):
                                    if n0 < NG:
                                        for q in quads:
                                            th.wait(act, b, th_steps(q, it))
                                            for n in range(4 * q, 4 * q + 4):
                                                if fs.n >= 4:
                                                    fs.wait(act, b, fs.n - 3)
                                                fs.inc(act.activation(x_ja[:, n % 4, :], xbuf(n), ACT.Relu,
                                                                      bias=x_st[:, 1, n:n + 1], accum_out=x_st[:, 2, n:n + 1]))
                                    if n0 and it < 8 and it % 2 == 0:
                                        evac_pt(N0 + n0 - 8 + it)

            def on_pool(pool):
                with pool.Fori(0, B) as b:
                    for g in range(GX):
                        kr.wait(pool, b, g + 1)
                        settle(pool)
                        for hh in range(HPG):
                            kz.inc(pool.tensor_scalar(head_keys(hh), x_k[:, 0, :], const("heads")[:, hh:hh + 1], 1.0,
                                                      ALU.mult, ALU.mult))
                        if not sparse:
                            for n in range(g * NG, (g + 1) * NG):
                                rdn.wait(pool, b, n + 1)
                                settle(pool)
                                scl.inc(pool.tensor_scalar(probs(n), probs(n), x_st[:, 2, n:n + 1], 1.0, ALU.mult, ALU.mult))

            def on_dve(dve, before, count):
                dve.wait_ge(before, count)
                dve.memset(x_vz[:], 0.0).then_inc(go, 1)
                with dve.Fori(0, B) as b:
                    x = xT[:, :, chunk(b)]
                    dve.wait_ge(go, b * KC + go0 + 1)
                    G.wait(dve, b, X_MEAN)
                    ln.link(dve, b, dve.tensor_tensor(x_xc[:], x, G.bank(X_MEAN).unsqueeze(1).broadcast_to([P, KC, S]), ALU.subtract))
                    dve.sem_inc(G.free[X_MEAN % 2], 1)
                    lnact.wait(dve, b, 2)
                    ln.link(dve, b, dve.reciprocal(x_r[:, 1, :], x_r[:, 0, :]))
                    ln.inc(dve.tensor_tensor(x_h[:], x_xc[:], x_r[:, 1, :].unsqueeze(1).broadcast_to([P, KC, S]), ALU.mult))

                    def evac_pt(n):
                        q = n // NT
                        tn.wait(dve, b, n + 1)
                        if q >= 2:
                            pv.wait(dve, b, q - 1)
                        W = width(n % NT)
                        j = n % NT
                        pte[1].inc(dve.tensor_copy(x_pt[:, q % 2, 0:W // P, j * P:(j + 1) * P],
                                                   ps[:, PT_BANK + 1, 0:W].rearrange("p (k c) -> p k c", c=P)))

                    for g in range(GX):
                        u = X_GRP + 3 * g
                        N0 = g * NG
                        G.wait(dve, b, u + 1)
                        kr.link(dve, b, dve.tensor_scalar(x_k[:, 0, :], G.bank(u + 1), bk[:, g:g + 1], None, ALU.add))
                        dve.sem_inc(G.free[(u + 1) % 2], 1)
                        G.wait(dve, b, u + 2)
                        for i in range(NT):
                            o = x_vz[:, i, :].rearrange("p (h c) -> p h c", h=HPG)[:, :, 0:HDX]
                            vr.inc(dve.tensor_tensor(o, G.bank(u + 2)[:, i * P:(i + 1) * P].rearrange("p (h c) -> p h c", h=HPG),
                                                     bv[:, g * P:(g + 1) * P].rearrange("p (h c) -> p h c", h=HPG), ALU.add))
                        vr.wait(dve, b, vr.n)
                        dve.sem_inc(G.free[(u + 2) % 2], 1)
                        dve.sem_inc(cused.sem, 1)
                        if not sparse:
                            for n in range(NG + LAG_T + 1):
                                if n < NG:
                                    m = N0 + n
                                    sf.wait(dve, b, m + 1)
                                    if m >= 3:
                                        ex.wait(dve, b, m - 2)
                                    settle(dve)
                                    W = width(m % NT)
                                    ttr.inc(dve.tensor_tensor_reduce(x_s[:, 0, 0, m % 3, 0:W], ps[:, m % S_BANKS, 0:W],
                                                                     const("tri")[:, S - W:S], -SCX, BIG, ALU.add, ALU.min,
                                                                     x_st[:, 0, m:m + 1]))
                                m = N0 + n - LAG_E
                                if 0 <= n - LAG_E < NG:
                                    ex.wait(dve, b, m + 1)
                                    rdn.inc(dve.reciprocal(x_st[:, 2, m:m + 1], x_st[:, 1, m:m + 1]))
                                m = n - LAG_T
                                if 0 <= m < NG and m % 2 == 1:
                                    evac_pt(N0 + m)
                        else:
                            for n0 in range(0, NG + 8, 8):
                                quads = range((N0 + n0) // NT, (N0 + n0) // NT + 2)
                                if n0 < NG:
                                    for q in quads:
                                        sev.wait(dve, b, 4 * (q + 1))
                                        v = slice(4 * q, 4 * q + 4)
                                        th.link(dve, b, dve.tensor_reduce(x_st[:, 7, v], x_s[:, n0 // 8 % 2, q % 2], AX.X, ALU.max))
                                        th.link(dve, b, dve.tensor_scalar(x_st[:, 7, v], x_st[:, 7, v], -1.0, None, ALU.add))
                                        th.link(dve, b, dve.tensor_scalar(x_st[:, 3, v], x_st[:, 0, v], -1.0, 1.0 / S, ALU.add, ALU.mult))
                                        th.link(dve, b, dve.tensor_tensor(x_st[:, 3, v], x_st[:, 3, v], x_st[:, 7, v], ALU.max))
                                        th.inc(dve.tensor_scalar(x_st[:, 1, v], x_st[:, 3, v], -1.0, None, ALU.mult))
                                for it in range(NEWTON):
                                    if n0 < NG:
                                        for q in quads:
                                            v = slice(4 * q, 4 * q + 4)
                                            for n in range(4 * q, 4 * q + 4):
                                                if cn.n >= 4:
                                                    cn.wait(dve, b, cn.n - 3)
                                                cn.inc(dve.tensor_scalar(x_jd[:, n % 4, :], xbuf(n), x_st[:, 3, n:n + 1], None,
                                                                         ALU.is_gt, ALU.add, accum_out=x_st[:, 4, n:n + 1]))
                                            cn.wait(dve, b, cn.n)
                                            th.link(dve, b, dve.tensor_scalar(x_st[:, 5, v], x_st[:, 4, v], 1.0, None, ALU.max))
                                            th.link(dve, b, dve.reciprocal(x_st[:, 5, v], x_st[:, 5, v]))
                                            fs.wait(dve, b, f_steps(q, it))
                                            th.link(dve, b, dve.scalar_tensor_tensor(x_st[:, 6, v], x_st[:, 2, v], -1.0, x_st[:, 5, v],
                                                                                     ALU.add, ALU.mult))
                                            th.inc(dve.tensor_tensor(x_st[:, 3, v], x_st[:, 3, v], x_st[:, 6, v], ALU.add))
                                            th.link(dve, b, dve.tensor_tensor(x_st[:, 1, v], x_st[:, 1, v], x_st[:, 6, v], ALU.subtract))
                                    if n0 and it < 8 and it % 2 == 1:
                                        evac_pt(N0 + n0 - 8 + it)
                                if n0 < NG:
                                    for n in range(N0 + n0, N0 + n0 + 8):
                                        pr.inc(dve.tensor_scalar(xbuf(n), xbuf(n), x_st[:, 3, n:n + 1], 0.0, ALU.subtract, ALU.max))
                        pv.wait(dve, b, HPG * (g + 1))
                        oev.inc(dve.tensor_copy(x_o[:, g, :], ps[:, O_BANK, :]))
                    for k in range(KC):
                        G.wait(dve, b, X_OUT + k)
                        xk = xT[:, k, chunk(b)]
                        dve.scalar_tensor_tensor(xk, G.bank(X_OUT + k), bo[:, k:k + 1], xk, ALU.add, ALU.add).then_inc(go, 1)
                    dve.wait_ge(go, b * KC + go0 + 1 + KC)
                    for k in range(KC):
                        dve.sem_inc(G.free[(X_OUT + k) % 2], 1)

            return on_pe, on_act, on_pool, on_dve, go, cld, cused

        class Norm:
            def __init__(self, tag, G, h, xc, sq, r):
                self.G, self.h, self.xc, self.sq, self.r = G, h, xc, sq, r
                self.steps, self.act_steps = Count(tag + "ln", 3), Count(tag + "lnact", 2)

            def on_pe(self, pe, b):
                for n, src in ((0, lambda k: xT[:, k, chunk(b)]), (1, lambda k: self.sq[:, k, :])):
                    if n:
                        self.act_steps.wait(pe, b, 1)
                    self.G.claim(pe, b, n)
                    for k in range(KC):
                        mm = pe.matmul(self.G.bank(n), meanw[:], src(k), start=(k == 0), stop=(k == KC - 1))
                    self.G.filled(mm, n)

            def on_act(self, act, b):
                self.steps.wait(act, b, 1)
                self.act_steps.inc(act.activation(self.sq[:], self.xc[:], ACT.Square))
                self.G.wait(act, b, 1)
                self.act_steps.inc(act.activation(self.r[:, 0, :], self.G.bank(1), ACT.Sqrt, bias=eps[:, 0:1]))
                i_free(act, self.G, b, 1, self.act_steps, 2)

            def on_dve(self, dve, b):
                self.G.wait(dve, b, 0)
                m = self.G.bank(0).unsqueeze(1).broadcast_to([P, KC, S])
                self.steps.link(dve, b, dve.tensor_tensor(self.xc[:], xT[:, :, chunk(b)], m, ALU.subtract))
                dve.sem_inc(self.G.free[0], 1)
                self.act_steps.wait(dve, b, 2)
                self.steps.link(dve, b, dve.reciprocal(self.r[:, 1, :], self.r[:, 0, :]))
                rs = self.r[:, 1, :].unsqueeze(1).broadcast_to([P, KC, S])
                self.steps.inc(dve.tensor_tensor(self.h[:], self.xc[:], rs, ALU.mult))

            def ready(self, eng, b):
                self.steps.wait(eng, b, 3)

        EG_GATE, EG_COMB = 2, 3
        EG = Gen("mg", 4)
        e_norm = Norm("m_", EG, m_hc, m_xc, m_sq, m_r)
        e_ones = sem("m_ones")
        e_go = sem("m_go")
        e_hcp = Count("m_hcp", 1)
        e_sig = Count("m_sig", 1)
        e_gate = Count("m_gate", 14)
        e_rec, e_fin = Count("m_rec", 2), Count("m_fin", 1)
        e_comb = sem("m_comb_out")
        e_wl = [sem(f"m_weights{k}") for k in range(2)]
        e_cbl = [sem(f"m_cb{k}") for k in range(2)]
        e_guf, e_silu, e_mul, e_act, e_dn, e_acc = (sem(f"m_{n}") for n in ("gu", "silu", "mul", "act", "down", "acc"))
        UE = 2 * B
        NE = E + 1
        DN_BANK = 4

        def at(eng, s, e, n):
            if not (isinstance(e, int) and e * UE + n <= 0):
                eng.wait_ge(s, e * UE + n)

        def experts(eng, step):
            step(0, 0, 0)
            with eng.Fori(0, E // 2) as i:
                step(i * 2 + 1, 1, i)
                step(i * 2 + 2, 0, i + 1)

        def stage3_pe(pe):
            with pe.Fori(0, B) as b:
                pe.wait_ge(e_go, b + 1)
                e_norm.on_pe(pe, b)
                e_norm.ready(pe, b)
                EG.claim(pe, b, EG_GATE)
                gw = col("gate_w").rearrange("p (k e) -> p k e", k=KC)
                for i in range(NT):
                    for k in range(KC):
                        mm = pe.matmul(EG.bank(EG_GATE)[:, i * E:(i + 1) * E], m_hc[:, k, i * P:(i + 1) * P], gw[:, k, :],
                                       start=(k == 0), stop=(k == KC - 1))
                EG.filled(mm, EG_GATE)
                e_fin.wait(pe, b, 1)
                EG.claim(pe, b, EG_COMB)
                for i in range(NT):
                    mm = pe.transpose(EG.bank(EG_COMB)[0:NE, i * P:(i + 1) * P], m_w17[:, i, :], ident)
                EG.filled(mm, EG_COMB)
            e_hcp.wait(pe, B - 1, 1)

            def down(e, buf, c):
                at(pe, e_act, e, 2 * c + 2)
                for m in range(KC):
                    at(pe, e_acc, e, 2 * c + m - 3)
                    for k in range(KC):
                        mm = pe.matmul(ps[:, DN_BANK + (2 * c + m) % 4, :], m_wd[:, buf, k, m * P:(m + 1) * P],
                                       m_a[:, c % 2, k, :], start=(k == 0), stop=(k == KC - 1))
                    mm.then_inc(e_dn, 1)

            def expert(e, buf, r):
                pe.wait_ge(e_wl[buf], r * 48 + 48)
                for c in range(B):
                    for h in range(2):
                        u = 2 * c + h
                        at(pe, e_mul, e, u - 1)
                        for m, w in ((0, m_wg), (1, m_wu)):
                            for k in range(KC):
                                mm = pe.matmul(ps[:, 2 * h + m, :], w[:, buf, k, h * P:(h + 1) * P],
                                               m_h[:, k, c * S:(c + 1) * S], start=(k == 0), stop=(k == KC - 1))
                        mm.then_inc(e_guf, 1)
                    if c:
                        down(e, buf, c - 1)
                    elif not isinstance(e, int):
                        down(e - 1, 1 - buf, B - 1)
            experts(pe, expert)
            down(E, 0, B - 1)

        def stage3_act(act):
            act.wait_ge(e_ones, 1)
            act.sem_inc(e_go, 1)
            with act.Fori(0, B) as b:
                e_norm.on_act(act, b)
                e_norm.ready(act, b)
                e_hcp.inc(act.copy(m_h[:, :, chunk(b)], m_hc[:]))
                EG.wait(act, b, EG_GATE)
                e_sig.inc(act.activation(m_sg[:].rearrange("p i e -> p (i e)"), EG.bank(EG_GATE)[:, 0:NT * E], ACT.Sigmoid))
                i_free(act, EG, b, EG_GATE, e_sig, 1)
                EG.wait(act, b, EG_COMB)
                act.copy(m_comb[:, chunk(b)], EG.bank(EG_COMB)[0:NE, :]).then_inc(e_go, 1)
                act.wait_ge(e_go, b + 2)
                act.sem_inc(EG.free[EG_COMB % 2], 1)

            def expert(e, buf, r):
                for u in range(UE):
                    at(act, e_guf, e, u + 1)
                    at(act, e_mul, e, u - 1)
                    act.activation(m_g[:, u % 2, :], ps[:, 2 * (u % 2), :], ACT.Silu).then_inc(e_silu, 1)
            experts(act, expert)

        def stage3_pool(pool):
            def expert(e, buf, r):
                pool.wait_ge(e_cbl[buf], r * 16 + 16)
                for u in range(UE):
                    c, h = divmod(u, 2)
                    at(pool, e_mul, e, u + 1)
                    at(pool, e_dn, e, 2 * c - 2)
                    pool.tensor_tensor(m_a[:, c % 2, h, :], m_m[:, u % 2, :], m_cb[:, buf, c * S:(c + 1) * S],
                                       ALU.mult).then_inc(e_act, 1)
            experts(pool, expert)

        def stage3_dve(dve, before, count):
            dve.wait_ge(before, count)
            dve.memset(m_w17[:], 1.0).then_inc(e_ones, 1)
            with dve.Fori(0, B) as b:
                e_norm.on_dve(dve, b)
                ch = lambda ins: e_gate.link(dve, b, ins)
                e_sig.wait(dve, b, 1)
                ch(dve.tensor_tensor(m_sel[:], m_sg[:], row("expert_bias").unsqueeze(1).broadcast_to([P, NT, E]), ALU.add))
                for i in range(NT):
                    o = m_sel[:, i, :].unsqueeze(1).broadcast_to([P, E, E])
                    s = m_sel[:, i, :].unsqueeze(2).broadcast_to([P, E, E])
                    e_gate.inc(dve.tensor_tensor(m_gt[:, i], o, s, ALU.is_gt))
                    e_gate.inc(dve.tensor_tensor(m_eq[:, i], o, s, ALU.is_equal))
                e_gate.wait(dve, b, 9)
                ch(dve.tensor_tensor(m_eq[:].rearrange("p i e f -> p i (e f)"), m_eq[:].rearrange("p i e f -> p i (e f)"),
                                     const("before").unsqueeze(1).broadcast_to([P, NT, E * E]), ALU.mult))
                ch(dve.tensor_tensor(m_gt[:].rearrange("p i e f -> p (i e f)"), m_gt[:].rearrange("p i e f -> p (i e f)"),
                                     m_eq[:].rearrange("p i e f -> p (i e f)"), ALU.add))
                ch(dve.tensor_reduce(m_sel[:], m_gt[:], AX.X, ALU.add))
                ch(dve.scalar_tensor_tensor(m_sel[:], m_sel[:], TOPK - 0.5, m_sg[:], ALU.is_lt, ALU.mult))
                ch(dve.tensor_reduce(m_sum[:], m_sel[:], AX.X, ALU.add))
                e_rec.link(dve, b, dve.reciprocal(m_sum[:], m_sum[:]))
                e_rec.link(dve, b, dve.tensor_tensor(m_sel[:], m_sel[:], m_sum[:].unsqueeze(2).broadcast_to([P, NT, E]), ALU.mult))
                dve.wait_ge(e_go, b + 1)
                e_fin.inc(dve.tensor_scalar(m_w17[:, :, 0:E], m_sel[:], ROUTE_SCALE, None, ALU.mult))

            def acc(e, c):
                for m in range(KC):
                    at(dve, e_dn, e, 2 * c + m + 1)
                    at(dve, e_acc, e, 2 * c + m - 1)
                    xk = xT[:, m, c * S:(c + 1) * S]
                    dve.tensor_tensor(xk, xk, ps[:, DN_BANK + (2 * c + m) % 4, :], ALU.add).then_inc(e_acc, 1)

            def expert(e, buf, r):
                for u in range(UE):
                    at(dve, e_silu, e, u + 1)
                    at(dve, e_act, e, u - 1)
                    dve.tensor_tensor(m_m[:, u % 2, :], m_g[:, u % 2, :], ps[:, 2 * (u % 2) + 1, :], ALU.mult).then_inc(e_mul, 1)
                    if u % 2:
                        if u > 1:
                            acc(e, u // 2 - 1)
                        elif not isinstance(e, int):
                            acc(e - 1, B - 1)
            experts(dve, expert)
            acc(E, B - 1)

        def stage3_loads(sp):
            def matrices(e, buf):
                for w, n in ((m_wg, "eg"), (m_wu, "eu"), (m_wd, "ed")):
                    src = a[n][:, bass.ds(e, 1)].rearrange("p o k n -> p (o k) n")
                    sp.dma_start(w[:, buf], src).then_inc(e_wl[buf], 16)

            def weights(e, buf):
                sp.dma_start(m_cb[:, buf, :], a["comb"][bass.ds(e, 1), :].broadcast_to([P, TOK])).then_inc(e_cbl[buf], 16)

            matrices(0, 0)
            matrices(1, 1)
            sp.wait_ge(e_go, 1 + B)
            sp.dma_start(a["comb"], m_comb[:]).then_inc(e_comb, 16)
            sp.wait_ge(e_comb, 16)
            weights(0, 0)
            weights(1, 1)
            def refill(e, buf):
                at(sp, e_dn, e - 1, 0)
                matrices(e, buf)
                at(sp, e_act, e - 1, 0)
                weights(e, buf)

            with sp.Fori(0, E // 2 - 1) as i:
                refill(i * 2 + 2, 0)
                refill(i * 2 + 3, 1)
            refill(E, 0)

        END3 = UE * NE

        NG_OUT = 2
        NGB = Gen("ng", NG_OUT + KC)
        n_norm = Norm("n_", NGB, n_h, n_xc, n_sq, n_r)
        n_go = sem("n_go")
        n_kvf, n_kva = Count("n_kvf", NT), Count("n_kva", NT)
        n_ch = Count("n_ch", 5 * NT + 3)
        n_agg, n_var, n_qh = Count("n_agg", NT), Count("n_var", 1), Count("n_qh", NT)
        n_rt = Count("n_root", 1)
        n_qf, n_qa, n_mx = Count("n_qf", NT), Count("n_qa", NT), Count("n_mx", NT)
        n_sub, n_ex, n_sum, n_rc, n_nm = (Count("n_" + x, NT) for x in ("sub", "exp", "sum", "rec", "nrm"))
        n_fin = Count("n_fin", NT * (2 + 2 * B))

        def stage4_pe(pe):
            with pe.Fori(0, B) as b:
                pe.wait_ge(n_go, b * KC + 1)
                n_norm.on_pe(pe, b)
                n_norm.ready(pe, b)
                pe.wait_ge(loads["w1"], 32)
                for i in range(NT):
                    if i >= 2:
                        n_kva.wait(pe, b, i - 1)
                    for k in range(KC):
                        mm = pe.matmul(ps[:, 4 + i % 2, 0:KV1], n_h[:, k, i * P:(i + 1) * P], wkv1[:, k, :],
                                       start=(k == 0), stop=(k == KC - 1))
                    n_kvf.inc(mm)
                for i in range(NT):
                    if i >= 2:
                        n_qa.wait(pe, b, i - 1)
                    for m in range(2):
                        for k in range(KC):
                            mm = pe.matmul(ps[:, 2 * (i % 2) + m, :], n_h[:, k, i * P:(i + 1) * P],
                                           wq1[:, k, m * S:(m + 1) * S], start=(k == 0), stop=(k == KC - 1))
                    n_qf.inc(mm)
                for k in range(KC):
                    NGB.claim(pe, b, NG_OUT + k)
                for i in range(NT):
                    n_fin.wait(pe, b, (i + 1) * (2 + 2 * B))
                    for k in range(KC):
                        mm = pe.transpose(NGB.bank(NG_OUT + k)[:, i * P:(i + 1) * P], n_y[:, i, k * P:(k + 1) * P], ident)
                        if i == NT - 1:
                            NGB.filled(mm, NG_OUT + k)

        def stage4_act(act):
            with act.Fori(0, B) as b:
                n_norm.on_act(act, b)
                n_var.wait(act, b, 1)
                n_rt.inc(act.activation(n_mv[:, 1], n_mv[:, 0], ACT.Sqrt, bias=eps[:, 0:1]))
                for i in range(NT):
                    n_sub.wait(act, b, i + 1)
                    n_ex.inc(act.activation(n_q[:, i % 3, :], n_q[:, i % 3, :], ACT.Exp))

        def heads_of(v):
            return v.rearrange("p (h c) -> p h c", h=H1)

        def stage4_pool(pool):
            with pool.Fori(0, B) as b:
                def normalise(i):
                    n_rc.wait(pool, b, i + 1)
                    q = heads_of(n_q[:, i % 3, :])
                    n_nm.inc(pool.tensor_tensor(q, q, n_sm[:, 2, i, :].unsqueeze(2).broadcast_to([P, H1, K1]), ALU.mult))
                for i in range(NT):
                    n_mx.wait(pool, b, i + 1)
                    q = heads_of(n_q[:, i % 3, :])
                    n_sub.inc(pool.tensor_tensor(q, q, n_sm[:, 0, i, :].unsqueeze(2).broadcast_to([P, H1, K1]), ALU.subtract))
                    if i:
                        normalise(i - 1)
                normalise(NT - 1)

        def stage4_dve(dve, before, count):
            dve.wait_ge(before, count)
            dve.memset(n_hist[:], 0.0).then_inc(n_go, 1)
            with dve.Fori(0, B) as b:
                ch = lambda ins: n_ch.link(dve, b, ins)
                dve.wait_ge(n_go, b * KC + 1)
                n_norm.on_dve(dve, b)
                for i in range(NT):
                    n_kvf.wait(dve, b, i + 1)
                    n_kva.link(dve, b, dve.tensor_tensor(n_kv[:, i, :], ps[:, 4 + i % 2, 0:KV1], row("bkv"), ALU.add))
                    for m, sl in ((0, slice(0, K1)), (1, slice(K1, KV1))):
                        n_ch.inc(dve.bn_stats(n_bs[:, i, m, :], n_kv[:, i, sl]))
                n_ch.wait(dve, b, 2 * NT)
                settle(dve)
                for i in range(NT):
                    for m in range(2):
                        ins = dve.bn_aggr(n_ba[:, i, m, :], n_bs[:, i, m, :])
                        if m:
                            n_ch.inc(ins)
                        else:
                            n_agg.inc(ins)
                n_agg.wait(dve, b, NT)
                n_ch.wait(dve, b, 3 * NT)
                n_var.inc(dve.tensor_copy(n_mv[:, 0], n_ba[:, :, :, 1]))

                def queries(i):
                    n_qf.wait(dve, b, i + 1)
                    if i >= 3:
                        n_fin.wait(dve, b, (i - 3) * (2 + 2 * B) + 1)
                    for m in range(2):
                        sl = slice(m * S, (m + 1) * S)
                        ins = dve.tensor_tensor(n_q[:, i % 3, sl], ps[:, 2 * (i % 2) + m, :], row("bq")[:, sl], ALU.add)
                        (n_qa if m else n_qh).inc(ins)
                    n_qh.wait(dve, b, i + 1)
                    n_qa.wait(dve, b, i + 1)
                    n_mx.inc(dve.tensor_reduce(n_sm[:, 0, i, :], heads_of(n_q[:, i % 3, :]), AX.X, ALU.max))

                def sums(i):
                    n_ex.wait(dve, b, i + 1)
                    n_sum.link(dve, b, dve.tensor_reduce(n_sm[:, 1, i, :], heads_of(n_q[:, i % 3, :]), AX.X, ALU.add))
                    n_rc.inc(dve.reciprocal(n_sm[:, 2, i, :], n_sm[:, 1, i, :]))

                def result(i):
                    fin = lambda ins: n_fin.link(dve, b, ins)
                    n_nm.wait(dve, b, i + 1)
                    fin(dve.tensor_reduce(n_qn[:, 0, :], n_q[:, i % 3, :].rearrange("p (h c) -> p c h", h=H1), AX.X, ALU.add))
                    fin(dve.tensor_scalar(n_qn[:, 1, :], n_qn[:, 0, :], const("scal")[:, bass.ds(b, 1)], None, ALU.mult))
                    for s in range(B):
                        n_fin.inc(dve.scalar_tensor_tensor(n_jk[:, s, :], n_qn[:, 1, :], 1.0, n_hist[:, i, s, 0:K1], ALU.mult, ALU.mult,
                                                           accum_out=n_d[:, s:s + 1]))
                    n_fin.wait(dve, b, n_fin.n)
                    v = lambda s: n_hist[:, i, s, K1:KV1]
                    fin(dve.tensor_scalar(n_y[:, i, :], v(0), n_d[:, 0:1], None, ALU.mult))
                    for s in range(1, B):
                        fin(dve.scalar_tensor_tensor(n_y[:, i, :], v(s), n_d[:, s:s + 1], n_y[:, i, :], ALU.mult, ALU.add))

                queries(0)
                n_rt.wait(dve, b, 1)
                ch(dve.reciprocal(n_mv[:, 1], n_mv[:, 1]))
                for i in range(NT):
                    for m, sl in ((0, slice(0, K1)), (1, slice(K1, KV1))):
                        n_ch.inc(dve.tensor_scalar(n_kv[:, i, sl], n_kv[:, i, sl], n_ba[:, i, m, 0:1], n_mv[:, 1, i, m:m + 1],
                                                   ALU.subtract, ALU.mult))
                queries(1)
                n_ch.wait(dve, b, n_ch.n)
                ch(dve.tensor_tensor(n_kv[:], n_kv[:], row("gkv").unsqueeze(1).broadcast_to([P, NT, KV1]), ALU.mult))
                ch(dve.tensor_tensor(n_hist[:, :, bass.ds(b, 1), :].rearrange("p i o c -> p i (o c)"), n_kv[:],
                                     row("betakv").unsqueeze(1).broadcast_to([P, NT, KV1]), ALU.add))
                sums(0)
                for i in range(2, NT + 2):
                    if i < NT:
                        queries(i)
                    if i - 1 < NT:
                        sums(i - 1)
                    result(i - 2)
                for k in range(KC):
                    NGB.wait(dve, b, NG_OUT + k)
                    xk = xT[:, k, chunk(b)]
                    dve.tensor_tensor(xk, xk, NGB.bank(NG_OUT + k), ALU.add).then_inc(n_go, 1)
                dve.wait_ge(n_go, b * KC + 1 + KC)
                for k in range(KC):
                    dve.sem_inc(NGB.free[(NG_OUT + k) % 2], 1)

        FG_SC, FG_OH, FG_OUT = 2, 3, 4
        FG = Gen("fg", 6)
        f_norm = Norm("f_", FG, f_h, f_xc, f_sq, f_r)
        f_go = sem("f_go")
        f_sgn = sem("f_sign")
        f_ch = Count("f_ch", 5)
        f_ohr = Count("f_ohr", 2)
        f_bc, f_hm = Count("f_bc", T1), Count("f_hm", T1)
        f_use = Count("f_use", T1 - 1)

        def stage6_pe(pe):
            pe.wait_ge(f_sgn, 1)
            pe.wait_ge(loads["wt1"], 32)
            with pe.Fori(0, B) as b:
                pe.wait_ge(f_go, b * KC + 1)
                f_norm.on_pe(pe, b)
                f_norm.ready(pe, b)
                FG.claim(pe, b, FG_SC)
                for i in range(NT):
                    for k in range(KC):
                        mm = pe.matmul(FG.bank(FG_SC)[:, i * T1:(i + 1) * T1], f_h[:, k, i * P:(i + 1) * P],
                                       f_sg[:, k * T1:(k + 1) * T1], start=(k == 0), stop=(k == KC - 1))
                FG.filled(mm, FG_SC)
                f_ch.wait(pe, b, 5)
                FG.claim(pe, b, FG_OH)
                for i in range(NT):
                    mm = pe.transpose(FG.bank(FG_OH)[0:T1, i * P:(i + 1) * P], f_c[:, i, :], ident)
                FG.filled(mm, FG_OH)
                f_ohr.wait(pe, b, 2)
                for k in range(KC):
                    FG.claim(pe, b, FG_OUT + k)
                    pe.matmul(FG.bank(FG_OUT + k), bt1[:, k * P:(k + 1) * P], f_oh[:], start=True, stop=False, skip_group_check=True)

                def spread(t):
                    if t >= 4:
                        f_hm.wait(pe, b, t - 3)
                    f_bc.inc(pe.matmul(ps[:, t % 4, :], f_one[:, t * P:(t + 1) * P], f_ohb[:], start=True, stop=True))

                spread(0)
                spread(1)
                for t in range(T1):
                    if t + 2 < T1:
                        spread(t + 2)
                    f_hm.wait(pe, b, t + 1)
                    for k in range(KC):
                        for c in range(KC):
                            mm = pe.matmul(FG.bank(FG_OUT + k), wt1[:, t, c, k * P:(k + 1) * P], f_m[:, t % 4, c, :], start=False,
                                           stop=(t == T1 - 1 and c == KC - 1), skip_group_check=True)
                        if t == T1 - 1:
                            FG.filled(mm, FG_OUT + k)
                    if t < T1 - 1:
                        f_use.inc(mm)

        def stage6_act(act):
            act.wait_ge(f_go, 1)
            act.activation(f_sg[:], col("sigs"), ACT.Sign).then_inc(f_sgn, 1)
            with act.Fori(0, B) as b:
                f_norm.on_act(act, b)
                FG.wait(act, b, FG_OH)
                f_ohr.inc(act.copy(f_oh[:], FG.bank(FG_OH)[0:T1, :]))
                f_ohr.inc(act.copy(f_ohb[:], FG.bank(FG_OH)[0:T1, :]))
                i_free(act, FG, b, FG_OH, f_ohr, 2)

        def stage6_dve(dve, before, count):
            dve.wait_ge(before, count)
            dve.tensor_copy(f_one[:].rearrange("p (t c) -> p t c", c=P),
                            ident[0:T1, 0:T1].unsqueeze(2).broadcast_to([T1, T1, P])).then_inc(f_go, 1)
            with dve.Fori(0, B) as b:
                ch = lambda ins: f_ch.link(dve, b, ins)
                dve.wait_ge(f_go, b * KC + 1)
                f_norm.on_dve(dve, b)
                FG.wait(dve, b, FG_SC)
                s = FG.bank(FG_SC)[:, 0:NT * T1].rearrange("p (i t) -> p i t", t=T1)
                wide = lambda v: v.unsqueeze(2).broadcast_to([P, NT, T1])
                ch(dve.tensor_reduce(f_mx[:, 0, :], s, AX.X, ALU.max))
                ch(dve.tensor_tensor(f_c[:], s, wide(f_mx[:, 0, :]), ALU.is_equal))
                dve.sem_inc(FG.free[FG_SC % 2], 1)
                ch(dve.tensor_tensor(f_c[:], f_c[:], const("first").unsqueeze(1).broadcast_to([P, NT, T1]), ALU.mult))
                ch(dve.tensor_reduce(f_mx[:, 1, :], f_c[:], AX.X, ALU.max))
                ch(dve.tensor_tensor(f_c[:], f_c[:], wide(f_mx[:, 1, :]), ALU.is_equal))
                for t in range(T1):
                    f_bc.wait(dve, b, t + 1)
                    if t >= 4:
                        f_use.wait(dve, b, t - 3)
                    f_hm.inc(dve.tensor_tensor(f_m[:, t % 4], f_h[:], ps[:, t % 4, :].unsqueeze(1).broadcast_to([P, KC, S]), ALU.mult))
                for k in range(KC):
                    FG.wait(dve, b, FG_OUT + k)
                    xk = xT[:, k, chunk(b)]
                    dve.tensor_tensor(xk, xk, FG.bank(FG_OUT + k), ALU.add).then_inc(f_go, 1)
                dve.wait_ge(f_go, b * KC + 1 + KC)
                for k in range(KC):
                    dve.sem_inc(FG.free[(FG_OUT + k) % 2], 1)

        STEPS = 4
        DEPTH = STEPS + 3
        GROUPS = 64
        START = 0.9
        MASS_TOL = 2e-5
        LASTSLOT = NQ + STEPS + 2

        def sparse_quick():
            T = "y_"
            wq, wk, wv, wo = xw[1]
            bq, bk, bo, bv = col("bq1"), col("bk1"), col("bo1"), row("bv1")
            Y_Q, Y_K, Y_V, Y_OUT = 2, (4, 6), (5, 7), 8
            G = Gen(T + "g", Y_OUT + KC)
            norm = Norm(T, G, x_h, x_xc, x_sq, x_r)
            go = sem(T + "go")
            cld = sem(T + "ctx")
            cused = Count(T + "cused", GX)
            qr, kr, kz, vr = Count(T + "q", GX), Count(T + "k", GX), Count(T + "kz", NQ), Count(T + "v", GX * NT)
            sf, sev = Count(T + "s", NX), Count(T + "sev", NX)
            fs, cn = Count(T + "f", NX * STEPS), Count(T + "cnt", NX * STEPS)
            st = Count(T + "start", NQ * 11)
            up = Count(T + "up", 4 * (NQ + STEPS - 1))
            pr, tn = Count(T + "p", NX), Count(T + "t", NX)
            pte = [Count(T + "pteA", NX // 2), Count(T + "pteD", NX // 2)]
            pv, oev = Count(T + "pv", NQ), Count(T + "oev", GX)
            bad = Count(T + "bad", 4)
            F_, C_, U_, M_ = (x_st[:, k, :] for k in range(4))

            def xb(n):
                return x_ring[:, n // NT % DEPTH, n % NT, :]

            def active(t):
                return range(max(0, t - STEPS), min(NQ, t))

            def steps_before(t):
                return NT * sum(len(active(s)) for s in range(t))

            def on_pe(pe):
                with pe.Fori(0, B) as b:
                    pe.wait_ge(go, b * KC + 1)
                    norm.on_pe(pe, b)
                    norm.ready(pe, b)
                    pe.wait_ge(loads["xw1"], 64)

                    def project(u, w, src, g):
                        G.claim(pe, b, u)
                        for k in range(KC):
                            mm = pe.matmul(G.bank(u), w[:, k, g * P:(g + 1) * P], src[:, k, :], start=(k == 0), stop=(k == KC - 1))
                        G.filled(mm, u)

                    def project_values(g):
                        G.claim(pe, b, Y_V[g])
                        for i in range(NT):
                            for k in range(KC):
                                mm = pe.matmul(G.bank(Y_V[g])[:, i * P:(i + 1) * P], x_c[:, k, i * P:(i + 1) * P],
                                               wv[:, k, g * P:(g + 1) * P], start=(k == 0), stop=(k == KC - 1))
                        G.filled(mm, Y_V[g])

                    for g in range(GX):
                        project(Y_Q + g, wq, x_h, g)
                    pe.wait_ge(cld, b * 16 + 16)
                    project(Y_K[0], wk, x_c, 0)
                    project_values(0)

                    def scores(n):
                        q = n // NT
                        if n % NT == 0:
                            qr.wait(pe, b, q // HPG + 1)
                            kz.wait(pe, b, q + 1)
                        if n >= S_BANKS:
                            sev.wait(pe, b, n - S_BANKS + 1)
                        j = n % NT
                        sf.inc(pe.matmul(ps[:, n % S_BANKS, :], x_q[:, q // HPG, j * P:(j + 1) * P], x_kz[:, q % 4, :],
                                         start=True, stop=True))

                    def turn(n):
                        pr.wait(pe, b, n + 1)
                        if n >= 2:
                            pte[n % 2].wait(pe, b, n // 2)
                        for k in range(NT):
                            mm = pe.transpose(ps[:, PT_BANK + n % 2, k * P:(k + 1) * P], xb(n)[:, k * P:(k + 1) * P], ident)
                        tn.inc(mm)

                    def values(q):
                        g, hh = divmod(q, HPG)
                        for c in pte:
                            c.wait(pe, b, 2 * (q + 1))
                        if hh == 0:
                            vr.wait(pe, b, NT * (g + 1))
                            if g:
                                oev.wait(pe, b, g)
                        for k in range(NT):
                            mm = pe.matmul(ps[:, O_BANK, :], x_vz[:, k, hh * P:(hh + 1) * P], x_pt[:, q % 2, k, :],
                                           start=(hh == 0 and k == 0), stop=(hh == HPG - 1 and k == NT - 1),
                                           skip_group_check=True)
                        pv.inc(mm)

                    for t in range(LASTSLOT):
                        q = t - STEPS - 2
                        if t < NQ:
                            for n in range(NT * t, NT * t + NT):
                                scores(n)
                        if t == HPG - 1:
                            project(Y_K[1], wk, x_c, 1)
                            project_values(1)
                        if 0 <= q < NQ:
                            for n in range(NT * q, NT * q + NT):
                                turn(n)
                            if q:
                                values(q - 1)
                    values(NQ - 1)
                    oev.wait(pe, b, GX)
                    for k in range(KC):
                        G.claim(pe, b, Y_OUT + k)
                        for g in range(GX):
                            mm = pe.matmul(G.bank(Y_OUT + k), wo[:, g, k * P:(k + 1) * P], x_o[:, g, :],
                                           start=(g == 0), stop=(g == GX - 1))
                        G.filled(mm, Y_OUT + k)

            def evac_turned(eng, copy, b, n):
                q, j = n // NT, n % NT
                tn.wait(eng, b, n + 1)
                if q >= 2:
                    pv.wait(eng, b, q - 1)
                pte[n % 2].inc(copy(x_pt[:, q % 2, :, j * P:(j + 1) * P],
                                    ps[:, PT_BANK + n % 2, :].rearrange("p (k c) -> p k c", c=P)))

            def on_act(act):
                with act.Fori(0, B) as b:
                    norm.on_act(act, b)
                    for t in range(LASTSLOT):
                        if t < NQ:
                            for n in range(NT * t, NT * t + NT):
                                sf.wait(act, b, n + 1)
                                if n >= NT * DEPTH:
                                    tn.wait(act, b, n - NT * DEPTH + 1)
                                sev.inc(act.copy(xb(n), ps[:, n % S_BANKS, :]))
                        q = t - STEPS - 2
                        turned = [n for n in range(NT * q, NT * q + NT) if n % 2 == 0] if 0 <= q < NQ else []
                        for s in active(t):
                            if s == t - 1:
                                st.wait(act, b, 11 * t)
                            if s == active(t)[0] and t > 1:
                                up.wait(act, b, 4 * (t - 1))
                            for n in range(NT * s, NT * s + NT):
                                if fs.n >= 2:
                                    fs.wait(act, b, fs.n - 1)
                                fs.inc(act.activation(x_xc[:, fs.n % 2, :], xb(n), ACT.Relu, scale=-1.0, bias=U_[:, n:n + 1],
                                                      accum_out=F_[:, n:n + 1]))
                            if turned:
                                evac_turned(act, act.copy, b, turned.pop(0))
                        for n in turned:
                            evac_turned(act, act.copy, b, n)
                        q = t - STEPS - 1
                        if 0 <= q < NQ:
                            up.wait(act, b, 4 * (t - 1))
                            for n in range(NT * q, NT * q + NT):
                                pr.inc(act.activation(xb(n), xb(n), ACT.Relu, scale=-1.0, bias=U_[:, n:n + 1],
                                                      accum_out=M_[:, n:n + 1]))

            def on_pool(pool):
                with pool.Fori(0, B) as b:
                    def keys(q):
                        if q % HPG == 0:
                            kr.wait(pool, b, q // HPG + 1)
                        if q >= 4:
                            sf.wait(pool, b, NT * (q - 3))
                        settle(pool)
                        kz.inc(pool.tensor_scalar(x_kz[:, q % 4, :], x_k[:, q // HPG, :], const("heads")[:, q % HPG:q % HPG + 1],
                                                  1.0, ALU.mult, ALU.mult))
                    for q in range(NQ):
                        keys(q)

            def on_dve(dve, before, count):
                dve.wait_ge(before, count)
                dve.memset(x_vz[:], 0.0).then_inc(go, 1)
                dve.memset(x_bad[:], 0.0).then_inc(bad0, 1)
                with dve.Fori(0, B) as b:
                    dve.wait_ge(go, b * KC + 1)
                    norm.on_dve(dve, b)
                    for g in range(GX):
                        G.wait(dve, b, Y_Q + g)
                        qr.link(dve, b, dve.tensor_scalar(x_q[:, g, :], G.bank(Y_Q + g), bq[:, g:g + 1], -SCX, ALU.add, ALU.mult))
                        dve.sem_inc(G.free[g % 2], 1)

                    def keys(g):
                        G.wait(dve, b, Y_K[g])
                        kr.link(dve, b, dve.tensor_scalar(x_k[:, g, :], G.bank(Y_K[g]), bk[:, g:g + 1], None, ALU.add))
                        dve.sem_inc(G.free[Y_K[g] % 2], 1)

                    def vals(g):
                        G.wait(dve, b, Y_V[g])
                        for i in range(NT):
                            o = x_vz[:, i, :].rearrange("p (h c) -> p h c", h=HPG)[:, :, 0:HDX]
                            vr.inc(dve.tensor_tensor(o, G.bank(Y_V[g])[:, i * P:(i + 1) * P].rearrange("p (h c) -> p h c", h=HPG),
                                                     bv[:, g * P:(g + 1) * P].rearrange("p (h c) -> p h c", h=HPG), ALU.add))
                        vr.wait(dve, b, vr.n)
                        dve.sem_inc(G.free[Y_V[g] % 2], 1)
                        dve.sem_inc(cused.sem, 1)

                    def outputs(g):
                        pv.wait(dve, b, HPG * (g + 1))
                        oev.inc(dve.tensor_copy(x_o[:, g, :], ps[:, O_BANK, :]))

                    def start(q):
                        lk = lambda ins: st.link(dve, b, ins)
                        v = slice(NT * q, NT * q + NT)
                        wide = lambda a: a.unsqueeze(2).broadcast_to([P, NT, GROUPS])
                        y = x_gm[:, :, 0:GROUPS]
                        sev.wait(dve, b, NT * (q + 1))
                        lk(dve.tensor_reduce(y, x_ring[:, q % DEPTH].rearrange("p t (a g) -> p t g a", g=GROUPS), AX.X, ALU.min))
                        lk(dve.tensor_reduce(F_[:, v], y, AX.X, ALU.add))
                        lk(dve.tensor_scalar(U_[:, v], F_[:, v], START, 1.0 / GROUPS, ALU.add, ALU.mult))
                        for it in range(1):
                            lk(dve.tensor_tensor(x_gd[:, 0], y, wide(U_[:, v]), ALU.subtract))
                            st.inc(dve.tensor_scalar(x_gd[:, 1], x_gd[:, 0], 0.0, None, ALU.is_lt))
                            lk(dve.tensor_scalar(x_gd[:, 0], x_gd[:, 0], 0.0, None, ALU.min))
                            lk(dve.tensor_reduce(x_sf[:, 0, :, :], x_gd[:], AX.X, ALU.add))
                            lk(dve.tensor_scalar(x_sf[:, 1, 1, :], x_sf[:, 0, 1, :], 1.0, None, ALU.max))
                            lk(dve.reciprocal(x_sf[:, 1, 1, :], x_sf[:, 1, 1, :]))
                            lk(dve.scalar_tensor_tensor(x_sf[:, 1, 0, :], x_sf[:, 0, 0, :], START, x_sf[:, 1, 1, :], ALU.add, ALU.mult))
                            lk(dve.tensor_tensor(U_[:, v], U_[:, v], x_sf[:, 1, 0, :], ALU.add))

                    keys(0)
                    vals(0)
                    for t in range(LASTSLOT):
                        q = t - STEPS - 2
                        turned = [n for n in range(NT * q, NT * q + NT) if n % 2 == 1] if 0 <= q < NQ else []
                        for s in active(t):
                            for n in range(NT * s, NT * s + NT):
                                if cn.n >= 2:
                                    cn.wait(dve, b, cn.n - 1)
                                cn.inc(dve.tensor_scalar(x_r[:, cn.n % 2, :], xb(n), U_[:, n:n + 1], None,
                                                         ALU.is_lt, ALU.add, accum_out=C_[:, n:n + 1]))
                            if turned:
                                evac_turned(dve, dve.tensor_copy, b, turned.pop(0))
                        for n in turned:
                            evac_turned(dve, dve.tensor_copy, b, n)
                        if q == HPG:
                            outputs(0)
                            vals(1)
                        if t < NQ:
                            start(t)
                        if t == HPG - 1:
                            keys(1)
                        if len(active(t)):
                            lk = lambda ins: up.link(dve, b, ins)
                            v = slice(NT * active(t)[0], NT * active(t)[-1] + NT)
                            cn.wait(dve, b, cn.n)
                            lk(dve.tensor_scalar(C_[:, v], C_[:, v], 1.0, None, ALU.max))
                            lk(dve.reciprocal(C_[:, v], C_[:, v]))
                            fs.wait(dve, b, steps_before(t + 1))
                            lk(dve.scalar_tensor_tensor(F_[:, v], F_[:, v], -1.0, C_[:, v], ALU.add, ALU.mult))
                            lk(dve.tensor_tensor(U_[:, v], U_[:, v], F_[:, v], ALU.subtract))
                    outputs(1)
                    pr.wait(dve, b, NX)
                    bad.link(dve, b, dve.tensor_scalar(M_[:], M_[:], -1.0, None, ALU.add))
                    bad.link(dve, b, dve.scalar_tensor_tensor(F_[:], M_[:], -1.0, M_[:], ALU.mult, ALU.max))
                    bad.link(dve, b, dve.tensor_reduce(x_bad[:, 1:2], F_[:], AX.X, ALU.max))
                    bad.link(dve, b, dve.tensor_tensor(x_bad[:, 0:1], x_bad[:, 0:1], x_bad[:, 1:2], ALU.max))
                    for k in range(KC):
                        G.wait(dve, b, Y_OUT + k)
                        if k == 0:
                            dve.wait_ge(kept, 16)
                        xk = xT[:, k, chunk(b)]
                        dve.scalar_tensor_tensor(xk, G.bank(Y_OUT + k), bo[:, k:k + 1], xk, ALU.add, ALU.add).then_inc(go, 1)
                    dve.wait_ge(go, b * KC + 1 + KC)
                    for k in range(KC):
                        dve.sem_inc(G.free[(Y_OUT + k) % 2], 1)
                dve.wait_ge(flag_t, 1)
                dve.tensor_reduce(x_flag[:, 0:1], ps[0:1, 0, 0:P], AX.X, ALU.max).then_inc(flag, 1)
                dve.wait_ge(flag, 1)
                dve.tensor_scalar(x_flag[:, 1:2], x_flag[:, 0:1], MASS_TOL, None, ALU.is_gt).then_inc(flag, 1)
                dve.wait_ge(flag, 2)
                dve.tensor_copy(x_flagi[:], x_flag[:, 1:2]).then_inc(flag, 1)

            return on_pe, on_act, on_pool, on_dve, go, cld, cused

        kept = sem("kept")
        restored = sem("restored")
        flag_t = sem("flag_turned")
        flag = sem("flag")
        bad0 = sem("bad_zero")
        cross0 = cross(0)
        quick = sparse_quick()
        general = cross(1)

        def stage5_general(eng, step):
            eng.wait_ge(flag, 3)
            wrong = eng.value_load(x_flagi[0:1, 0:1], min_val=0, max_val=1)
            with eng.If(wrong > 0):
                step()

        END1 = 1 + A_GO * B
        ENDX = 1 + KC * B

        def context(sp, stage):
            cld, cused = stage[5], stage[6]
            c = a["ctx"]
            sp.dma_start(x_c[:], c[:, :, 0:S]).then_inc(cld, 16)
            with sp.Fori(1, B) as b:
                cused.wait(sp, b - 1, GX)
                sp.dma_start(x_c[:], c[:, :, chunk(b)]).then_inc(cld, 16)

        chain = [(1, a_go, END1), (2, cross0[4], ENDX), (3, e_acc, END3), (4, n_go, ENDX), (5, quick[4], ENDX), (6, f_go, ENDX)]

        def before(k):
            return chain[k - 2][1:]

        loaded = {"x": 1, "small": 3, "aw": 4, "xw0": 4, "xw1": 4, "w1": 2, "wt1": 2}

        @blk.sync
        def _(sp):
            sp.dma_start(xT[:], a["x"]).then_inc(loads["x"], 16)
            sp.dma_start(cols[:], a["cols"]).then_inc(loads["small"], 16)
            sp.dma_start(cst[:], a["consts"]).then_inc(loads["small"], 16)
            sp.dma_start(rows[:], a["rows"].broadcast_to([P, NROWS])).then_inc(loads["small"], 16)
            for n, w in zip("qkvo", aw):
                sp.dma_start(w[:], a[f"w0{n}"]).then_inc(loads["aw"], 16)
            for l in range(2):
                for n, w in zip("qkvo", xw[l]):
                    sp.dma_start(w[:], a[f"wx{l}{n}"]).then_inc(loads[f"xw{l}"], 16)
            sp.dma_start(wq1[:], a["w1q"]).then_inc(loads["w1"], 16)
            sp.dma_start(wkv1[:], a["w1kv"]).then_inc(loads["w1"], 16)
            sp.dma_start(wt1[:], a["wt1"]).then_inc(loads["wt1"], 16)
            sp.dma_start(bt1[:], a["bt1"]).then_inc(loads["wt1"], 16)
            sp.wait_ge(*before(2))
            context(sp, cross0)
            sp.wait_ge(*before(3))
            stage3_loads(sp)
            sp.wait_ge(*before(5))
            sp.dma_start(a["kept"], xT[:]).then_inc(kept, 16)
            context(sp, quick)

            def again():
                sp.dma_start(xT[:], a["kept"]).then_inc(restored, 16)
                context(sp, general)
            stage5_general(sp, again)
            sp.wait_ge(*chain[-1][1:])
            for name, n in loaded.items():
                sp.wait_ge(loads[name], 16 * n)
            sp.dma_start(a["out"], xT[:]).then_inc(stored, 16)
            sp.wait_ge(stored, 16)

        @blk.gpsimd
        def _(pool):
            pool.memset(meanw[:], 1.0 / D).then_inc(init_pool, 1)
            pool.memset(a_kz[:], 0.0).then_inc(init_pool, 1)
            pool.memset(a_vg[:], 0.0).then_inc(init_pool, 1)
            stage1_pool(pool)
            cross0[2](pool)
            stage3_pool(pool)
            stage4_pool(pool)
            quick[2](pool)
            stage5_general(pool, lambda: general[2](pool))

        @blk.scalar
        def _(act):
            stage1_act(act)
            cross0[1](act)
            stage3_act(act)
            stage4_act(act)
            quick[1](act)
            stage5_general(act, lambda: general[1](act))
            stage6_act(act)

        @blk.vector
        def _(dve):
            dve.memset(eps[:, 0:1], EPS_LN).then_inc(init_dve, 1)
            dve.memset(eps[:, 1:2], EPS_RMS).then_inc(init_dve, 1)
            stage1_dve(dve)
            cross0[3](dve, *before(2))
            stage3_dve(dve, *before(3))
            stage4_dve(dve, *before(4))
            quick[3](dve, *before(5))
            stage5_general(dve, lambda: general[3](dve, restored, 16))
            stage6_dve(dve, *before(6))

        @blk.tensor
        def _(pe):
            stage1_pe(pe)
            cross0[0](pe)
            stage3_pe(pe)
            stage4_pe(pe)
            quick[0](pe)
            pe.wait_ge(quick[4], ENDX)
            pe.transpose(ps[0:1, 0, 0:P], x_bad[:, 0:1], ident).then_inc(flag_t, 1)
            stage5_general(pe, lambda: general[0](pe))
            stage6_pe(pe)


def kernel(**inputs):
    import concourse.bacc as bacc
    from concourse.bass_utils import run_bass_kernel_spmd

    i = {k: np.asarray(v) for k, v in inputs.items()}

    def halves(w):
        return np.ascontiguousarray(w.reshape(KC, P, -1).transpose(1, 0, 2))

    def tokens(x):
        return halves(np.ascontiguousarray(x.transpose(2, 0, 1)).reshape(D, TOK))

    arrays = {
        "x": tokens(i["x"]),
        "w0q": halves(i["L0_attn_w_q"]), "w0k": halves(i["L0_attn_w_k"]), "w0v": halves(i["L0_attn_w_v"]),
        "w0o": np.ascontiguousarray(i["L0_attn_w_out"].reshape(PAIRS, P, D).transpose(1, 0, 2)),
        "consts": constants(),
        "ctx": tokens(i["ctx_1024"]),
    }
    vec = {"norm_w": "L0_attn_norm_w", "scorer_w": "L0_attn_scorer_w", "bq0": "L0_xattn_bq", "bk0": "L0_xattn_bk",
           "bo0": "L0_xattn_bo", "bq1": "L1_xattn_bq", "bk1": "L1_xattn_bk", "bo1": "L1_xattn_bo"}
    parts = [halves(i[n].reshape(D, 1)).reshape(P, KC) for n in vec.values()]
    parts += [halves(i["L1_ffn_tile_sigs"].T).reshape(P, -1), halves(i["L0_ffn_gate_w"].T).reshape(P, -1)]
    arrays["cols"] = np.concatenate(parts, axis=1)
    arrays["rows"] = np.concatenate([i[n].reshape(-1) for n in (
        "L0_xattn_bv", "L0_attn_scorer_b", "L0_ffn_expert_bias", "L1_attn_bq", "L1_attn_bk", "L1_attn_bv",
        "L1_attn_k_gamma", "L1_attn_v_gamma", "L1_attn_k_beta", "L1_attn_v_beta", "L1_xattn_bv")])[None]
    for n in "qkvo":
        arrays[f"wx0{n}"] = halves(i[f"L0_xattn_W{n}"].T)
        arrays[f"wx1{n}"] = halves(i[f"L1_xattn_W{n}"])
    arrays["w1q"] = halves(i["L1_attn_Wq"].T)
    arrays["w1kv"] = halves(np.concatenate([i["L1_attn_Wk"], i["L1_attn_Wv"]]).T)
    arrays["wt1"] = np.ascontiguousarray(i["L1_ffn_W"].reshape(T1, KC, P, D).transpose(2, 0, 1, 3))
    arrays["bt1"] = i["L1_ffn_b"]
    for n, routed in (("gate", "L0_ffn_w_gate"), ("up", "L0_ffn_w_up"), ("down", "L0_ffn_w_down")):
        w = np.concatenate([i[routed], i[f"L0_ffn_shared_{n}_w"][None]]).transpose(0, 2, 1)
        arrays["e" + n[0]] = np.ascontiguousarray(w.reshape(E + 1, KC, P, -1).transpose(2, 0, 1, 3))
    nc = bacc.Bacc("TRN2", target_bir_lowering=False, num_devices=1)
    args = {n: nc.dram_tensor(f"in_{n}", v.shape, F32, kind="ExternalInput").ap() for n, v in arrays.items()}
    args["kept"] = nc.dram_tensor("kept_x", (P, KC, TOK), F32, kind="Internal").ap()
    args["comb"] = nc.dram_tensor("combine", (E + 1, TOK), F32, kind="Internal").ap()
    args["out"] = nc.dram_tensor("out_x", (P, KC, TOK), F32, kind="ExternalOutput").ap()
    program(nc, args)
    r = run_bass_kernel_spmd(nc, [{f"in_{n}": v for n, v in arrays.items()}], core_ids=[0])
    y = r.results[0]["out_x"]
    return np.ascontiguousarray(y.transpose(1, 0, 2).reshape(D, B, S).transpose(1, 2, 0))
```

```python
from contextlib import ExitStack

import numpy as np

import concourse.bass as bass
from concourse import mybir

P = 128
B, S, D = 4, 512, 256
KC = D // P
TOK = B * S
NT = S // P

H0, HD0, WIN, G0 = 16, 64, 256, 64
PAIRS = H0 // 2
INNER = H0 * HD0
NWIN = S // WIN
LG = G0 + WIN

HX, HDX = 16, 16
GX = 2
HPG = P // HDX
E, TOPK, I = 16, 8, 256
ROUTE_SCALE = 2.826
H1, K1 = 16, 64
KV1 = K1 + D
T1 = 8
NEG = -1.0e30
BIG = 3.0e38
EPS_LN, EPS_RMS = 1e-5, 1e-6
NEWTON = 24

F32 = mybir.dt.float32
BF16 = mybir.dt.bfloat16
ALU = mybir.AluOpType
ACT = mybir.ActivationFunctionType
AX = mybir.AxisListType

def offsets(parts):
    at, n = {}, 0
    for name, width in parts:
        at[name] = (n, n + width)
        n += width
    return at, n

COLS, NCOLS = offsets([("norm_w", KC), ("scorer_w", KC), ("bq0", KC), ("bk0", KC), ("bo0", KC),
                       ("bq1", KC), ("bk1", KC), ("bo1", KC), ("sigs", KC * T1), ("gate_w", KC * E)])
ROWS, NROWS = offsets([("bv0", D), ("scorer_b", 1), ("expert_bias", E), ("bq", INNER), ("bkv", KV1),
                       ("gkv", KV1), ("betakv", KV1), ("bv1", D)])
CONSTS, NCONSTS = offsets([("ident", P), ("tri", S), ("earlier", 896), ("slots", P), ("pos", NT), ("heads", HPG),
                           ("before", E * E), ("first", T1), ("scal", B)])


def constants():
    c = np.zeros((P, NCONSTS), np.float32)
    p = np.arange(P)[:, None]

    def put(name, v):
        a, b = CONSTS[name]
        c[:, a:b] = v

    put("ident", np.eye(P))
    put("tri", np.where(np.arange(S)[None] - (S - P) <= p, 0.0, NEG))
    put("earlier", (np.arange(896)[None] - (S - P) < p))
    put("slots", np.arange(P)[None] % G0)
    put("pos", np.arange(NT)[None] * P + p)
    put("heads", p // HDX == np.arange(HPG)[None])
    e, f = np.arange(E)[:, None], np.arange(E)[None]
    put("before", (f < e).reshape(1, -1))
    put("first", T1 - np.arange(T1)[None])
    put("scal", 1.0 / (np.sqrt(np.arange(1, B + 1))[None] * H1))
    return c


def program(nc, a):
    with ExitStack() as ctx:
        def sb(name, shape, dt=F32, c=ctx):
            return c.enter_context(nc.sbuf_tensor(name, shape, dt))

        sems, raised = {}, {}

        def sem(name):
            if name not in sems:
                sems[name] = ctx.enter_context(nc.semaphore(name))
            return sems[name]

        def shared(name, total):
            base = raised.get(name, 0)
            raised[name] = base + total
            return sem(name), base

        xT = sb("xT", [P, KC, TOK])
        rows = sb("rows", [P, NROWS])
        cols = sb("cols", [P, NCOLS])
        cst = sb("cst", [P, NCONSTS])
        meanw = sb("meanw", [P, P])
        eps = sb("eps", [P, 2])
        xw = [[sb(f"xw{l}_{n}", [P, KC, D]) for n in "qkvo"] for l in range(2)]
        wq1 = sb("wq1", [P, KC, INNER])
        wkv1 = sb("wkv1", [P, KC, KV1])
        wt1 = sb("wt1", [P, T1, KC, D])
        bt1 = sb("bt1", [T1, D])

        def col(name):
            lo, hi = COLS[name]
            return cols[:, lo:hi]

        def row(name):
            lo, hi = ROWS[name]
            return rows[:, lo:hi]

        def const(name):
            lo, hi = CONSTS[name]
            return cst[:, lo:hi]

        ident = const("ident")
        ps = ctx.enter_context(nc.psum_tensor("ps", [P, 8, 512], F32))
        S_BANKS, PT_BANK, O_BANK, G_BANK = 3, 3, 5, 6

        with ExitStack() as st:
            aw = [sb(f"aw_{n}", [P, KC, INNER], c=st) for n in "qkv"] + [sb("aw_o", [P, PAIRS, D], c=st)]
            a_h = sb("a_h", [P, KC, S], c=st)
            a_xc = sb("a_xc", [P, KC, S], c=st)
            a_sq = sb("a_sq", [P, KC, S], c=st)
            a_r = sb("a_r", [P, 2, S], c=st)
            a_q = sb("a_q", [P, 2, S], c=st)
            a_kz = sb("a_kz", [P, 2, 2, NWIN, LG], c=st)
            a_v = sb("a_v", [P, 2, NT, P], c=st)
            a_vg = sb("a_vg", [P, 2, P], c=st)
            a_scw = sb("a_scw", [P, KC, P], c=st)
            a_tokid = sb("a_tokid", [P, NT, P], c=st)
            a_sc = sb("a_sc", [P, S], c=st)
            a_junk = sb("a_junk", [P, S], c=st)
            a_col = sb("a_col", [P, 4, NT], c=st)
            a_sel = sb("a_sel", [P, NT, P], c=st)
            a_hg = sb("a_hg", [P, KC, P], c=st)
            a_mask = sb("a_mask", [P, NT, 2, LG], c=st)
            a_s = sb("a_s", [P, 3, LG], c=st)
            a_p = sb("a_p", [P, 3, 2 * LG], c=st)
            a_mn = sb("a_mn", [P, 64], c=st)
            a_den = sb("a_den", [P, 64], c=st)
            a_rd = sb("a_rd", [P, 64], c=st)
            a_pt = sb("a_pt", [P, 2, 5, WIN], c=st)
            a_o = sb("a_o", [P, PAIRS, S], c=st)

        with ExitStack() as st:
            x_h = sb("x_h", [P, KC, S], c=st)
            x_xc = sb("x_xc", [P, KC, S], c=st)
            x_sq = sb("x_sq", [P, KC, S], c=st)
            x_o = x_sq
            x_r = sb("x_r", [P, 2, S], c=st)
            x_c = sb("x_c", [P, KC, S], c=st)
            x_q = sb("x_q", [P, GX, S], c=st)
            x_k = sb("x_k", [P, GX, S], c=st)
            x_kz = sb("x_kz", [P, HPG // 2, S], c=st)
            x_vz = sb("x_vz", [P, NT, HPG * (P + HDX)], c=st)
            x_pt = sb("x_pt", [P, NT, S], c=st)
            x_ring = sb("x_ring", [P, 8, NT, S], c=st)
            x_s = x_ring[:, 0:4].rearrange("p (a b) t s -> p a b t s", a=2)
            x_ja, x_jd = x_ring[:, 4], x_ring[:, 5]
            x_gm = x_h[:, 0, 0:256].rearrange("p (a w) -> p a w", w=64)
            x_gd = sb("x_gd", [P, 2, NT, 64], c=st)
            x_flagi = sb("x_flagi", [1, 1], mybir.dt.int32, c=st)
            x_st = sb("x_st", [P, 8, 64], c=st)
            x_sf = x_st[:, 4, 0:4 * NT].rearrange("p (a b i) -> p a b i", a=2, b=2)
            x_bad, x_bad1, x_flag = x_st[:, 5, 0:4 * NT], x_st[:, 5, 50:51], x_st[0:1, 5, 52:54]
            x_dev = x_st[:, 6, 0:8 * NT].rearrange("p (a i) -> p a i", a=2)
        with ExitStack() as st:
            m_hc, m_xc, m_sq, m_r = (sb("m_" + n, [P, KC, S], c=st) for n in ("hc", "xc", "sq", "r"))
            m_h = sb("m_h", [P, KC, TOK], c=st)
            m_w17 = sb("m_w17", [P, NT, E + 1], c=st)
            m_comb = sb("m_comb", [E + 1, TOK], c=st)
            m_sg, m_sel = (sb("m_" + n, [P, NT, E], c=st) for n in ("sg", "sel"))
            m_sum = sb("m_sum", [P, NT], c=st)
            m_gt, m_eq = (sb("m_" + n, [P, NT, E, E], c=st) for n in ("gt", "eq"))
            m_wg, m_wu, m_wd = (sb("m_" + n, [P, 2, KC, D], c=st) for n in ("wg", "wu", "wd"))
            m_cb = sb("m_cb", [P, 2, TOK], c=st)
            m_g, m_m = (sb("m_" + n, [P, 2, S], c=st) for n in ("g", "m"))
            m_a = sb("m_a", [P, 2, KC, S], c=st)
        with ExitStack() as st:
            n_h, n_xc, n_sq, n_r = (sb("n_" + n, [P, KC, S], c=st) for n in ("h", "xc", "sq", "r"))
            n_hist = sb("n_hist", [P, NT, B, KV1], c=st)
            n_kv = sb("n_kv", [P, NT, KV1], c=st)
            n_bs, n_ba = sb("n_bs", [P, NT, 2, 6], c=st), sb("n_ba", [P, NT, 2, 2], c=st)
            n_mv = sb("n_mv", [P, 2, NT, 2], c=st)
            n_q = sb("n_q", [P, 3, INNER], c=st)
            n_sm = sb("n_sm", [P, 3, NT, H1], c=st)
            n_qn = sb("n_qn", [P, 2, K1], c=st)
            n_jk, n_d = sb("n_jk", [P, B, K1], c=st), sb("n_d", [P, B], c=st)
            n_y = sb("n_y", [P, NT, D], c=st)
        with ExitStack() as st:
            f_h, f_xc, f_sq, f_r = (sb("f_" + n, [P, KC, S], c=st) for n in ("h", "xc", "sq", "r"))
            f_sg = sb("f_sg", [P, KC * T1], c=st)
            f_one = sb("f_one", [T1, T1 * P], BF16, c=st)
            f_oh, f_ohb = sb("f_oh", [T1, S], c=st), sb("f_ohb", [T1, S], BF16, c=st)
            f_c, f_mx = sb("f_c", [P, NT, T1], c=st), sb("f_mx", [P, 2, NT], c=st)
            f_m = sb("f_m", [P, 4, KC, S], c=st)

        loads = {n: sem(f"load_{n}") for n in ("x0", "x", "small", "aw", "xw0", "xw1", "w1", "wt1")}
        init_pool = sem("init_pool")
        init_dve = sem("init_dve")
        stored = sem("stored")

        class Gen:
            def __init__(self, tag, per, ahead=(0, 0)):
                self.full = [sem(f"{tag}_full{k}") for k in range(2)]
                self.free = [sem(f"{tag}_free{k}") for k in range(2)]
                self.half = per // 2
                before = shared(f"{tag}_full0", B * self.half + ahead[0])[1]
                self.base = [before + n for n in ahead]
                assert per % 2 == 0

            def bank(self, n):
                return ps[:, G_BANK + n % 2, :]

            def claim(self, pe, b, n):
                if n >= 2:
                    pe.wait_ge(self.free[n % 2], b * self.half + self.base[n % 2] + n // 2)

            def filled(self, ins, n):
                ins.then_inc(self.full[n % 2], 1)

            def wait(self, eng, b, n):
                eng.wait_ge(self.full[n % 2], b * self.half + self.base[n % 2] + n // 2 + 1)

            def read(self, ins, n):
                ins.then_inc(self.free[n % 2], 1)

        class Count:
            def __init__(self, name, per, ahead=0):
                self.per, self.n = per, 0
                self.sem, self.base = shared(name, B * per + ahead)

            def inc(self, ins):
                ins.then_inc(self.sem, 1)
                self.n += 1
                return self.n

            def wait(self, eng, b, n):
                eng.wait_ge(self.sem, b * self.per + self.base + n)

            def link(self, eng, b, ins):
                self.inc(ins)
                self.wait(eng, b, self.n)

            def close(self):
                assert self.n == self.per, (self.sem, self.n, self.per)

        blk = ctx.enter_context(nc.Block())

        carried = {}

        def settle(eng):
            if eng.engine not in carried:
                carried[eng.engine] = sem(f"carried{len(carried)}")
            eng.sem_inc(carried[eng.engine], 1)

        def chunk(b):
            return bass.ds(b * S, S)

        NU = PAIRS * NWIN * 2 * 2
        GA_TOK, GA_SC, GA_HG, GA_IDX, GA_PAIR = 0, 2, 3, 4, 5
        LATE = PAIRS
        NORM_UNIT = 8 * LATE + 2
        GA_MEAN = GA_PAIR + 4 * LATE
        GA_VAR, GA_RMS, GA_OUT = GA_MEAN + 1, GA_MEAN + 2, GA_PAIR + 4 * PAIRS + 3

        def pair_use(p):
            return GA_PAIR + 4 * p + (3 if p >= LATE else 0)
        GA = Gen("ga", GA_OUT + 2, ahead=(1, 2))
        a_go = sem("a_go")
        A_GO = 2
        a_ln = Count("a_ln", 10, ahead=10)
        a_lnact = Count("a_lnact", 4, ahead=4)
        a_hr = Count("a_h", KC)
        a_xn = Count("a_xn", 1)
        a_tok = Count("a_tok", 2)
        a_dv = Count("a_dv", 26)
        a_selr = Count("a_selr", 1)
        a_hgr = Count("a_hgr", 1)
        a_qr = Count("a_qr", PAIRS)
        a_vr = Count("a_vr", PAIRS)
        a_kr = Count("a_kr", 8 * PAIRS)
        a_sf = Count("a_sf", NU)
        a_ttr = Count("a_ttr", NU)
        a_exp = Count("a_exp", NU)
        a_rdn = Count("a_rdn", NU)
        a_scl = Count("a_scl", NU)
        a_t = Count("a_t", NU)
        a_pe = [Count("a_pteA", NU // 2), Count("a_pteD", NU // 2)]
        a_pv = Count("a_pv", PAIRS * NWIN)
        a_oev = Count("a_oev", PAIRS)

        def unit_a(n):
            p, r = divmod(n, 8)
            w, r = divmod(r, 4)
            j, h = divmod(r, 2)
            return p, w, j, h

        def a_span(j, h):
            w = G0 + P * (j + 1)
            return slice(0, w) if h else slice(LG - w, LG)

        def a_local(k, h):
            o = G0 + k * P if h else (1 - k) * P
            return slice(o, o + P)

        def a_global(h):
            return slice(0, G0) if h else slice(WIN, LG)

        def probs(n):
            h, sp = n % 2, a_span(n // 2 % 2, n % 2)
            return a_p[:, (n // 2) % 3, h * LG + sp.start:h * LG + sp.stop]

        LAG_E, LAG_T, LAG_PV = 1, 3, 4

        def behind(b):
            return chunk(0) if b is None else chunk((b + 1) % B)

        def of_behind(b, n):
            return (0, n) if b is None else (b, n + 4)

        def dve_behind(b, n):
            return (0, n) if b is None else (b, n + 10)

        def wait_norm_bank(eng, b, n):
            if b is None:
                eng.wait_ge(GA.full[n % 2], 2 if n == GA_RMS else 1)
            else:
                GA.wait(eng, b, n)

        def model_mean(pe, b, n, src):
            if b is not None:
                GA.claim(pe, b, n)
            elif n == GA_RMS:
                pe.wait_ge(GA.free[n % 2], 1)
            for k in range(KC):
                mm = pe.matmul(GA.bank(n), meanw[:], src(k), start=(k == 0), stop=(k == KC - 1))
            GA.filled(mm, n)

        def a_mean(pe, b):
            model_mean(pe, b, GA_MEAN, lambda k: xT[:, k, behind(b)])

        def a_variance(pe, b):
            a_lnact.wait(pe, *of_behind(b, 1))
            model_mean(pe, b, GA_VAR, lambda k: a_sq[:, k, :])

        def a_meansquare(pe, b):
            a_lnact.wait(pe, *of_behind(b, 3))
            model_mean(pe, b, GA_RMS, lambda k: a_sq[:, k, :])

        def a_square(act, b, n):
            a_ln.wait(act, *dve_behind(b, 1 if n == 1 else 6))
            a_lnact.inc(act.activation(a_sq[:], a_xc[:], ACT.Square))

        def a_root(act, b, n, bank, e):
            wait_norm_bank(act, b, bank)
            a_lnact.inc(act.activation(a_r[:, 0, :], GA.bank(bank), ACT.Sqrt, bias=eps[:, e:e + 1]))
            a_lnact.wait(act, *of_behind(b, n))
            act.sem_inc(GA.free[bank % 2], 1)

        def a_center(dve, b):
            wait_norm_bank(dve, b, GA_MEAN)
            m = GA.bank(GA_MEAN).unsqueeze(1).broadcast_to([P, KC, S])
            a_ln.inc(dve.tensor_tensor(a_xc[:], xT[:, :, behind(b)], m, ALU.subtract))
            a_ln.wait(dve, *dve_behind(b, 1))
            dve.sem_inc(GA.free[GA_MEAN % 2], 1)

        def a_invert(dve, b, n, i):
            a_lnact.wait(dve, *of_behind(b, n))
            c = slice(i * P, (i + 1) * P)
            a_ln.inc(dve.reciprocal(a_r[:, 1, c], a_r[:, 0, c]))

        def a_normalise(dve, b):
            a_ln.wait(dve, *dve_behind(b, 5))
            a_ln.inc(dve.tensor_tensor(a_xc[:], a_xc[:], a_r[:, 1, :].unsqueeze(1).broadcast_to([P, KC, S]), ALU.mult))

        def stage1_pe(pe):
            wq, wk, wv, wo = aw
            pe.wait_ge(loads["x0"], 16)
            pe.wait_ge(init_pool, 1)
            a_mean(pe, None)
            a_variance(pe, None)
            a_meansquare(pe, None)
            pe.wait_ge(loads["small"], 48)
            pe.wait_ge(init_pool, 3)
            pe.wait_ge(init_dve, 16)
            with pe.Fori(0, B) as b:
                pe.wait_ge(a_go, b * A_GO + 1)

                a_hr.wait(pe, b, KC)
                for k in range(KC):
                    GA.claim(pe, b, GA_TOK + k)
                    for i in range(NT):
                        mm = pe.transpose(GA.bank(GA_TOK + k)[:, i * P:(i + 1) * P], a_h[:, k, i * P:(i + 1) * P], ident)
                    GA.filled(mm, GA_TOK + k)
                GA.claim(pe, b, GA_SC)
                for k in range(KC):
                    mm = pe.matmul(GA.bank(GA_SC), a_scw[:, k, :], a_h[:, k, :], start=(k == 0), stop=(k == KC - 1))
                GA.filled(mm, GA_SC)
                a_selr.wait(pe, b, 1)
                a_tok.wait(pe, b, 2)
                GA.claim(pe, b, GA_HG)
                for k in range(KC):
                    for i in range(NT):
                        mm = pe.matmul(GA.bank(GA_HG)[:, k * P:(k + 1) * P], htok(i, k), a_sel[:, i, :],
                                       start=(i == 0), stop=(i == NT - 1))
                GA.filled(mm, GA_HG)
                GA.claim(pe, b, GA_IDX)
                for i in range(NT):
                    mm = pe.matmul(GA.bank(GA_IDX)[:, 0:G0], a_tokid[:, i, :], a_sel[:, i, 0:G0],
                                   start=(i == 0), stop=(i == NT - 1))
                GA.filled(mm, GA_IDX)
                pe.wait_ge(loads["aw"], 64)
                a_hgr.wait(pe, b, 1)

                def project(p):
                    g = pair_use(p)
                    sl = slice(p * P, (p + 1) * P)
                    for m, w in ((0, wq), (1, wk)):
                        GA.claim(pe, b, g + m)
                        for k in range(KC):
                            mm = pe.matmul(GA.bank(g + m), w[:, k, sl], a_h[:, k, :], start=(k == 0), stop=(k == KC - 1))
                        GA.filled(mm, g + m)
                    GA.claim(pe, b, g + 2)
                    for i in range(NT):
                        for k in range(KC):
                            mm = pe.matmul(GA.bank(g + 2)[:, i * P:(i + 1) * P], a_h[:, k, i * P:(i + 1) * P], wv[:, k, sl],
                                           start=(k == 0), stop=(k == KC - 1))
                    GA.filled(mm, g + 2)
                    GA.claim(pe, b, g + 3)
                    for k in range(KC):
                        pe.matmul(GA.bank(g + 3)[:, 0:P], wk[:, k, sl], a_hg[:, k, :], start=(k == 0), stop=(k == KC - 1))
                    for k in range(KC):
                        mm = pe.matmul(GA.bank(g + 3)[:, P:2 * P], a_hg[:, k, :], wv[:, k, sl], start=(k == 0), stop=(k == KC - 1))
                    GA.filled(mm, g + 3)

                def scores(n):
                    p, w, j, h = unit_a(n)
                    if n % 8 == 0:
                        a_qr.wait(pe, b, p + 1)
                        a_kr.wait(pe, b, 8 * (p + 1))
                    if n >= S_BANKS:
                        a_ttr.wait(pe, b, n - S_BANKS + 1)
                    sp = a_span(j, h)
                    t = (w * 2 + j) * P
                    a_sf.inc(pe.matmul(ps[:, n % S_BANKS, sp], a_q[:, p % 2, t:t + P], a_kz[:, p % 2, h, w, sp],
                                       start=True, stop=True))

                def turn(n):
                    p, w, j, h = unit_a(n)
                    a_scl.wait(pe, b, n + 1)
                    if n >= 2:
                        a_pe[h].wait(pe, b, n // 2)
                    pb = a_p[:, (n // 2) % 3]
                    for k in range(j + 1):
                        lo = a_local(k, h)
                        mm = pe.transpose(ps[:, PT_BANK + h, k * P:(k + 1) * P], pb[:, h * LG + lo.start:h * LG + lo.stop],
                                          ident)
                    if h == 1:
                        mm = pe.transpose(ps[:, PT_BANK + 1, (j + 1) * P:(j + 2) * P], pb[:, WIN:WIN + 2 * G0], ident)
                    a_t.inc(mm)

                def values(wi):
                    p, w = divmod(wi, NWIN)
                    for q in a_pe:
                        q.wait(pe, b, 2 * (wi + 1))
                    if w == 0:
                        a_vr.wait(pe, b, p + 1)
                        if p >= 1:
                            a_oev.wait(pe, b, p)
                    pt = a_pt[:, wi % 2]
                    o = ps[:, O_BANK, w * WIN:(w + 1) * WIN]
                    pe.matmul(o, a_vg[:, p % 2, :], pt[:, 4, :], start=True, stop=False, skip_group_check=True)
                    for h in range(2):
                        for k in range(2):
                            v = a_v[:, p % 2, w * 2 + k, h * HD0:(h + 1) * HD0]
                            mm = pe.matmul(ps[h * HD0:(h + 1) * HD0, O_BANK, w * WIN + k * P:(w + 1) * WIN], v,
                                           pt[:, 2 * h + k, k * P:WIN], start=False, stop=(h == 1 and k == 1),
                                           skip_group_check=True)
                    a_pv.inc(mm)

                project(0)
                for n in range(NU + LAG_PV + 1):
                    if n < NU:
                        scores(n)
                        if n % 8 == 5 and n // 8 + 1 < PAIRS:
                            project(n // 8 + 1)
                    if n == NORM_UNIT - 11:
                        pe.wait_ge(loads["x"], 16)
                        a_mean(pe, b)
                    if n == NORM_UNIT - 9:
                        a_variance(pe, b)
                    if n == NORM_UNIT - 4:
                        a_meansquare(pe, b)
                    if 0 <= n - LAG_T < NU:
                        turn(n - LAG_T)
                    m = n - LAG_PV - 1
                    if m >= 0 and m % 4 == 3:
                        values(m // 4)
                a_oev.wait(pe, b, PAIRS)
                for k in range(KC):
                    GA.claim(pe, b, GA_OUT + k)
                    for p in range(PAIRS):
                        mm = pe.matmul(GA.bank(GA_OUT + k), wo[:, p, k * P:(k + 1) * P], a_o[:, p, :],
                                       start=(p == 0), stop=(p == PAIRS - 1))
                    GA.filled(mm, GA_OUT + k)

        def htok(i, k):
            return a_htok[:, i, k * P:(k + 1) * P]

        def stage1_act(act):
            act.wait_ge(init_dve, 2)
            a_square(act, None, 1)
            a_root(act, None, 2, GA_VAR, 0)
            a_square(act, None, 3)
            a_root(act, None, 4, GA_RMS, 1)
            with act.Fori(0, B) as b:
                for k in range(KC):
                    GA.wait(act, b, GA_TOK + k)
                    i = act.copy(a_htok[:, :, k * P:(k + 1) * P], GA.bank(GA_TOK + k).rearrange("p (i c) -> p i c", i=NT))
                    a_tok.inc(i)
                    i_free(act, GA, b, GA_TOK + k, a_tok, k + 1)
                GA.wait(act, b, GA_HG)
                i = act.copy(a_hg[:].rearrange("p k c -> p (k c)"), GA.bank(GA_HG)[:, 0:KC * P])
                a_hgr.inc(i)
                i_free(act, GA, b, GA_HG, a_hgr, 1)

                def evac_qv(p):
                    g = pair_use(p)
                    GA.wait(act, b, g)
                    if p >= 2:
                        a_sf.wait(act, b, 8 * (p - 1))
                    a_qr.inc(act.copy(a_q[:, p % 2, :], GA.bank(g)))
                    i_free(act, GA, b, g, a_qr, p + 1)
                    GA.wait(act, b, g + 2)
                    if p >= 2:
                        a_pv.wait(act, b, NWIN * (p - 1))
                    a_vr.inc(act.copy(a_v[:, p % 2].rearrange("p i c -> p (i c)"), GA.bank(g + 2)))
                    i_free(act, GA, b, g + 2, a_vr, p + 1)

                def exps(n):
                    p, w, j, h = unit_a(n)
                    sp = a_span(j, h)
                    a_ttr.wait(act, b, n + 1)
                    if n >= 6:
                        a_t.wait(act, b, n - 4)
                    a_exp.inc(act.activation(probs(n), a_s[:, n % 3, sp], ACT.Exp, scale=-1.0,
                                             bias=a_mn[:, n:n + 1], accum_out=a_den[:, n:n + 1]))

                def evac_pt(n):
                    p, w, j, h = unit_a(n)
                    wi = n // 4
                    a_t.wait(act, b, n + 1)
                    if wi >= 2:
                        a_pv.wait(act, b, wi - 1)
                    a_pe[0].inc(act.copy(a_pt[:, wi % 2, 0:j + 1, j * P:(j + 1) * P],
                                         ps[:, PT_BANK, 0:(j + 1) * P].rearrange("p (k c) -> p k c", c=P)))

                evac_qv(0)
                for n in range(NU + LAG_T + 1):
                    if n == NORM_UNIT - 10:
                        a_square(act, b, 1)
                    if n == NORM_UNIT - 8:
                        a_root(act, b, 2, GA_VAR, 0)
                    if n == NORM_UNIT - 4:
                        a_square(act, b, 3)
                    if n == NORM_UNIT - 3:
                        a_root(act, b, 4, GA_RMS, 1)
                    if 0 <= n - LAG_E < NU:
                        exps(n - LAG_E)
                    if n < NU and n % 8 == 5 and n // 8 + 1 < PAIRS:
                        evac_qv(n // 8 + 1)
                    m = n - LAG_T
                    if 0 <= m < NU and m % 2 == 0:
                        evac_pt(m)

        def i_free(eng, G, b, g, count, n):
            count.wait(eng, b, n)
            eng.sem_inc(G.free[g % 2], 1)

        def stage1_pool(pool):
            with pool.Fori(0, B) as b:
                a_ln.wait(pool, b, 6)
                a_xn.inc(pool.tensor_tensor(xT[:, :, chunk(b)], xT[:, :, chunk(b)], a_xc[:], ALU.add))
                for n in range(NU):
                    p, w, j, h = unit_a(n)
                    a_rdn.wait(pool, b, n + 1)
                    settle(pool)
                    v = probs(n)
                    a_scl.inc(pool.tensor_scalar(v, v, a_rd[:, n:n + 1], 1.0, ALU.mult, ALU.mult))

        a_htok = a_o[:, 0:2, :].rearrange("p a (i c) -> p (a i) c", c=D)

        def stage1_dve(dve):
            a_center(dve, None)
            for i in range(NT):
                a_invert(dve, None, 2, i)
            a_normalise(dve, None)
            for i in range(NT):
                a_invert(dve, None, 4, i)
            tri = const("tri")
            dve.wait_ge(loads["small"], 48)
            for t in range(NT):
                for h in range(2):
                    for k in range(t % 2 + 1):
                        o = S - P * (t % 2 - k + 1)
                        dve.tensor_copy(a_mask[:, t, h, a_local(k, h)], tri[:, o:o + P]).then_inc(init_dve, 1)
            dve.tensor_copy(a_scw[:], col("scorer_w").unsqueeze(2).broadcast_to([P, KC, P])).then_inc(init_dve, 1)
            dve.tensor_copy(a_tokid[:], const("pos").unsqueeze(2).broadcast_to([P, NT, P])).then_inc(init_dve, 1)
            dve.wait_ge(init_dve, 16)
            dve.wait_ge(init_pool, 3)
            dve.tensor_copy(a_col[0:1, 0, 0:1], cols[0:1, 0:1]).then_inc(a_go, 1)
            with dve.Fori(0, B) as b:
                dve.wait_ge(a_go, b * A_GO + 1)
                a_ln.wait(dve, b, 10)
                for k in range(KC):
                    a_hr.inc(dve.scalar_tensor_tensor(a_h[:, k, :], a_xc[:, k, :], col("norm_w")[:, k:k + 1],
                                                      a_r[:, 1, :], ALU.mult, ALU.mult))
                ch = lambda ins: a_dv.link(dve, b, ins)
                GA.wait(dve, b, GA_SC)
                ch(dve.tensor_scalar(a_sc[:], GA.bank(GA_SC), row("scorer_b"), None, ALU.add))
                dve.sem_inc(GA.free[GA_SC % 2], 1)
                for i in range(NT):
                    ch(dve.tensor_tensor_reduce(a_junk[:, 0:P], a_sc[:, i * P:(i + 1) * P], ident, 1.0, 0.0,
                                                ALU.mult, ALU.add, a_col[:, 0, i:i + 1]))
                for i in range(NT):
                    ch(dve.tensor_scalar(a_junk[:], a_sc[:], a_col[:, 0, i:i + 1], None, ALU.is_gt, ALU.add,
                                         accum_out=a_col[:, 1, i:i + 1]))
                    o = S - P - i * P
                    ch(dve.scalar_tensor_tensor(a_junk[:], a_sc[:], a_col[:, 0, i:i + 1], const("earlier")[:, o:o + S],
                                                ALU.is_equal, ALU.mult, accum_out=a_col[:, 2, i:i + 1]))
                ch(dve.tensor_tensor(a_col[:, 3, :], a_col[:, 1, :], a_col[:, 2, :], ALU.add))
                for i in range(NT):
                    ch(dve.tensor_scalar(a_sel[:, i, :], const("slots"), a_col[:, 3, i:i + 1], None, ALU.is_equal))
                a_selr.inc(dve.tensor_copy(a_col[0:1, 0, 0:1], a_col[0:1, 0, 0:1]))
                GA.wait(dve, b, GA_IDX)
                for t in range(NT):
                    for h in range(2):
                        ch(dve.tensor_scalar(a_mask[:, t, h, a_global(h)], GA.bank(GA_IDX)[:, 0:G0],
                                             const("pos")[:, t:t + 1], NEG, ALU.is_gt, ALU.mult))
                dve.sem_inc(GA.free[GA_IDX % 2], 1)

                def evac_k(p):
                    g = pair_use(p)
                    GA.wait(dve, b, g + 1)
                    if p >= 2:
                        a_sf.wait(dve, b, 8 * (p - 1))
                    for h in range(2):
                        r = slice(h * HD0, (h + 1) * HD0)
                        kb = ps[r, G_BANK + (g + 1) % 2, :].rearrange("p (w k c) -> p w k c", w=NWIN, c=P)
                        for k in range(2):
                            a_kr.inc(dve.tensor_copy(a_kz[r, p % 2, h, :, a_local(k, h)], kb[:, :, k, :]))
                    a_kr.wait(dve, b, a_kr.n)
                    dve.sem_inc(GA.free[(g + 1) % 2], 1)
                    GA.wait(dve, b, g + 3)
                    if p >= 2:
                        a_pv.wait(dve, b, NWIN * (p - 1))
                    for h in range(2):
                        r = slice(h * HD0, (h + 1) * HD0)
                        gb = ps[r, G_BANK + (g + 3) % 2, :]
                        a_kr.inc(dve.tensor_copy(a_kz[r, p % 2, h, :, a_global(h)], gb[:, 0:G0].unsqueeze(1).broadcast_to([HD0, NWIN, G0])))
                        a_kr.inc(dve.tensor_copy(a_vg[r, p % 2, h * HD0:(h + 1) * HD0], gb[:, P + h * HD0:P + (h + 1) * HD0]))
                    a_kr.wait(dve, b, a_kr.n)
                    dve.sem_inc(GA.free[(g + 3) % 2], 1)

                def ttr(n):
                    p, w, j, h = unit_a(n)
                    sp = a_span(j, h)
                    a_sf.wait(dve, b, n + 1)
                    if n >= 3:
                        a_exp.wait(dve, b, n - 2)
                    settle(dve)
                    a_ttr.inc(dve.tensor_tensor_reduce(a_s[:, n % 3, sp], ps[:, n % S_BANKS, sp],
                                                       a_mask[:, w * 2 + j, h, sp], -HD0 ** -0.5, BIG, ALU.add, ALU.min,
                                                       a_mn[:, n:n + 1]))

                def recip(n):
                    a_exp.wait(dve, b, n + 1)
                    a_rdn.inc(dve.reciprocal(a_rd[:, n:n + 1], a_den[:, n:n + 1]))

                def evac_pt(n):
                    p, w, j, h = unit_a(n)
                    wi = n // 4
                    a_t.wait(dve, b, n + 1)
                    if wi >= 2:
                        a_pv.wait(dve, b, wi - 1)
                    v = ps[:, PT_BANK + 1, 0:(j + 2) * P].rearrange("p (k c) -> p k c", c=P)
                    step = 2 if j == 0 else 1
                    a_pe[1].inc(dve.tensor_copy(a_pt[:, wi % 2, 2:5:step, j * P:(j + 1) * P], v))

                def evac_o(p):
                    a_pv.wait(dve, b, NWIN * (p + 1))
                    a_oev.inc(dve.tensor_copy(a_o[:, p, :], ps[:, O_BANK, :]))

                evac_k(0)
                for n in range(NU + LAG_PV + 3):
                    if n == NORM_UNIT - 10:
                        a_xn.wait(dve, b, 1)
                        dve.wait_ge(loads["x"], 16)
                        a_center(dve, b)
                    if 0 <= n - (NORM_UNIT - 8) < NT:
                        a_invert(dve, b, 2, n - (NORM_UNIT - 8))
                    if n == NORM_UNIT - 5:
                        a_normalise(dve, b)
                    if 0 <= n - NORM_UNIT < NT:
                        a_invert(dve, b, 4, n - NORM_UNIT)
                    if n < NU:
                        ttr(n)
                    if 0 <= n - LAG_E < NU:
                        recip(n - LAG_E)
                    if n < NU and n % 8 == 5 and n // 8 + 1 < PAIRS:
                        evac_k(n // 8 + 1)
                    m = n - LAG_T
                    if 0 <= m < NU and m % 2 == 1:
                        evac_pt(m)
                    m = n - LAG_PV - 2
                    if m >= 0 and m % 8 == 7:
                        evac_o(m // 8)
                for k in range(KC):
                    GA.wait(dve, b, GA_OUT + k)
                    xk = xT[:, k, chunk(b)]
                    dve.tensor_tensor(xk, xk, GA.bank(GA_OUT + k), ALU.add).then_inc(a_go, 1)
                dve.wait_ge(a_go, b * A_GO + 3)
                for k in range(KC):
                    dve.sem_inc(GA.free[(GA_OUT + k) % 2], 1)
            for q in (a_hr, a_dv, a_selr, a_kr, a_ttr, a_rdn, a_pe[1], a_oev):
                q.close()

        def now(b):
            return 0 if b is None else b

        class Norm:
            def __init__(self, tag, G, use, h, xc, sq, r):
                self.G, self.use, self.h, self.xc, self.sq, self.r = G, use, h, xc, sq, r
                self.steps, self.act_steps = Count(tag + "ln", 2, ahead=2), Count(tag + "lnact", 2, ahead=2)
                self.made = Count(tag + "h", 1)

            def source(self, b):
                return chunk(0) if b is None else chunk((b + 1) % B)

            def claim(self, pe, b, k):
                if b is not None:
                    self.G.claim(pe, b, self.use + k)

            def wait_bank(self, eng, b, k):
                n = (self.use + k) % 2
                if b is None:
                    eng.wait_ge(self.G.full[n], self.G.base[n])
                else:
                    self.G.wait(eng, b, self.use + k)

            def mean(self, pe, b):
                self.claim(pe, b, 0)
                for k in range(KC):
                    mm = pe.matmul(self.G.bank(self.use), meanw[:], xT[:, k, self.source(b)], start=(k == 0), stop=(k == KC - 1))
                self.G.filled(mm, self.use)

            def center(self, dve, b):
                self.wait_bank(dve, b, 0)
                m = self.G.bank(self.use).unsqueeze(1).broadcast_to([P, KC, S])
                self.steps.link(dve, now(b), dve.tensor_tensor(self.xc[:], xT[:, :, self.source(b)], m, ALU.subtract))
                dve.sem_inc(self.G.free[self.use % 2], 1)

            def square(self, act, b):
                self.steps.wait(act, now(b), 1 if b is None else 3)
                self.act_steps.inc(act.activation(self.sq[:], self.xc[:], ACT.Square))

            def variance(self, pe, b):
                self.act_steps.wait(pe, now(b), 1 if b is None else 3)
                self.claim(pe, b, 1)
                for k in range(KC):
                    mm = pe.matmul(self.G.bank(self.use + 1), meanw[:], self.sq[:, k, :], start=(k == 0), stop=(k == KC - 1))
                self.G.filled(mm, self.use + 1)

            def root(self, act, b):
                self.wait_bank(act, b, 1)
                self.act_steps.inc(act.activation(self.r[:, 0, :], self.G.bank(self.use + 1), ACT.Sqrt, bias=eps[:, 0:1]))
                i_free(act, self.G, now(b), self.use + 1, self.act_steps, 2 if b is None else 4)

            def inverse(self, dve, b):
                self.act_steps.wait(dve, now(b), 2 if b is None else 4)
                self.steps.link(dve, now(b), dve.reciprocal(self.r[:, 0, :], self.r[:, 0, :]))

            def scale(self, dve, b):
                self.steps.wait(dve, b, 2)
                rs = self.r[:, 0, :].unsqueeze(1).broadcast_to([P, KC, S])
                self.made.inc(dve.tensor_tensor(self.h[:], self.xc[:], rs, ALU.mult))

            def ready(self, eng, b):
                self.made.wait(eng, b, 1)

            def first_pe(self, pe):
                self.mean(pe, None)
                self.variance(pe, None)

            def first_act(self, act):
                self.square(act, None)
                self.root(act, None)

            def first_dve(self, dve):
                self.center(dve, None)
                self.inverse(dve, None)

        SCX = HDX ** -0.5
        NG = HPG * NT
        NX = GX * NG
        NQ = GX * HPG

        def cross(l):
            sparse = l == 1
            T = "x_"
            wq, wk, wv, wo = xw[l]
            bq, bk, bo, bv = col(f"bq{l}"), col(f"bk{l}"), col(f"bo{l}"), row(f"bv{l}")
            X_GRP, X_NORM, X_OUT = 0, 3 * GX, 3 * GX + 2
            G = Gen(T + "g", X_OUT + KC, ahead=(1, 1))
            norm = Norm(T, G, X_NORM, x_h, x_xc, x_k, x_r)
            go, go0 = shared(T + "go", 1 + KC * B)
            cld, cld0 = shared(T + "ctx", 16 * B)
            cused = Count(T + "cused", GX)
            qr, kr, kz, vr = Count(T + "q", GX), Count(T + "k", GX), Count(T + "kz", GX * HPG), Count(T + "v", GX * NT)
            sf, ttr, ex, rdn, scl = (Count(T + n, NX) for n in ("s", "ttr", "exp", "rdn", "scl"))
            tn = Count(T + "t", NX)
            pte = [Count(T + "pteA", NX // 2), Count(T + "pteD", NX // 2)]
            pv, oev = Count(T + "pv", NQ), Count(T + "oev", GX)
            if sparse:
                sev = Count(T + "sev", NX)
                fs = Count(T + "f", NX * NEWTON)
                cn = Count(T + "cnt", NX * NEWTON)
                th = Count(T + "tau", NQ * (5 + 5 * NEWTON))
                pr = Count(T + "p", NX)

            def width(j):
                return S if sparse else P * (j + 1)

            LAG_E, LAG_T, LAG_PV = 1, 3, 4
            STRETCHES, LEN = (range(GX), NG) if sparse else ((0,), NX)
            QK_AT, V_AT, SWITCH_AT = NG - 10, NG - 2, NG + LAG_PV + 2

            def head_keys(hh):
                return x_kz[:, hh, :] if hh < 4 else x_ring[:, 6, hh - 4, :]

            def turned_probs(q):
                return x_ring[:, 7] if q % 2 else x_pt

            def xbuf(n):
                return x_s[:, n // 8 % 2, n // 4 % 2, n % 4, :]

            def probs(n):
                return xbuf(n) if sparse else x_ring[:, 2 + n // 4 % 2, n % 4, 0:width(n % NT)]

            def logits(n):
                return x_ring[:, n // 4 % 2, n % 4, 0:width(n % NT)]

            def f_steps(q, it):
                return 8 * NEWTON * (q // 2) + 8 * it + 4 * (q % 2 + 1)

            def th_steps(q, it):
                base = q // 2 * 2 * (5 + 5 * NEWTON) + 10
                return base if it == 0 else base + (2 * (it - 1) + q % 2 + 1) * 5

            def on_pe(pe):
                pe.wait_ge(go, go0 + 1)
                norm.first_pe(pe)
                with pe.Fori(0, B) as b:
                    pe.wait_ge(go, b * KC + go0 + 1)
                    norm.ready(pe, b)
                    pe.wait_ge(loads[f"xw{l}"], 64)

                    def project_qk(g):
                        u = X_GRP + 3 * g
                        sl = slice(g * P, (g + 1) * P)
                        for m, w, src in ((0, wq, x_h), (1, wk, x_c)):
                            if m == 1 and g == 0:
                                pe.wait_ge(cld, b * 16 + cld0 + 16)
                            G.claim(pe, b, u + m)
                            for k in range(KC):
                                mm = pe.matmul(G.bank(u + m), w[:, k, sl], src[:, k, :], start=(k == 0), stop=(k == KC - 1))
                            G.filled(mm, u + m)

                    def project_v(g):
                        u = X_GRP + 3 * g
                        sl = slice(g * P, (g + 1) * P)
                        G.claim(pe, b, u + 2)
                        for i in range(NT):
                            for k in range(KC):
                                mm = pe.matmul(G.bank(u + 2)[:, i * P:(i + 1) * P], x_c[:, k, i * P:(i + 1) * P], wv[:, k, sl],
                                               start=(k == 0), stop=(k == KC - 1))
                        G.filled(mm, u + 2)

                    def scores(n):
                        g, hh, j = n // NG, n // NT % HPG, n % NT
                        if hh == 0 and j == 0:
                            qr.wait(pe, b, g + 1)
                        if j == 0:
                            kz.wait(pe, b, n // NT + 1)
                        if n >= S_BANKS:
                            (sev if sparse else ttr).wait(pe, b, n - S_BANKS + 1)
                        W = width(j)
                        sf.inc(pe.matmul(ps[:, n % S_BANKS, 0:W], x_q[:, g, j * P:(j + 1) * P], head_keys(hh)[:, 0:W],
                                         start=True, stop=True))

                    def turn(n):
                        (pr if sparse else scl).wait(pe, b, n + 1)
                        if n >= 2:
                            pte[n % 2].wait(pe, b, n // 2)
                        for k in range(width(n % NT) // P):
                            mm = pe.transpose(ps[:, PT_BANK + n % 2, k * P:(k + 1) * P], probs(n)[:, k * P:(k + 1) * P], ident)
                        tn.inc(mm)

                    def values(q):
                        g, hh = divmod(q, HPG)
                        for c in pte:
                            c.wait(pe, b, 2 * (q + 1))
                        if hh == 0:
                            vr.wait(pe, b, NT * (g + 1))
                            if g:
                                oev.wait(pe, b, g)
                        for k in range(NT):
                            lo = 0 if sparse else k * P
                            mm = pe.matmul(ps[:, O_BANK, lo:S], x_vz[:, k, hh * P:(hh + 1) * P], turned_probs(q)[:, k, lo:S],
                                           start=(hh == 0 and k == 0), stop=(hh == HPG - 1 and k == NT - 1),
                                           skip_group_check=True)
                        pv.inc(mm)

                    for g in STRETCHES:
                        if g:
                            oev.wait(pe, b, g)
                        project_qk(g)
                        project_v(g)
                        N0 = g * NG
                        if not sparse:
                            for n in range(LEN + LAG_PV + 1):
                                if n == QK_AT:
                                    project_qk(1)
                                if n == V_AT:
                                    project_v(1)
                                if n == NG + 10:
                                    norm.mean(pe, b)
                                if n == NG + 20:
                                    norm.variance(pe, b)
                                if n < LEN:
                                    scores(N0 + n)
                                if 0 <= n - LAG_T < LEN:
                                    turn(N0 + n - LAG_T)
                                m = n - LAG_PV - 1
                                if m >= 0 and m % NT == NT - 1:
                                    values((N0 + m) // NT)
                        else:
                            for n0 in range(0, NG + 8, 8):
                                for n in range(n0, n0 + 8):
                                    if n < NG:
                                        scores(N0 + n)
                                for n in range(n0 - 8, n0):
                                    if n >= 0:
                                        turn(N0 + n)
                                        if n % NT == NT - 1:
                                            values((N0 + n) // NT)
                    if sparse:
                        norm.mean(pe, b)
                        norm.variance(pe, b)
                    oev.wait(pe, b, GX)
                    for k in range(KC):
                        G.claim(pe, b, X_OUT + k)
                        for g in range(GX):
                            mm = pe.matmul(G.bank(X_OUT + k), wo[:, g, k * P:(k + 1) * P], x_o[:, g, :],
                                           start=(g == 0), stop=(g == GX - 1))
                        G.filled(mm, X_OUT + k)

            def on_act(act):
                norm.first_act(act)
                with act.Fori(0, B) as b:
                    def evac_pt(n):
                        q = n // NT
                        tn.wait(act, b, n + 1)
                        if q >= 2:
                            pv.wait(act, b, q - 1)
                        W = width(n % NT)
                        j = n % NT
                        pte[0].inc(act.copy(turned_probs(q)[:, 0:W // P, j * P:(j + 1) * P],
                                            ps[:, PT_BANK, 0:W].rearrange("p (k c) -> p k c", c=P)))

                    def queries(g):
                        u = X_GRP + 3 * g
                        G.wait(act, b, u)
                        qr.inc(act.activation(x_q[:, g, :], G.bank(u), ACT.Identity, bias=bq[:, g:g + 1]))
                        i_free(act, G, b, u, qr, g + 1)

                    for g in STRETCHES:
                        queries(g)
                        N0 = g * NG
                        if not sparse:
                            for n in range(LEN + LAG_T + 1):
                                if n == QK_AT + 1:
                                    queries(1)
                                if n == NG + 13:
                                    kz.wait(act, b, GX * HPG)
                                    norm.square(act, b)
                                if n == NG + 22:
                                    norm.root(act, b)
                                m = N0 + n - LAG_E
                                if 0 <= n - LAG_E < LEN:
                                    ttr.wait(act, b, m + 1)
                                    if m >= 8:
                                        tn.wait(act, b, m - 7)
                                    ex.inc(act.activation(probs(m), logits(m), ACT.Exp, scale=-1.0,
                                                          bias=x_st[:, 0, m:m + 1], accum_out=x_st[:, 1, m:m + 1]))
                                m = n - LAG_T
                                if 0 <= m < LEN and m % 2 == 0:
                                    evac_pt(N0 + m)
                        else:
                            for n0 in range(0, NG + 8, 8):
                                quads = range((N0 + n0) // NT, (N0 + n0) // NT + 2)
                                if n0 < NG:
                                    for n in range(N0 + n0, N0 + n0 + 8):
                                        sf.wait(act, b, n + 1)
                                        if n >= 16:
                                            tn.wait(act, b, n - 15)
                                        sev.inc(act.activation(xbuf(n), ps[:, n % S_BANKS, :], ACT.Identity, scale=SCX,
                                                               accum_out=x_st[:, 0, n:n + 1]))
                                for it in range(NEWTON):
                                    if n0 < NG:
                                        for q in quads:
                                            th.wait(act, b, th_steps(q, it))
                                            for n in range(4 * q, 4 * q + 4):
                                                if fs.n >= 4:
                                                    fs.wait(act, b, fs.n - 3)
                                                fs.inc(act.activation(x_ja[:, n % 4, :], xbuf(n), ACT.Relu,
                                                                      bias=x_st[:, 1, n:n + 1], accum_out=x_st[:, 2, n:n + 1]))
                                    if n0 and it < 8 and it % 2 == 0:
                                        evac_pt(N0 + n0 - 8 + it)

                    if sparse:
                        kz.wait(act, b, GX * HPG)
                        norm.square(act, b)
                        norm.root(act, b)

            def on_pool(pool):
                with pool.Fori(0, B) as b:
                    def keys(q):
                        if q % HPG == 0:
                            kr.wait(pool, b, q // HPG + 1)
                        if q >= HPG:
                            sf.wait(pool, b, NT * (q - HPG + 1))
                        settle(pool)
                        kz.inc(pool.tensor_scalar(head_keys(q % HPG), x_k[:, q // HPG, :], const("heads")[:, q % HPG:q % HPG + 1],
                                                  1.0, ALU.mult, ALU.mult))

                    for q in range(NQ if sparse else 2):
                        keys(q)
                    if not sparse:
                        for n in range(NX):
                            rdn.wait(pool, b, n + 1)
                            settle(pool)
                            scl.inc(pool.tensor_scalar(probs(n), probs(n), x_st[:, 2, n:n + 1], 1.0, ALU.mult, ALU.mult))
                            if n % NT == 1 and n // NT + 2 < HPG:
                                keys(n // NT + 2)
                            if n > QK_AT + 2 and n % 2 == 1 and HPG + (n - QK_AT - 3) // 2 < NQ:
                                keys(HPG + (n - QK_AT - 3) // 2)

            def on_dve(dve, before, count):
                dve.wait_ge(before, count)
                dve.memset(x_vz[:], 0.0).then_inc(go, 1)
                norm.first_dve(dve)
                with dve.Fori(0, B) as b:
                    dve.wait_ge(go, b * KC + go0 + 1)
                    norm.scale(dve, b)

                    def evac_pt(n):
                        q = n // NT
                        tn.wait(dve, b, n + 1)
                        if q >= 2:
                            pv.wait(dve, b, q - 1)
                        W = width(n % NT)
                        j = n % NT
                        pte[1].inc(dve.tensor_copy(turned_probs(q)[:, 0:W // P, j * P:(j + 1) * P],
                                                   ps[:, PT_BANK + 1, 0:W].rearrange("p (k c) -> p k c", c=P)))

                    def keys(g):
                        u = X_GRP + 3 * g
                        G.wait(dve, b, u + 1)
                        kr.link(dve, b, dve.tensor_scalar(x_k[:, g, :], G.bank(u + 1), bk[:, g:g + 1], None, ALU.add))
                        dve.sem_inc(G.free[(u + 1) % 2], 1)

                    def vals(g):
                        u = X_GRP + 3 * g
                        G.wait(dve, b, u + 2)
                        for i in range(NT):
                            o = x_vz[:, i, :].rearrange("p (h c) -> p h c", h=HPG)[:, :, 0:HDX]
                            vr.inc(dve.tensor_tensor(o, G.bank(u + 2)[:, i * P:(i + 1) * P].rearrange("p (h c) -> p h c", h=HPG),
                                                     bv[:, g * P:(g + 1) * P].rearrange("p (h c) -> p h c", h=HPG), ALU.add))
                        vr.wait(dve, b, vr.n)
                        dve.sem_inc(G.free[(u + 2) % 2], 1)
                        dve.sem_inc(cused.sem, 1)

                    def outputs(g):
                        pv.wait(dve, b, HPG * (g + 1))
                        oev.inc(dve.tensor_copy(x_o[:, g, :], ps[:, O_BANK, :]))

                    for g in STRETCHES:
                        N0 = g * NG
                        keys(g)
                        vals(g)
                        if not sparse:
                            for n in range(LEN + LAG_T + 1):
                                if n == QK_AT + 2:
                                    keys(1)
                                if n == SWITCH_AT:
                                    outputs(0)
                                    vals(1)
                                if n == NG + 12:
                                    norm.center(dve, b)
                                if n == NG + 25:
                                    norm.inverse(dve, b)
                                if n < LEN:
                                    m = N0 + n
                                    sf.wait(dve, b, m + 1)
                                    if m >= 8:
                                        ex.wait(dve, b, m - 7)
                                    settle(dve)
                                    W = width(m % NT)
                                    ttr.inc(dve.tensor_tensor_reduce(logits(m), ps[:, m % S_BANKS, 0:W],
                                                                     const("tri")[:, S - W:S], -SCX, BIG, ALU.add, ALU.min,
                                                                     x_st[:, 0, m:m + 1]))
                                m = N0 + n - LAG_E
                                if 0 <= n - LAG_E < LEN:
                                    ex.wait(dve, b, m + 1)
                                    rdn.inc(dve.reciprocal(x_st[:, 2, m:m + 1], x_st[:, 1, m:m + 1]))
                                m = n - LAG_T
                                if 0 <= m < LEN and m % 2 == 1:
                                    evac_pt(N0 + m)
                        else:
                            for n0 in range(0, NG + 8, 8):
                                quads = range((N0 + n0) // NT, (N0 + n0) // NT + 2)
                                if n0 < NG:
                                    for q in quads:
                                        sev.wait(dve, b, 4 * (q + 1))
                                        v = slice(4 * q, 4 * q + 4)
                                        th.link(dve, b, dve.tensor_reduce(x_st[:, 7, v], x_s[:, n0 // 8 % 2, q % 2], AX.X, ALU.max))
                                        th.link(dve, b, dve.tensor_scalar(x_st[:, 7, v], x_st[:, 7, v], -1.0, None, ALU.add))
                                        th.link(dve, b, dve.tensor_scalar(x_st[:, 3, v], x_st[:, 0, v], -1.0, 1.0 / S, ALU.add, ALU.mult))
                                        th.link(dve, b, dve.tensor_tensor(x_st[:, 3, v], x_st[:, 3, v], x_st[:, 7, v], ALU.max))
                                        th.inc(dve.tensor_scalar(x_st[:, 1, v], x_st[:, 3, v], -1.0, None, ALU.mult))
                                for it in range(NEWTON):
                                    if n0 < NG:
                                        for q in quads:
                                            v = slice(4 * q, 4 * q + 4)
                                            for n in range(4 * q, 4 * q + 4):
                                                if cn.n >= 4:
                                                    cn.wait(dve, b, cn.n - 3)
                                                cn.inc(dve.tensor_scalar(x_jd[:, n % 4, :], xbuf(n), x_st[:, 3, n:n + 1], None,
                                                                         ALU.is_gt, ALU.add, accum_out=x_st[:, 4, n:n + 1]))
                                            cn.wait(dve, b, cn.n)
                                            th.link(dve, b, dve.tensor_scalar(x_st[:, 5, v], x_st[:, 4, v], 1.0, None, ALU.max))
                                            th.link(dve, b, dve.reciprocal(x_st[:, 5, v], x_st[:, 5, v]))
                                            fs.wait(dve, b, f_steps(q, it))
                                            th.link(dve, b, dve.scalar_tensor_tensor(x_st[:, 6, v], x_st[:, 2, v], -1.0, x_st[:, 5, v],
                                                                                     ALU.add, ALU.mult))
                                            th.inc(dve.tensor_tensor(x_st[:, 3, v], x_st[:, 3, v], x_st[:, 6, v], ALU.add))
                                            th.link(dve, b, dve.tensor_tensor(x_st[:, 1, v], x_st[:, 1, v], x_st[:, 6, v], ALU.subtract))
                                    if n0 and it < 8 and it % 2 == 1:
                                        evac_pt(N0 + n0 - 8 + it)
                                if n0 < NG:
                                    for n in range(N0 + n0, N0 + n0 + 8):
                                        pr.inc(dve.tensor_scalar(xbuf(n), xbuf(n), x_st[:, 3, n:n + 1], 0.0, ALU.subtract, ALU.max))
                        outputs(g if sparse else GX - 1)
                    if sparse:
                        norm.center(dve, b)
                        norm.inverse(dve, b)
                    for k in range(KC):
                        G.wait(dve, b, X_OUT + k)
                        xk = xT[:, k, chunk(b)]
                        dve.scalar_tensor_tensor(xk, G.bank(X_OUT + k), bo[:, k:k + 1], xk, ALU.add, ALU.add).then_inc(go, 1)
                    dve.wait_ge(go, b * KC + go0 + 1 + KC)
                    for k in range(KC):
                        dve.sem_inc(G.free[(X_OUT + k) % 2], 1)

            return on_pe, on_act, on_pool, on_dve, go, cld, cused

        EG_GATE, EG_NORM, EG_COMB = 0, 1, 3
        EG = Gen("mg", 4, ahead=(1, 1))
        e_norm = Norm("m_", EG, EG_NORM, m_hc, m_xc, m_sq, m_r)
        e_ones = sem("m_ones")
        e_go = sem("m_go")
        e_hcp = Count("m_hcp", 1)
        e_sig = Count("m_sig", 1)
        e_gate = Count("m_gate", 17)
        e_comb = sem("m_comb_out")
        e_wl = [sem(f"m_weights{k}") for k in range(2)]
        e_cbl = [sem(f"m_cb{k}") for k in range(2)]
        e_guf, e_silu, e_mul, e_act, e_dn, e_acc = (sem(f"m_{n}") for n in ("gu", "silu", "mul", "act", "down", "acc"))
        UE = 2 * B
        NE = E + 1
        DN_BANK = 4

        def at(eng, s, e, n):
            if not (isinstance(e, int) and e * UE + n <= 0):
                eng.wait_ge(s, e * UE + n)

        def experts(eng, step):
            step(0, 0, 0)
            with eng.Fori(0, E // 2) as i:
                step(i * 2 + 1, 1, i)
                step(i * 2 + 2, 0, i + 1)

        def stage3_pe(pe):
            pe.wait_ge(e_go, 1)
            e_norm.first_pe(pe)
            with pe.Fori(0, B) as b:
                pe.wait_ge(e_go, b + 1)
                e_norm.ready(pe, b)
                gw = col("gate_w").rearrange("p (k e) -> p k e", k=KC)
                for i in range(NT):
                    for k in range(KC):
                        mm = pe.matmul(EG.bank(EG_GATE)[:, i * E:(i + 1) * E], m_hc[:, k, i * P:(i + 1) * P], gw[:, k, :],
                                       start=(k == 0), stop=(k == KC - 1))
                EG.filled(mm, EG_GATE)
                e_norm.mean(pe, b)
                e_norm.variance(pe, b)
                e_gate.wait(pe, b, 17)
                EG.claim(pe, b, EG_COMB)
                for i in range(NT):
                    mm = pe.transpose(EG.bank(EG_COMB)[0:NE, i * P:(i + 1) * P], m_w17[:, i, :], ident)
                EG.filled(mm, EG_COMB)
            e_hcp.wait(pe, B - 1, 1)

            def down(e, buf, c):
                at(pe, e_act, e, 2 * c + 2)
                for m in range(KC):
                    at(pe, e_acc, e, 2 * c + m - 3)
                    for k in range(KC):
                        mm = pe.matmul(ps[:, DN_BANK + (2 * c + m) % 4, :], m_wd[:, buf, k, m * P:(m + 1) * P],
                                       m_a[:, c % 2, k, :], start=(k == 0), stop=(k == KC - 1))
                    mm.then_inc(e_dn, 1)

            def expert(e, buf, r):
                pe.wait_ge(e_wl[buf], r * 48 + 48)
                for c in range(B):
                    for h in range(2):
                        u = 2 * c + h
                        at(pe, e_mul, e, u - 1)
                        for m, w in ((0, m_wg), (1, m_wu)):
                            for k in range(KC):
                                mm = pe.matmul(ps[:, 2 * h + m, :], w[:, buf, k, h * P:(h + 1) * P],
                                               m_h[:, k, c * S:(c + 1) * S], start=(k == 0), stop=(k == KC - 1))
                        mm.then_inc(e_guf, 1)
                    if c:
                        down(e, buf, c - 1)
                    elif not isinstance(e, int):
                        down(e - 1, 1 - buf, B - 1)
            experts(pe, expert)
            down(E, 0, B - 1)

        def stage3_act(act):
            act.wait_ge(e_ones, 1)
            act.sem_inc(e_go, 1)
            e_norm.first_act(act)
            with act.Fori(0, B) as b:
                e_norm.ready(act, b)
                e_hcp.inc(act.copy(m_h[:, :, chunk(b)], m_hc[:]))
                EG.wait(act, b, EG_GATE)
                e_sig.inc(act.activation(m_sg[:].rearrange("p i e -> p (i e)"), EG.bank(EG_GATE)[:, 0:NT * E], ACT.Sigmoid))
                i_free(act, EG, b, EG_GATE, e_sig, 1)
                e_norm.square(act, b)
                e_norm.root(act, b)
                EG.wait(act, b, EG_COMB)
                act.copy(m_comb[:, chunk(b)], EG.bank(EG_COMB)[0:NE, :]).then_inc(e_go, 1)
                act.wait_ge(e_go, b + 2)
                act.sem_inc(EG.free[EG_COMB % 2], 1)

            def expert(e, buf, r):
                for u in range(UE):
                    at(act, e_guf, e, u + 1)
                    at(act, e_mul, e, u - 1)
                    act.activation(m_g[:, u % 2, :], ps[:, 2 * (u % 2), :], ACT.Silu).then_inc(e_silu, 1)
            experts(act, expert)

        def stage3_pool(pool):
            def expert(e, buf, r):
                pool.wait_ge(e_cbl[buf], r * 16 + 16)
                for u in range(UE):
                    c, h = divmod(u, 2)
                    at(pool, e_mul, e, u + 1)
                    at(pool, e_dn, e, 2 * c - 2)
                    pool.tensor_tensor(m_a[:, c % 2, h, :], m_m[:, u % 2, :], m_cb[:, buf, c * S:(c + 1) * S],
                                       ALU.mult).then_inc(e_act, 1)
            experts(pool, expert)

        def stage3_dve(dve, before, count):
            dve.wait_ge(before, count)
            dve.memset(m_w17[:], 1.0).then_inc(e_ones, 1)
            e_norm.first_dve(dve)
            with dve.Fori(0, B) as b:
                dve.wait_ge(e_go, b + 1)
                e_norm.scale(dve, b)
                e_norm.center(dve, b)
                ch = lambda ins: e_gate.link(dve, b, ins)
                e_sig.wait(dve, b, 1)
                ch(dve.tensor_tensor(m_sel[:], m_sg[:], row("expert_bias").unsqueeze(1).broadcast_to([P, NT, E]), ALU.add))
                for i in range(NT):
                    o = m_sel[:, i, :].unsqueeze(1).broadcast_to([P, E, E])
                    s = m_sel[:, i, :].unsqueeze(2).broadcast_to([P, E, E])
                    e_gate.inc(dve.tensor_tensor(m_gt[:, i], o, s, ALU.is_gt))
                    e_gate.inc(dve.tensor_tensor(m_eq[:, i], o, s, ALU.is_equal))
                e_gate.wait(dve, b, 9)
                ch(dve.tensor_tensor(m_eq[:].rearrange("p i e f -> p i (e f)"), m_eq[:].rearrange("p i e f -> p i (e f)"),
                                     const("before").unsqueeze(1).broadcast_to([P, NT, E * E]), ALU.mult))
                ch(dve.tensor_tensor(m_gt[:].rearrange("p i e f -> p (i e f)"), m_gt[:].rearrange("p i e f -> p (i e f)"),
                                     m_eq[:].rearrange("p i e f -> p (i e f)"), ALU.add))
                ch(dve.tensor_reduce(m_sel[:], m_gt[:], AX.X, ALU.add))
                ch(dve.scalar_tensor_tensor(m_sel[:], m_sel[:], TOPK - 0.5, m_sg[:], ALU.is_lt, ALU.mult))
                ch(dve.tensor_reduce(m_sum[:], m_sel[:], AX.X, ALU.add))
                ch(dve.reciprocal(m_sum[:], m_sum[:]))
                ch(dve.tensor_tensor(m_sel[:], m_sel[:], m_sum[:].unsqueeze(2).broadcast_to([P, NT, E]), ALU.mult))
                e_gate.inc(dve.tensor_scalar(m_w17[:, :, 0:E], m_sel[:], ROUTE_SCALE, None, ALU.mult))
                e_norm.inverse(dve, b)

            def acc(e, c):
                for m in range(KC):
                    at(dve, e_dn, e, 2 * c + m + 1)
                    at(dve, e_acc, e, 2 * c + m - 1)
                    xk = xT[:, m, c * S:(c + 1) * S]
                    dve.tensor_tensor(xk, xk, ps[:, DN_BANK + (2 * c + m) % 4, :], ALU.add).then_inc(e_acc, 1)

            def expert(e, buf, r):
                for u in range(UE):
                    at(dve, e_silu, e, u + 1)
                    at(dve, e_act, e, u - 1)
                    dve.tensor_tensor(m_m[:, u % 2, :], m_g[:, u % 2, :], ps[:, 2 * (u % 2) + 1, :], ALU.mult).then_inc(e_mul, 1)
                    if u % 2:
                        if u > 1:
                            acc(e, u // 2 - 1)
                        elif not isinstance(e, int):
                            acc(e - 1, B - 1)
            experts(dve, expert)
            acc(E, B - 1)

        def stage3_loads(sp):
            def matrices(e, buf):
                for w, n in ((m_wg, "eg"), (m_wu, "eu"), (m_wd, "ed")):
                    src = a[n][:, bass.ds(e, 1)].rearrange("p o k n -> p (o k) n")
                    sp.dma_start(w[:, buf], src).then_inc(e_wl[buf], 16)

            def weights(e, buf):
                sp.dma_start(m_cb[:, buf, :], a["comb"][bass.ds(e, 1), :].broadcast_to([P, TOK])).then_inc(e_cbl[buf], 16)

            matrices(0, 0)
            matrices(1, 1)
            sp.wait_ge(e_go, 1 + B)
            sp.dma_start(a["comb"], m_comb[:]).then_inc(e_comb, 16)
            sp.wait_ge(e_comb, 16)
            weights(0, 0)
            weights(1, 1)
            def refill(e, buf):
                at(sp, e_dn, e - 1, 0)
                matrices(e, buf)
                at(sp, e_act, e - 1, 0)
                weights(e, buf)

            with sp.Fori(0, E // 2 - 1) as i:
                refill(i * 2 + 2, 0)
                refill(i * 2 + 3, 1)
            refill(E, 0)

        END3 = UE * NE

        NG_NORM, NG_OUT = 0, 2
        NGB = Gen("ng", NG_OUT + KC, ahead=(1, 1))
        n_norm = Norm("n_", NGB, NG_NORM, n_h, n_xc, n_sq, n_r)
        n_go = sem("n_go")
        n_kvf, n_kva = Count("n_kvf", NT), Count("n_kva", NT)
        n_ch = Count("n_ch", 6 * NT + 3)
        n_var = Count("n_var", 1)
        n_rt = Count("n_root", 1)
        n_qf, n_qa, n_mx = Count("n_qf", NT), Count("n_qa", 2 * NT), Count("n_mx", NT)
        n_sub, n_ex, n_nm = (Count("n_" + x, NT) for x in ("sub", "exp", "nrm"))
        n_rc = Count("n_rec", 2 * NT)
        n_fin = Count("n_fin", NT * (2 + 2 * B))

        def stage4_pe(pe):
            pe.wait_ge(n_go, 1)
            n_norm.first_pe(pe)
            with pe.Fori(0, B) as b:
                pe.wait_ge(n_go, b * KC + 1)
                n_norm.ready(pe, b)
                pe.wait_ge(loads["w1"], 32)
                for i in range(NT):
                    if i >= 2:
                        n_kva.wait(pe, b, i - 1)
                    for k in range(KC):
                        mm = pe.matmul(ps[:, 4 + i % 2, 0:KV1], n_h[:, k, i * P:(i + 1) * P], wkv1[:, k, :],
                                       start=(k == 0), stop=(k == KC - 1))
                    n_kvf.inc(mm)
                for i in range(NT):
                    if i >= 2:
                        n_qa.wait(pe, b, 2 * (i - 1))
                    for m in range(2):
                        for k in range(KC):
                            mm = pe.matmul(ps[:, 2 * (i % 2) + m, :], n_h[:, k, i * P:(i + 1) * P],
                                           wq1[:, k, m * S:(m + 1) * S], start=(k == 0), stop=(k == KC - 1))
                    n_qf.inc(mm)
                n_norm.mean(pe, b)
                n_norm.variance(pe, b)
                for k in range(KC):
                    NGB.claim(pe, b, NG_OUT + k)
                for i in range(NT):
                    n_fin.wait(pe, b, (i + 1) * (2 + 2 * B))
                    for k in range(KC):
                        mm = pe.transpose(NGB.bank(NG_OUT + k)[:, i * P:(i + 1) * P], n_y[:, i, k * P:(k + 1) * P], ident)
                        if i == NT - 1:
                            NGB.filled(mm, NG_OUT + k)

        def stage4_act(act):
            n_norm.first_act(act)
            with act.Fori(0, B) as b:
                n_var.wait(act, b, 1)
                n_rt.inc(act.activation(n_mv[:, 1], n_mv[:, 0], ACT.Sqrt, bias=eps[:, 0:1]))
                for i in range(NT):
                    n_sub.wait(act, b, i + 1)
                    n_ex.inc(act.activation(n_q[:, i % 3, :], n_q[:, i % 3, :], ACT.Exp))
                n_norm.square(act, b)
                n_norm.root(act, b)

        def heads_of(v):
            return v.rearrange("p (h c) -> p h c", h=H1)

        def stage4_pool(pool):
            with pool.Fori(0, B) as b:
                def normalise(i):
                    n_rc.wait(pool, b, 2 * (i + 1))
                    q = heads_of(n_q[:, i % 3, :])
                    n_nm.inc(pool.tensor_tensor(q, q, n_sm[:, 2, i, :].unsqueeze(2).broadcast_to([P, H1, K1]), ALU.mult))
                for i in range(NT):
                    n_mx.wait(pool, b, i + 1)
                    q = heads_of(n_q[:, i % 3, :])
                    n_sub.inc(pool.tensor_tensor(q, q, n_sm[:, 0, i, :].unsqueeze(2).broadcast_to([P, H1, K1]), ALU.subtract))
                    if i:
                        normalise(i - 1)
                normalise(NT - 1)

        def stage4_dve(dve, before, count):
            dve.wait_ge(before, count)
            dve.memset(n_hist[:], 0.0).then_inc(n_go, 1)
            n_norm.first_dve(dve)
            with dve.Fori(0, B) as b:
                ch = lambda ins: n_ch.link(dve, b, ins)
                dve.wait_ge(n_go, b * KC + 1)
                n_norm.scale(dve, b)
                for i in range(NT):
                    n_kvf.wait(dve, b, i + 1)
                    n_kva.link(dve, b, dve.tensor_tensor(n_kv[:, i, :], ps[:, 4 + i % 2, 0:KV1], row("bkv"), ALU.add))
                    for m, sl in ((0, slice(0, K1)), (1, slice(K1, KV1))):
                        n_ch.inc(dve.bn_stats(n_bs[:, i, m, :], n_kv[:, i, sl]))
                n_ch.wait(dve, b, 2 * NT)
                settle(dve)
                for i in range(NT):
                    for m in range(2):
                        n_ch.inc(dve.bn_aggr(n_ba[:, i, m, :], n_bs[:, i, m, :]))
                n_ch.wait(dve, b, 4 * NT)
                n_var.inc(dve.tensor_copy(n_mv[:, 0], n_ba[:, :, :, 1]))

                def queries(i):
                    n_qf.wait(dve, b, i + 1)
                    if i >= 3:
                        n_fin.wait(dve, b, (i - 3) * (2 + 2 * B) + 1)
                    for m in range(2):
                        sl = slice(m * S, (m + 1) * S)
                        ins = dve.tensor_tensor(n_q[:, i % 3, sl], ps[:, 2 * (i % 2) + m, :], row("bq")[:, sl], ALU.add)
                        n_qa.inc(ins)
                    n_qa.wait(dve, b, 2 * (i + 1))
                    n_mx.inc(dve.tensor_reduce(n_sm[:, 0, i, :], heads_of(n_q[:, i % 3, :]), AX.X, ALU.max))

                def sums(i):
                    n_ex.wait(dve, b, i + 1)
                    n_rc.link(dve, b, dve.tensor_reduce(n_sm[:, 1, i, :], heads_of(n_q[:, i % 3, :]), AX.X, ALU.add))
                    n_rc.inc(dve.reciprocal(n_sm[:, 2, i, :], n_sm[:, 1, i, :]))

                def result(i):
                    fin = lambda ins: n_fin.link(dve, b, ins)
                    n_nm.wait(dve, b, i + 1)
                    fin(dve.tensor_reduce(n_qn[:, 0, :], n_q[:, i % 3, :].rearrange("p (h c) -> p c h", h=H1), AX.X, ALU.add))
                    fin(dve.tensor_scalar(n_qn[:, 1, :], n_qn[:, 0, :], const("scal")[:, bass.ds(b, 1)], None, ALU.mult))
                    for s in range(B):
                        n_fin.inc(dve.scalar_tensor_tensor(n_jk[:, s, :], n_qn[:, 1, :], 1.0, n_hist[:, i, s, 0:K1], ALU.mult, ALU.mult,
                                                           accum_out=n_d[:, s:s + 1]))
                    n_fin.wait(dve, b, n_fin.n)
                    v = lambda s: n_hist[:, i, s, K1:KV1]
                    fin(dve.tensor_scalar(n_y[:, i, :], v(0), n_d[:, 0:1], None, ALU.mult))
                    for s in range(1, B):
                        fin(dve.scalar_tensor_tensor(n_y[:, i, :], v(s), n_d[:, s:s + 1], n_y[:, i, :], ALU.mult, ALU.add))

                queries(0)
                n_rt.wait(dve, b, 1)
                ch(dve.reciprocal(n_mv[:, 1], n_mv[:, 1]))
                for i in range(NT):
                    for m, sl in ((0, slice(0, K1)), (1, slice(K1, KV1))):
                        n_ch.inc(dve.tensor_scalar(n_kv[:, i, sl], n_kv[:, i, sl], n_ba[:, i, m, 0:1], n_mv[:, 1, i, m:m + 1],
                                                   ALU.subtract, ALU.mult))
                queries(1)
                n_ch.wait(dve, b, n_ch.n)
                ch(dve.tensor_tensor(n_kv[:], n_kv[:], row("gkv").unsqueeze(1).broadcast_to([P, NT, KV1]), ALU.mult))
                ch(dve.tensor_tensor(n_hist[:, :, bass.ds(b, 1), :].rearrange("p i o c -> p i (o c)"), n_kv[:],
                                     row("betakv").unsqueeze(1).broadcast_to([P, NT, KV1]), ALU.add))
                sums(0)
                for i in range(2, NT + 2):
                    if i < NT:
                        queries(i)
                    if i - 1 < NT:
                        sums(i - 1)
                    if i == NT - 1:
                        n_norm.center(dve, b)
                    result(i - 2)
                n_norm.inverse(dve, b)
                for k in range(KC):
                    NGB.wait(dve, b, NG_OUT + k)
                    xk = xT[:, k, chunk(b)]
                    dve.tensor_tensor(xk, xk, NGB.bank(NG_OUT + k), ALU.add).then_inc(n_go, 1)
                dve.wait_ge(n_go, b * KC + 1 + KC)
                for k in range(KC):
                    dve.sem_inc(NGB.free[(NG_OUT + k) % 2], 1)

        FG_SC, FG_OH, FG_NORM, FG_OUT = 0, 1, 2, 4
        FG = Gen("fg", 6, ahead=(1, 1))
        f_norm = Norm("f_", FG, FG_NORM, f_h, f_xc, f_sq, f_r)
        f_go = sem("f_go")
        f_sgn = sem("f_sign")
        f_ch = Count("f_ch", 5)
        f_ohr = Count("f_ohr", 2)
        f_bc, f_hm = Count("f_bc", T1), Count("f_hm", T1)
        f_use = Count("f_use", T1 - 1)

        def stage6_pe(pe):
            pe.wait_ge(f_sgn, 1)
            pe.wait_ge(loads["wt1"], 32)
            f_norm.first_pe(pe)
            with pe.Fori(0, B) as b:
                pe.wait_ge(f_go, b * KC + 1)
                f_norm.ready(pe, b)
                FG.claim(pe, b, FG_SC)
                for i in range(NT):
                    for k in range(KC):
                        mm = pe.matmul(FG.bank(FG_SC)[:, i * T1:(i + 1) * T1], f_h[:, k, i * P:(i + 1) * P],
                                       f_sg[:, k * T1:(k + 1) * T1], start=(k == 0), stop=(k == KC - 1))
                FG.filled(mm, FG_SC)
                f_ch.wait(pe, b, 5)
                FG.claim(pe, b, FG_OH)
                for i in range(NT):
                    mm = pe.transpose(FG.bank(FG_OH)[0:T1, i * P:(i + 1) * P], f_c[:, i, :], ident)
                FG.filled(mm, FG_OH)
                f_ohr.wait(pe, b, 2)
                def spread(t):
                    if t >= 4:
                        f_hm.wait(pe, b, t - 3)
                    f_bc.inc(pe.matmul(ps[:, t % 4, :], f_one[:, t * P:(t + 1) * P], f_ohb[:], start=True, stop=True))
                spread(0)
                f_norm.mean(pe, b)
                spread(1)
                f_norm.variance(pe, b)
                for k in range(KC):
                    FG.claim(pe, b, FG_OUT + k)
                    pe.matmul(FG.bank(FG_OUT + k), bt1[:, k * P:(k + 1) * P], f_oh[:], start=True, stop=False, skip_group_check=True)

                for t in range(T1):
                    if t + 2 < T1:
                        spread(t + 2)
                    f_hm.wait(pe, b, t + 1)
                    for k in range(KC):
                        for c in range(KC):
                            mm = pe.matmul(FG.bank(FG_OUT + k), wt1[:, t, c, k * P:(k + 1) * P], f_m[:, t % 4, c, :], start=False,
                                           stop=(t == T1 - 1 and c == KC - 1), skip_group_check=True)
                        if t == T1 - 1:
                            FG.filled(mm, FG_OUT + k)
                    if t < T1 - 1:
                        f_use.inc(mm)

        def stage6_act(act):
            act.wait_ge(f_go, 1)
            act.activation(f_sg[:], col("sigs"), ACT.Sign).then_inc(f_sgn, 1)
            f_norm.first_act(act)
            with act.Fori(0, B) as b:
                FG.wait(act, b, FG_OH)
                f_ohr.inc(act.copy(f_oh[:], FG.bank(FG_OH)[0:T1, :]))
                f_ohr.inc(act.copy(f_ohb[:], FG.bank(FG_OH)[0:T1, :]))
                i_free(act, FG, b, FG_OH, f_ohr, 2)
                f_norm.square(act, b)
                f_norm.root(act, b)

        def stage6_dve(dve, before, count):
            dve.wait_ge(before, count)
            dve.tensor_copy(f_one[:].rearrange("p (t c) -> p t c", c=P),
                            ident[0:T1, 0:T1].unsqueeze(2).broadcast_to([T1, T1, P])).then_inc(f_go, 1)
            f_norm.first_dve(dve)
            with dve.Fori(0, B) as b:
                ch = lambda ins: f_ch.link(dve, b, ins)
                dve.wait_ge(f_go, b * KC + 1)
                f_norm.scale(dve, b)
                FG.wait(dve, b, FG_SC)
                s = FG.bank(FG_SC)[:, 0:NT * T1].rearrange("p (i t) -> p i t", t=T1)
                wide = lambda v: v.unsqueeze(2).broadcast_to([P, NT, T1])
                ch(dve.tensor_reduce(f_mx[:, 0, :], s, AX.X, ALU.max))
                ch(dve.tensor_tensor(f_c[:], s, wide(f_mx[:, 0, :]), ALU.is_equal))
                dve.sem_inc(FG.free[FG_SC % 2], 1)
                ch(dve.tensor_tensor(f_c[:], f_c[:], const("first").unsqueeze(1).broadcast_to([P, NT, T1]), ALU.mult))
                ch(dve.tensor_reduce(f_mx[:, 1, :], f_c[:], AX.X, ALU.max))
                ch(dve.tensor_tensor(f_c[:], f_c[:], wide(f_mx[:, 1, :]), ALU.is_equal))
                for t in range(T1):
                    if t == 0:
                        f_norm.center(dve, b)
                    if t == T1 - 1:
                        f_norm.inverse(dve, b)
                    f_bc.wait(dve, b, t + 1)
                    if t >= 4:
                        f_use.wait(dve, b, t - 3)
                    f_hm.inc(dve.tensor_tensor(f_m[:, t % 4], f_h[:], ps[:, t % 4, :].unsqueeze(1).broadcast_to([P, KC, S]), ALU.mult))
                for k in range(KC):
                    FG.wait(dve, b, FG_OUT + k)
                    xk = xT[:, k, chunk(b)]
                    dve.tensor_tensor(xk, xk, FG.bank(FG_OUT + k), ALU.add).then_inc(f_go, 1)
                dve.wait_ge(f_go, b * KC + 1 + KC)
                for k in range(KC):
                    dve.sem_inc(FG.free[(FG_OUT + k) % 2], 1)

        STEPS = 4
        DEPTH = 8
        GROUPS = 32
        START = 0.8
        MASS_TOL = 2e-5
        FINAL, TURN = STEPS + 1, STEPS + 2
        assert NQ % DEPTH == 0 and DEPTH >= TURN + 1

        def sparse_quick():
            T = "y_"
            wq, wk, wv, wo = xw[1]
            bq, bk, bo, bv = col("bq1"), col("bk1"), col("bo1"), row("bv1")
            full, free = [sem(f"{T}full{k}") for k in range(2)], [sem(f"{T}free{k}") for k in range(2)]
            USES = {"V0": (0, 0), "OUT0": (1, 0), "OUT1": (0, 1), "K1": (1, 1), "mean": (0, 2), "var": (1, 2),
                    "V1": (0, 3), "Q0": (1, 3), "Q1": (0, 4), "K0": (1, 4)}
            AHEAD = {"mean": 0, "Q1": 1, "var": 0, "Q0": 1, "K0": 2}

            def use_count(b, name):
                if b is None:
                    return AHEAD[name]
                bank, n = USES[name]
                if isinstance(b, int) and (b, name) in ((0, "V0"), (B, "OUT1")):
                    n += 1 if b == 0 else -1
                return b * 5 + (1 + bank + n)

            def bank(name):
                return ps[:, G_BANK + USES[name][0], :]

            def claim(pe, b, name):
                n = use_count(b, name)
                if not (isinstance(n, int) and n == 0):
                    pe.wait_ge(free[USES[name][0]], n)

            def filled(ins, name):
                ins.then_inc(full[USES[name][0]], 1)

            def wait_use(eng, b, name):
                eng.wait_ge(full[USES[name][0]], use_count(b, name) + 1)

            def give_back(eng, name):
                eng.sem_inc(free[USES[name][0]], 1)

            go = sem(T + "go")
            cld = sem(T + "ctx")
            cused = Count(T + "cused", 1)
            ln, lnact, made = Count(T + "ln", 2), Count(T + "lnact", 2), Count(T + "h", 1)
            qr, kr, kz, vr = Count(T + "q", GX), Count(T + "k", GX), Count(T + "kz", NQ), Count(T + "v", GX * NT)
            sf, sev = Count(T + "s", NX), Count(T + "sev", NX)
            fs, cn = Count(T + "f", NX * STEPS), Count(T + "cnt", NX * STEPS)
            st = Count(T + "start", NQ * 11)
            up = Count(T + "up", 4 * (NQ + STEPS - 1))
            pr, tn = Count(T + "p", NX), Count(T + "t", NX)
            pte = [Count(T + "pteA", NX // 2), Count(T + "pteD", NX // 2)]
            pv, oev = Count(T + "pv", NQ), Count(T + "oev", GX)
            F_, C_, U_, M_ = (x_st[:, k, :] for k in range(4))
            act_junk = x_r[:, 1, :].bitcast(BF16).rearrange("p (a s) -> p a s", a=2)
            dve_junk = x_h[:, 1, :].bitcast(BF16).rearrange("p (a s) -> p a s", a=2)
            h = x_xc

            def section(kind, counts):
                for c in counts:
                    if kind == "body":
                        c.start = c.n - c.per
                    if kind != "first":
                        c.n = c.start

            def sections(eng, slots, counts):
                slots("first", 0, NQ)
                with eng.Fori(1, B) as b:
                    section("body", counts)
                    slots("body", b, NQ)
                section("last", counts)
                slots("last", B, TURN + 1)

            def wait(c, eng, b, n):
                if not (isinstance(b, int) and b * c.per + n <= 0):
                    c.wait(eng, b, n)

            def xb(n):
                return x_ring[:, n // NT % DEPTH, n % NT, :]

            def colof(n):
                return n % NX

            def there(kind, q):
                return q >= 0 if kind == "first" else q < 0 if kind == "last" else True

            def active(kind, t):
                return [q for q in range(t - STEPS, t) if there(kind, q)]

            def stretches(kind, t):
                old = [q for q in active(kind, t) if q < 0]
                new = [q for q in active(kind, t) if q >= 0]
                return [slice(NT * (g[0] % NQ), NT * (g[-1] % NQ) + NT) for g in (old, new) if g]

            def sums_after(kind, t):
                first = sum(NT * len(active("first", s)) for s in range(NQ))
                n = sum(NT * len(active(kind, s)) for s in range(t + 1))
                return n if kind == "first" else n + first - fs.per

            def updates_after(kind, t):
                first = sum(4 * len(stretches("first", s)) for s in range(NQ))
                n = sum(4 * len(stretches(kind, s)) for s in range(t + 1))
                return n if kind == "first" else n + first - up.per

            def next_one(b):
                return 0 if b is None else (b + 1) % B

            def nb(b, n):
                return (0, n) if b is None else (b, n + 2)

            def on_pe(pe):
                def project(b, name, w, src, g):
                    claim(pe, b, name)
                    for k in range(KC):
                        mm = pe.matmul(bank(name), w[:, k, g * P:(g + 1) * P], src[:, k, :], start=(k == 0), stop=(k == KC - 1))
                    filled(mm, name)

                def project_values(b, g):
                    claim(pe, b, f"V{g}")
                    for i in range(NT):
                        for k in range(KC):
                            mm = pe.matmul(bank(f"V{g}")[:, i * P:(i + 1) * P], x_c[:, k, i * P:(i + 1) * P],
                                           wv[:, k, g * P:(g + 1) * P], start=(k == 0), stop=(k == KC - 1))
                    filled(mm, f"V{g}")

                def mean(b):
                    claim(pe, b, "mean")
                    for k in range(KC):
                        mm = pe.matmul(bank("mean"), meanw[:], xT[:, k, chunk(next_one(b))], start=(k == 0), stop=(k == KC - 1))
                    filled(mm, "mean")

                def variance(b):
                    lnact.wait(pe, *nb(b, 1))
                    claim(pe, b, "var")
                    for k in range(KC):
                        mm = pe.matmul(bank("var"), meanw[:], x_k[:, k, :], start=(k == 0), stop=(k == KC - 1))
                    filled(mm, "var")

                def queries(b):
                    made.wait(pe, 0 if b is None else b, 1 if b is None else 2)
                    for g in range(GX):
                        project(b, f"Q{g}", wq, h, g)
                    pe.wait_ge(cld, 16 if b is None else b * 16 + 32)
                    project(b, "K0", wk, x_c, 0)

                pe.wait_ge(go, 1)
                pe.wait_ge(loads["xw1"], 64)
                mean(None)
                variance(None)
                queries(None)

                def slots(kind, b, count):
                    def scores(n):
                        q = n // NT
                        if n % NT == 0:
                            wait(qr, pe, b, q // HPG + 1)
                            wait(kz, pe, b, q + 1)
                        wait(sev, pe, b, n - S_BANKS + 1 if n >= S_BANKS else 0)
                        j = n % NT
                        sf.inc(pe.matmul(ps[:, n % S_BANKS, :], x_q[:, q // HPG, j * P:(j + 1) * P], x_kz[:, q % 4, :], start=True, stop=True))

                    def turn(n):
                        wait(pr, pe, b, n + 1)
                        wait(pte[n % 2], pe, b, n // 2)
                        for k in range(NT):
                            mm = pe.transpose(ps[:, PT_BANK + n % 2, k * P:(k + 1) * P], xb(n)[:, k * P:(k + 1) * P], ident)
                        tn.inc(mm)

                    def values(q):
                        hh, g = q % HPG, q % NQ // HPG
                        for c in pte:
                            wait(c, pe, b, 2 * (q + 1))
                        if hh == 0:
                            wait(vr, pe, b, NT * (g + 1))
                            wait(oev, pe, b, g)
                        for k in range(NT):
                            mm = pe.matmul(ps[:, O_BANK, :], x_vz[:, k, hh * P:(hh + 1) * P], x_pt[:, k, :],
                                           start=(hh == 0 and k == 0), stop=(hh == HPG - 1 and k == NT - 1),
                                           skip_group_check=True)
                        pv.inc(mm)

                    for t in range(count):
                        q = t - TURN
                        if kind != "last":
                            for n in range(NT * t, NT * t + NT):
                                scores(n)
                        if there(kind, q):
                            for n in range(NT * q, NT * q + NT):
                                turn(n)
                            values(q)
                        if kind != "last" and t == TURN - 1:
                            project_values(b, 0)
                        if t == TURN and kind != "first":
                            wait(oev, pe, b, 0)
                            for k in range(KC):
                                claim(pe, b, f"OUT{k}")
                                for g in range(GX):
                                    mm = pe.matmul(bank(f"OUT{k}"), wo[:, g, k * P:(k + 1) * P], x_o[:, g, :],
                                                   start=(g == 0), stop=(g == GX - 1))
                                filled(mm, f"OUT{k}")
                        if kind != "last":
                            if t == HPG - 1:
                                project(b, "K1", wk, x_c, 1)
                            if t == NORM_SLOT:
                                mean(b)
                            if t == NORM_SLOT + 1:
                                variance(b)
                                project_values(b, 1)
                            if t == NQ - 1:
                                queries(b)

                sections(pe, slots, ())

            NORM_SLOT = 12

            def evac_turned(eng, copy, b, n):
                q, j = n // NT, n % NT
                wait(tn, eng, b, n + 1)
                wait(pv, eng, b, q)
                pte[n % 2].inc(copy(x_pt[:, :, j * P:(j + 1) * P],
                                    ps[:, PT_BANK + n % 2, :].rearrange("p (k c) -> p k c", c=P)))

            def turned_units(kind, t, parity):
                q = t - TURN
                return [n for n in range(NT * q, NT * q + NT) if n % 2 == parity] if there(kind, q) else []

            def on_act(act):
                def square(b):
                    ln.wait(act, *nb(b, 1))
                    lnact.inc(act.activation(x_k[:], h[:], ACT.Square))

                def root(b):
                    wait_use(act, b, "var")
                    lnact.inc(act.activation(x_r[:, 0, :], bank("var"), ACT.Sqrt, bias=eps[:, 0:1]))
                    lnact.wait(act, *nb(b, 2))
                    give_back(act, "var")

                square(None)
                root(None)

                def slots(kind, b, count):
                    for t in range(count):
                        evac = list(range(NT * t, NT * t + NT)) if kind != "last" else []

                        def evac_scores(n):
                            wait(sf, act, b, n + 1)
                            wait(tn, act, b, n - NT * DEPTH + 1)
                            sev.inc(act.copy(xb(n), ps[:, n % S_BANKS, :]))

                        if evac:
                            evac_scores(evac.pop(0))
                        if kind != "last":
                            if t == NORM_SLOT + 1:
                                wait(kz, act, b, NQ)
                                square(b)
                            if t == NORM_SLOT + 2:
                                root(b)
                        turned = turned_units(kind, t, 0)
                        for s in active(kind, t):
                            if s == t - 1:
                                wait(st, act, b, 11 * t)
                            if s == active(kind, t)[0]:
                                wait(up, act, b, updates_after(kind, t - 1))
                            for n in range(NT * s, NT * s + NT):
                                wait(fs, act, b, fs.n - 1)
                                c = colof(n)
                                fs.inc(act.activation(act_junk[:, fs.n % 2, :], xb(n), ACT.Relu, scale=-1.0, bias=U_[:, c:c + 1],
                                                      accum_out=F_[:, c:c + 1]))
                            if turned:
                                evac_turned(act, act.copy, b, turned.pop(0))
                            if evac:
                                evac_scores(evac.pop(0))
                        for n in evac:
                            evac_scores(n)
                        for n in turned:
                            evac_turned(act, act.copy, b, n)
                        q = t - FINAL
                        if there(kind, q):
                            wait(up, act, b, updates_after(kind, t - 1))
                            for n in range(NT * q, NT * q + NT):
                                c = colof(n)
                                pr.inc(act.activation(xb(n), xb(n), ACT.Relu, scale=-1.0, bias=U_[:, c:c + 1],
                                                      accum_out=M_[:, c:c + 1]))

                sections(act, slots, (fs, sev, pr, pte[0], lnact))

            def on_pool(pool):
                def keys(b):
                    for q in range(NQ):
                        if q % HPG == 0:
                            wait(kr, pool, b, q // HPG + 1)
                        wait(sf, pool, b, NT * (q - 3))
                        settle(pool)
                        kz.inc(pool.tensor_scalar(x_kz[:, q % 4, :], x_k[:, q // HPG, :], const("heads")[:, q % HPG:q % HPG + 1],
                                                  1.0, ALU.mult, ALU.mult))
                keys(0)
                with pool.Fori(1, B) as b:
                    keys(b)

            def on_dve(dve, before, count0):
                def center(b):
                    wait_use(dve, b, "mean")
                    m = bank("mean").unsqueeze(1).broadcast_to([P, KC, S])
                    ln.inc(dve.tensor_tensor(h[:], xT[:, :, chunk(next_one(b))], m, ALU.subtract))
                    ln.wait(dve, *nb(b, 1))
                    give_back(dve, "mean")

                def scale(b):
                    lnact.wait(dve, *nb(b, 2))
                    ln.inc(dve.reciprocal(x_r[:, 0, :], x_r[:, 0, :]))
                    ln.wait(dve, *nb(b, 2))
                    made.inc(dve.tensor_tensor(h[:], h[:], x_r[:, 0, :].unsqueeze(1).broadcast_to([P, KC, S]), ALU.mult))

                def keys(b, g):
                    name = f"K{g}"
                    wait_use(dve, b, name)
                    kr.inc(dve.tensor_scalar(x_k[:, g, :], bank(name), bk[:, g:g + 1], None, ALU.add))
                    kr.wait(dve, 0 if b is None else b, kr.n)
                    give_back(dve, name)

                def queries(b):
                    for g in range(GX):
                        wait_use(dve, b, f"Q{g}")
                        qr.inc(dve.tensor_scalar(x_q[:, g, :], bank(f"Q{g}"), bq[:, g:g + 1], -SCX, ALU.add, ALU.mult))
                        qr.wait(dve, 0 if b is None else b, qr.n)
                        give_back(dve, f"Q{g}")
                    keys(b, 0)

                def vals(b, g):
                    name = f"V{g}"
                    wait_use(dve, b, name)
                    for i in range(NT):
                        o = x_vz[:, i, :].rearrange("p (h c) -> p h c", h=HPG)[:, :, 0:HDX]
                        vr.inc(dve.tensor_tensor(o, bank(name)[:, i * P:(i + 1) * P].rearrange("p (h c) -> p h c", h=HPG),
                                                 bv[:, g * P:(g + 1) * P].rearrange("p (h c) -> p h c", h=HPG), ALU.add))
                    vr.wait(dve, b, vr.n)
                    give_back(dve, name)
                    if g == GX - 1:
                        dve.sem_inc(cused.sem, 1)

                dve.wait_ge(before, count0)
                dve.memset(x_vz[:], 0.0).then_inc(go, 1)
                dve.memset(x_bad[:], 0.0).then_inc(flag, 1)
                dve.wait_ge(flag, 1)
                dve.wait_ge(go, 1)
                center(None)
                scale(None)
                queries(None)

                def slots(kind, b, count):
                    def outputs(g):
                        wait(pv, dve, b, HPG * (g + 1))
                        oev.inc(dve.tensor_copy(x_o[:, g % GX, :], ps[:, O_BANK, :]))

                    lk_st = lambda ins: st.link(dve, b, ins)
                    y = x_gm[:, :, 0:GROUPS]

                    def minima(q):
                        wait(sev, dve, b, NT * (q + 1))
                        lk_st(dve.tensor_reduce(y, x_ring[:, q % DEPTH].rearrange("p t (a g) -> p t g a", g=GROUPS), AX.X, ALU.min))

                    def start(q):
                        lk = lk_st
                        v = slice(NT * q, NT * q + NT)
                        wide = lambda a: a.unsqueeze(2).broadcast_to([P, NT, GROUPS])
                        d, m = x_gd[:, 0, :, 0:GROUPS], x_gd[:, 1, :, 0:GROUPS]
                        lk(dve.tensor_reduce(F_[:, v], y, AX.X, ALU.add))
                        lk(dve.tensor_scalar(U_[:, v], F_[:, v], START, 1.0 / GROUPS, ALU.add, ALU.mult))
                        lk(dve.tensor_tensor(d, y, wide(U_[:, v]), ALU.subtract))
                        st.inc(dve.tensor_scalar(m, d, 0.0, None, ALU.is_lt))
                        lk(dve.tensor_scalar(d, d, 0.0, None, ALU.min))
                        lk(dve.tensor_reduce(x_sf[:, 0, :, :], x_gd[:, :, :, 0:GROUPS], AX.X, ALU.add))
                        lk(dve.tensor_scalar(x_sf[:, 1, 1, :], x_sf[:, 0, 1, :], 1.0, None, ALU.max))
                        lk(dve.reciprocal(x_sf[:, 1, 1, :], x_sf[:, 1, 1, :]))
                        lk(dve.scalar_tensor_tensor(x_sf[:, 1, 0, :], x_sf[:, 0, 0, :], START, x_sf[:, 1, 1, :], ALU.add, ALU.mult))
                        lk(dve.tensor_tensor(U_[:, v], U_[:, v], x_sf[:, 1, 0, :], ALU.add))

                    def check(q):
                        v = slice(NT * (q % NQ), NT * (q % NQ + 4))
                        wait(pr, dve, b, NT * (q + 4))
                        bad.link(dve, b, dve.tensor_scalar(x_dev[:, 0], M_[:, v], -1.0, None, ALU.add))
                        bad.link(dve, b, dve.scalar_tensor_tensor(x_dev[:, 1], x_dev[:, 0], -1.0, x_dev[:, 0], ALU.mult, ALU.max))
                        bad.link(dve, b, dve.tensor_tensor(x_bad[:], x_bad[:], x_dev[:, 1], ALU.max))

                    for t in range(count):
                        turned = turned_units(kind, t, 1)
                        extra = []
                        if t == TURN:
                            if kind != "first":
                                extra.append(lambda: outputs(-1))
                            if kind != "last":
                                extra.append(lambda: vals(b, 0))
                        if t == HPG + TURN:
                            extra += [lambda: outputs(0), lambda: vals(b, 1)]
                        for s in active(kind, t) or (None,):
                            if s is not None:
                                for n in range(NT * s, NT * s + NT):
                                    wait(cn, dve, b, cn.n - 1)
                                    c = colof(n)
                                    cn.inc(dve.tensor_scalar(dve_junk[:, cn.n % 2, :], xb(n), U_[:, c:c + 1], None,
                                                             ALU.is_lt, ALU.add, accum_out=C_[:, c:c + 1]))
                            while extra:
                                extra.pop(0)()
                            if turned:
                                evac_turned(dve, dve.tensor_copy, b, turned.pop(0))
                        for n in turned:
                            evac_turned(dve, dve.tensor_copy, b, n)
                        if there(kind, t - TURN) and (t - TURN) % 4 == 3:
                            check(t - TURN - 3)
                        if t == TURN + 1 - (kind == "last") and kind != "first":
                            for k in range(KC):
                                wait_use(dve, b, f"OUT{k}")
                                if k == 0:
                                    dve.wait_ge(kept, 16)
                                xk = xT[:, k, chunk(b - 1)]
                                dve.scalar_tensor_tensor(xk, bank(f"OUT{k}"), bo[:, k:k + 1], xk, ALU.add, ALU.add).then_inc(go, 1)
                            dve.wait_ge(go, (b - 1) * KC + 1 + KC)
                            for k in range(KC):
                                give_back(dve, f"OUT{k}")
                        if kind != "last":
                            if t == HPG - 1:
                                keys(b, 1)
                            if t == NORM_SLOT:
                                center(b)
                            if t == NORM_SLOT + 2:
                                scale(b)
                            minima(t)
                        if active(kind, t):
                            cn.wait(dve, b, cn.n)
                            for v in stretches(kind, t):
                                lk = lambda ins: up.link(dve, b, ins)
                                lk(dve.tensor_scalar(C_[:, v], C_[:, v], 1.0, None, ALU.max))
                                lk(dve.reciprocal(C_[:, v], C_[:, v]))
                                fs.wait(dve, b, sums_after(kind, t))
                                lk(dve.scalar_tensor_tensor(F_[:, v], F_[:, v], -1.0, C_[:, v], ALU.add, ALU.mult))
                                lk(dve.tensor_tensor(U_[:, v], U_[:, v], F_[:, v], ALU.subtract))
                        if kind != "last":
                            start(t)
                            if t == NQ - 1:
                                queries(b)

                sections(dve, slots, (cn, st, up, pte[1], oev, qr, kr, vr, bad, ln, made))
                dve.tensor_reduce(x_bad1[:], x_bad[:], AX.X, ALU.max).then_inc(flag, 1)
                dve.wait_ge(flag_t, 1)
                dve.tensor_reduce(x_flag[:, 0:1], ps[0:1, 0, 0:P], AX.X, ALU.max).then_inc(flag, 1)
                dve.wait_ge(flag, 3)
                dve.tensor_scalar(x_flag[:, 1:2], x_flag[:, 0:1], MASS_TOL, None, ALU.is_gt).then_inc(flag, 1)
                dve.wait_ge(flag, 4)
                dve.tensor_copy(x_flagi[:], x_flag[:, 1:2]).then_inc(flag, 1)

            bad = Count(T + "bad", 3 * NQ // 4)

            def on_sync(sp):
                sp.dma_start(x_c[:], a["ctx"][:, :, 0:S]).then_inc(cld, 16)
                with sp.Fori(1, B + 1) as b:
                    cused.wait(sp, b - 1, 1)
                    sp.dma_start(x_c[:], a["ctx"][:, :, chunk(b % B)]).then_inc(cld, 16)

            return on_pe, on_act, on_pool, on_dve, go, on_sync

        kept = sem("kept")
        restored = sem("restored")
        flag_t = sem("flag_turned")
        flag = sem("flag")
        cross0 = cross(0)
        quick = sparse_quick()
        general = cross(1)

        def stage5_general(eng, step):
            eng.wait_ge(flag, 5)
            wrong = eng.value_load(x_flagi[0:1, 0:1], min_val=0, max_val=1)
            with eng.If(wrong > 0):
                step()

        END1 = 1 + A_GO * B
        ENDX = 1 + KC * B

        def context(sp, stage):
            cld, cused = stage[5], stage[6]
            c = a["ctx"]
            sp.dma_start(x_c[:], c[:, :, 0:S]).then_inc(cld, 16)
            with sp.Fori(1, B) as b:
                cused.wait(sp, b - 1, GX)
                sp.dma_start(x_c[:], c[:, :, chunk(b)]).then_inc(cld, 16)

        chain = [(1, a_go, END1), (2, cross0[4], ENDX), (3, e_acc, END3), (4, n_go, ENDX), (5, quick[4], ENDX)]

        def before(k):
            return chain[k - 2][1:]

        loaded = {"x0": 1, "x": 1, "small": 3, "aw": 4, "xw0": 4, "xw1": 4, "w1": 2, "wt1": 2}

        @blk.sync
        def _(sp):
            sp.dma_start(xT[:, :, 0:S], a["x"][:, :, 0:S]).then_inc(loads["x0"], 16)
            sp.dma_start(cols[:], a["cols"]).then_inc(loads["small"], 16)
            sp.dma_start(cst[:], a["consts"]).then_inc(loads["small"], 16)
            sp.dma_start(rows[:], a["rows"].broadcast_to([P, NROWS])).then_inc(loads["small"], 16)
            for n, w in zip("qkvo", aw):
                sp.dma_start(w[:], a[f"w0{n}"]).then_inc(loads["aw"], 16)
            sp.dma_start(xT[:, :, S:TOK], a["x"][:, :, S:TOK]).then_inc(loads["x"], 16)
            for l in range(2):
                for n, w in zip("qkvo", xw[l]):
                    sp.dma_start(w[:], a[f"wx{l}{n}"]).then_inc(loads[f"xw{l}"], 16)
            sp.dma_start(wq1[:], a["w1q"]).then_inc(loads["w1"], 16)
            sp.dma_start(wkv1[:], a["w1kv"]).then_inc(loads["w1"], 16)
            sp.dma_start(wt1[:], a["wt1"]).then_inc(loads["wt1"], 16)
            sp.dma_start(bt1[:], a["bt1"]).then_inc(loads["wt1"], 16)
            sp.wait_ge(*before(2))
            context(sp, cross0)
            sp.wait_ge(*before(3))
            stage3_loads(sp)
            sp.wait_ge(*before(5))
            sp.dma_start(a["kept"], xT[:]).then_inc(kept, 16)
            quick[5](sp)

            def again():
                sp.dma_start(xT[:], a["kept"]).then_inc(restored, 16)
                context(sp, general)
            stage5_general(sp, again)
            for name, n in loaded.items():
                sp.wait_ge(loads[name], 16 * n)
            with sp.Fori(0, B) as b:
                sp.wait_ge(f_go, b * KC + 1 + KC)
                sp.dma_start(a["out"][:, :, chunk(b)], xT[:, :, chunk(b)]).then_inc(stored, 16)
            sp.wait_ge(stored, 16 * B)

        @blk.gpsimd
        def _(pool):
            pool.memset(meanw[:], 1.0 / D).then_inc(init_pool, 1)
            pool.memset(a_kz[:], 0.0).then_inc(init_pool, 1)
            pool.memset(a_vg[:], 0.0).then_inc(init_pool, 1)
            stage1_pool(pool)
            cross0[2](pool)
            stage3_pool(pool)
            stage4_pool(pool)
            quick[2](pool)
            stage5_general(pool, lambda: general[2](pool))

        @blk.scalar
        def _(act):
            stage1_act(act)
            cross0[1](act)
            stage3_act(act)
            stage4_act(act)
            quick[1](act)
            stage5_general(act, lambda: general[1](act))
            stage6_act(act)

        @blk.vector
        def _(dve):
            dve.memset(eps[:, 0:1], EPS_LN).then_inc(init_dve, 1)
            dve.memset(eps[:, 1:2], EPS_RMS).then_inc(init_dve, 1)
            stage1_dve(dve)
            cross0[3](dve, *before(2))
            stage3_dve(dve, *before(3))
            stage4_dve(dve, *before(4))
            quick[3](dve, *before(5))
            stage5_general(dve, lambda: general[3](dve, restored, 16))
            stage6_dve(dve, *before(6))

        @blk.tensor
        def _(pe):
            stage1_pe(pe)
            cross0[0](pe)
            stage3_pe(pe)
            stage4_pe(pe)
            quick[0](pe)
            pe.wait_ge(quick[4], ENDX)
            pe.wait_ge(flag, 2)
            pe.transpose(ps[0:1, 0, 0:P], x_bad1[:], ident).then_inc(flag_t, 1)
            stage5_general(pe, lambda: general[0](pe))
            stage6_pe(pe)


def kernel(**inputs):
    import concourse.bacc as bacc
    from concourse.bass_utils import run_bass_kernel_spmd

    i = {k: np.asarray(v) for k, v in inputs.items()}

    def halves(w):
        return np.ascontiguousarray(w.reshape(KC, P, -1).transpose(1, 0, 2))

    def tokens(x):
        return halves(np.ascontiguousarray(x.transpose(2, 0, 1)).reshape(D, TOK))

    arrays = {
        "x": tokens(i["x"]),
        "w0q": halves(i["L0_attn_w_q"]), "w0k": halves(i["L0_attn_w_k"]), "w0v": halves(i["L0_attn_w_v"]),
        "w0o": np.ascontiguousarray(i["L0_attn_w_out"].reshape(PAIRS, P, D).transpose(1, 0, 2)),
        "consts": constants(),
        "ctx": tokens(i["ctx_1024"]),
    }
    vec = {"norm_w": "L0_attn_norm_w", "scorer_w": "L0_attn_scorer_w", "bq0": "L0_xattn_bq", "bk0": "L0_xattn_bk",
           "bo0": "L0_xattn_bo", "bq1": "L1_xattn_bq", "bk1": "L1_xattn_bk", "bo1": "L1_xattn_bo"}
    parts = [halves(i[n].reshape(D, 1)).reshape(P, KC) for n in vec.values()]
    parts += [halves(i["L1_ffn_tile_sigs"].T).reshape(P, -1), halves(i["L0_ffn_gate_w"].T).reshape(P, -1)]
    arrays["cols"] = np.concatenate(parts, axis=1)
    arrays["rows"] = np.concatenate([i[n].reshape(-1) for n in (
        "L0_xattn_bv", "L0_attn_scorer_b", "L0_ffn_expert_bias", "L1_attn_bq", "L1_attn_bk", "L1_attn_bv",
        "L1_attn_k_gamma", "L1_attn_v_gamma", "L1_attn_k_beta", "L1_attn_v_beta", "L1_xattn_bv")])[None]
    for n in "qkvo":
        arrays[f"wx0{n}"] = halves(i[f"L0_xattn_W{n}"].T)
        arrays[f"wx1{n}"] = halves(i[f"L1_xattn_W{n}"])
    arrays["w1q"] = halves(i["L1_attn_Wq"].T)
    arrays["w1kv"] = halves(np.concatenate([i["L1_attn_Wk"], i["L1_attn_Wv"]]).T)
    arrays["wt1"] = np.ascontiguousarray(i["L1_ffn_W"].reshape(T1, KC, P, D).transpose(2, 0, 1, 3))
    arrays["bt1"] = i["L1_ffn_b"]
    for n, routed in (("gate", "L0_ffn_w_gate"), ("up", "L0_ffn_w_up"), ("down", "L0_ffn_w_down")):
        w = np.concatenate([i[routed], i[f"L0_ffn_shared_{n}_w"][None]]).transpose(0, 2, 1)
        arrays["e" + n[0]] = np.ascontiguousarray(w.reshape(E + 1, KC, P, -1).transpose(2, 0, 1, 3))
    nc = bacc.Bacc("TRN2", target_bir_lowering=False, num_devices=1)
    args = {n: nc.dram_tensor(f"in_{n}", v.shape, F32, kind="ExternalInput").ap() for n, v in arrays.items()}
    args["kept"] = nc.dram_tensor("kept_x", (P, KC, TOK), F32, kind="Internal").ap()
    args["comb"] = nc.dram_tensor("combine", (E + 1, TOK), F32, kind="Internal").ap()
    args["out"] = nc.dram_tensor("out_x", (P, KC, TOK), F32, kind="ExternalOutput").ap()
    program(nc, args)
    r = run_bass_kernel_spmd(nc, [{f"in_{n}": v for n, v in arrays.items()}], core_ids=[0])
    y = r.results[0]["out_x"]
    return np.ascontiguousarray(y.transpose(1, 0, 2).reshape(D, B, S).transpose(1, 2, 0))
```
